# Optimizing a Trainium2 kernel written in Bass

```python
import numpy as np
import jax
import jax.numpy as jnp

def _softmax(x, axis=-1):
    return jax.nn.softmax(x, axis=axis)

def _gelu(x):
    return jax.nn.gelu(x, approximate=True)

def _silu(x):
    return jax.nn.silu(x)

def _sigmoid(x):
    return jax.nn.sigmoid(x)

def _layernorm(x, axis=-1, eps=1e-05):
    m = jnp.mean(x, axis=axis, keepdims=True)
    v = jnp.var(x, axis=axis, keepdims=True)
    return (x - m) / jnp.sqrt(v + eps)

def _scatter_add(tgt, idx, src, axis=0):
    return tgt.at[idx].add(src)

def _segment_sum(src, seg, n):
    return jax.ops.segment_sum(src, seg, n)
kernel_name = 'mk_gnn_ffn_d2_gnn_r8_4e29ac'

def setup_inputs(seed: int=0):
    np.random.seed(seed)
    _w = jnp.asarray

    def _rec_inputs():
        import jax
        import jax.numpy as jnp
        _gk = jax.random.key(seed)
        x = -0.0002117 + 1 * jax.random.normal(jax.random.fold_in(_gk, 1), (1250, 512), jnp.float32)
        _s = jax.random.randint(jax.random.fold_in(_gk, 2), (20000,), 0, 1250, jnp.int32)
        _d = jax.random.randint(jax.random.fold_in(_gk, 3), (20000,), 0, 1250, jnp.int32)
        _loop = jnp.arange(1250, dtype=jnp.int32)
        src = jnp.concatenate([_s, _d, _loop])
        dst = jnp.concatenate([_d, _s, _loop])
        _o = jnp.argsort(dst, stable=True)
        src = src[_o]
        dst = dst[_o]
        edge_weight = jax.random.uniform(jax.random.fold_in(_gk, 13), (41250,), jnp.float32, 0.0, 0.999998)
        return (x, src, dst, edge_weight)
    x, src, dst, edge_weight = _rec_inputs()

    def _L0_gnn_setup():
        import jax, jax.numpy as jnp
        import numpy as np
        N_NODES = 6250
        N_EDGES = 100000
        M_IN = 512
        H_OUT = 512
        key = jax.random.key(seed)
        k1, k2, k3, k4, k5 = jax.random.split(key, 5)
        X = jax.random.normal(k1, (N_NODES, M_IN), dtype=jnp.float32)
        limit = float(np.sqrt(6.0 / (M_IN + H_OUT)))
        W = jax.random.uniform(k2, (M_IN, H_OUT), dtype=jnp.float32, minval=-limit, maxval=limit)
        edge_src = jax.random.randint(k3, (N_EDGES,), 0, N_NODES, dtype=jnp.int64 if jax.config.jax_enable_x64 else jnp.int32)
        edge_dst = jax.random.randint(k4, (N_EDGES,), 0, N_NODES, dtype=jnp.int64 if jax.config.jax_enable_x64 else jnp.int32)
        edge_vals = jax.random.uniform(k5, (N_EDGES,), dtype=jnp.float32, minval=0.0, maxval=1.0)
        return {'X': X, 'W': W, 'edge_src': edge_src, 'edge_dst': edge_dst, 'edge_vals': edge_vals}
    _L0_gnn_all = _L0_gnn_setup()
    _L0_gnn_in = {k: v for k, v in _L0_gnn_all.items() if k in ('W',)}
    del _L0_gnn_all

    def _L0_ffn_setup():
        import jax, jax.numpy as jnp
        import numpy as np
        EPS = 1e-05
        NUM_HEADS = 8
        TOP_K = 2
        CAP_FACTOR = 2

        def layernorm(x, g, b):
            m = jnp.mean(x, axis=-1, keepdims=True)
            v = jnp.var(x, axis=-1, keepdims=True)
            return (x - m) * jax.lax.rsqrt(v + EPS) * g + b
        key = jax.random.key(seed)
        ks = jax.random.split(key, 16)
        B, S, H, E, F = (2, 256, 512, 64, 256)
        s = 0.02
        return {'x': jax.random.normal(ks[0], (B, S, H), jnp.float32), 'ln1_g': jnp.ones((H,), jnp.float32), 'ln1_b': jnp.zeros((H,), jnp.float32), 'wq': jax.random.normal(ks[1], (H, H), jnp.float32) * s, 'wk': jax.random.normal(ks[2], (H, H), jnp.float32) * s, 'wv': jax.random.normal(ks[3], (H, H), jnp.float32) * s, 'wo': jax.random.normal(ks[4], (H, H), jnp.float32) * s, 'ln2_g': jnp.ones((H,), jnp.float32), 'ln2_b': jnp.zeros((H,), jnp.float32), 'wr': jax.random.normal(ks[5], (H, E), jnp.float32) * s, 'w1': jax.random.normal(ks[6], (E, H, F), jnp.float32) * s, 'b1': jnp.zeros((E, F), jnp.float32), 'w2': jax.random.normal(ks[7], (E, F, H), jnp.float32) * s, 'b2': jnp.zeros((E, H), jnp.float32)}
    _L0_ffn_all = _L0_ffn_setup()
    _L0_ffn_in = {k: v for k, v in _L0_ffn_all.items() if k in ('ln1_g', 'ln1_b', 'wq', 'wk', 'wv', 'wo', 'ln2_g', 'ln2_b', 'wr', 'w1', 'b1', 'w2', 'b2')}
    del _L0_ffn_all

    def _L1_gnn_setup():
        import jax, jax.numpy as jnp
        import numpy as np
        N_NODES = 6250
        N_EDGES = 100000
        D_IN = 512
        D_OUT = 512
        EPS = 1e-05
        key = jax.random.key(seed)
        k1, k2, k3, k4, k5 = jax.random.split(key, 5)
        x = jax.random.normal(k1, (N_NODES, D_IN), dtype=jnp.float32)
        edge_index = jax.random.randint(k2, (2, N_EDGES), 0, N_NODES, dtype=jnp.int64)
        s = 1.0 / np.sqrt(D_IN)
        W_l = jax.random.uniform(k3, (D_OUT, D_IN), jnp.float32, -s, s)
        b_l = jnp.zeros((D_OUT,), jnp.float32)
        W_r = jax.random.uniform(k4, (D_OUT, D_IN), jnp.float32, -s, s)
        gamma = jnp.ones((D_OUT,), jnp.float32)
        beta = jnp.zeros((D_OUT,), jnp.float32)
        return {'x': x, 'edge_index': edge_index, 'W_l': W_l, 'b_l': b_l, 'W_r': W_r, 'gamma': gamma, 'beta': beta}
    _L1_gnn_all = _L1_gnn_setup()
    _L1_gnn_in = {k: v for k, v in _L1_gnn_all.items() if k in ('W_l', 'b_l', 'W_r', 'gamma', 'beta')}
    del _L1_gnn_all

    def _L1_ffn_setup():
        import jax, jax.numpy as jnp
        import numpy as np
        NUM_EXPERTS = 8
        TOP_K = 2
        key = jax.random.key(seed)
        ks = jax.random.split(key, 6)
        d, h, E = (512, 256, NUM_EXPERTS)
        s = 0.02
        return {'x': jax.random.normal(ks[0], (4, 512, d), dtype=jnp.float32), 'Wr': jax.random.normal(ks[1], (d, E), dtype=jnp.float32) * s, 'W1': jax.random.normal(ks[2], (E, d, h), dtype=jnp.float32) * s, 'b1': jax.random.normal(ks[3], (E, h), dtype=jnp.float32) * s, 'W2': jax.random.normal(ks[4], (E, h, d), dtype=jnp.float32) * s, 'b2': jax.random.normal(ks[5], (E, d), dtype=jnp.float32) * s}
    _L1_ffn_all = _L1_ffn_setup()
    _L1_ffn_in = {k: v for k, v in _L1_ffn_all.items() if k in ('Wr', 'W1', 'b1', 'W2', 'b2')}
    del _L1_ffn_all
    return {'x': x, 'src': src, 'dst': dst, 'edge_weight': edge_weight, 'L0_gnn_W': _L0_gnn_in['W'], 'L0_ffn_ln1_g': _L0_ffn_in['ln1_g'], 'L0_ffn_ln1_b': _L0_ffn_in['ln1_b'], 'L0_ffn_wq': _L0_ffn_in['wq'], 'L0_ffn_wk': _L0_ffn_in['wk'], 'L0_ffn_wv': _L0_ffn_in['wv'], 'L0_ffn_wo': _L0_ffn_in['wo'], 'L0_ffn_ln2_g': _L0_ffn_in['ln2_g'], 'L0_ffn_ln2_b': _L0_ffn_in['ln2_b'], 'L0_ffn_wr': _L0_ffn_in['wr'], 'L0_ffn_w1': _L0_ffn_in['w1'], 'L0_ffn_b1': _L0_ffn_in['b1'], 'L0_ffn_w2': _L0_ffn_in['w2'], 'L0_ffn_b2': _L0_ffn_in['b2'], 'L1_gnn_W_l': _L1_gnn_in['W_l'], 'L1_gnn_b_l': _L1_gnn_in['b_l'], 'L1_gnn_W_r': _L1_gnn_in['W_r'], 'L1_gnn_gamma': _L1_gnn_in['gamma'], 'L1_gnn_beta': _L1_gnn_in['beta'], 'L1_ffn_Wr': _L1_ffn_in['Wr'], 'L1_ffn_W1': _L1_ffn_in['W1'], 'L1_ffn_b1': _L1_ffn_in['b1'], 'L1_ffn_W2': _L1_ffn_in['W2'], 'L1_ffn_b2': _L1_ffn_in['b2']}

def reference(x, src, dst, edge_weight, L0_gnn_W, L0_ffn_ln1_g, L0_ffn_ln1_b, L0_ffn_wq, L0_ffn_wk, L0_ffn_wv, L0_ffn_wo, L0_ffn_ln2_g, L0_ffn_ln2_b, L0_ffn_wr, L0_ffn_w1, L0_ffn_b1, L0_ffn_w2, L0_ffn_b2, L1_gnn_W_l, L1_gnn_b_l, L1_gnn_W_r, L1_gnn_gamma, L1_gnn_beta, L1_ffn_Wr, L1_ffn_W1, L1_ffn_b1, L1_ffn_W2, L1_ffn_b2):
    import jax
    import jax.numpy as jnp

    def _L0_gnn_ref(X, W, edge_src, edge_dst, edge_vals):
        import jax, jax.numpy as jnp
        import numpy as np
        N_NODES = 6250
        N_EDGES = 100000
        M_IN = 512
        H_OUT = 512
        Z = jnp.matmul(X, W)
        msg = Z[edge_src] * edge_vals[:, None]
        agg = jax.ops.segment_sum(msg, edge_dst, num_segments=X.shape[0])
        return jax.nn.relu(agg)

    def _L0_ffn_ref(x, ln1_g, ln1_b, wq, wk, wv, wo, ln2_g, ln2_b, wr, w1, b1, w2, b2):
        import jax, jax.numpy as jnp
        import numpy as np
        EPS = 1e-05
        NUM_HEADS = 8
        TOP_K = 2
        CAP_FACTOR = 2

        def layernorm(x, g, b):
            m = jnp.mean(x, axis=-1, keepdims=True)
            v = jnp.var(x, axis=-1, keepdims=True)
            return (x - m) * jax.lax.rsqrt(v + EPS) * g + b
        B, S, H = x.shape
        NH = NUM_HEADS
        dh = H // NH
        x1 = layernorm(x, ln1_g, ln1_b)
        q = (x1 @ wq).reshape(B, S, NH, dh)
        k = (x1 @ wk).reshape(B, S, NH, dh)
        v = (x1 @ wv).reshape(B, S, NH, dh)
        scores = jnp.einsum('bqhd,bkhd->bhqk', q, k) * dh ** (-0.5)
        p = jax.nn.softmax(scores, axis=-1)
        attn_out = jnp.einsum('bhqk,bkhd->bqhd', p, v).reshape(B, S, H) @ wo
        x = x + attn_out
        x2 = layernorm(x, ln2_g, ln2_b).reshape(B * S, H)
        T = B * S
        E = wr.shape[1]
        C = CAP_FACTOR * (T * TOP_K // E)
        probs = jax.nn.softmax(x2 @ wr, axis=-1)
        gate_v, gate_i = jax.lax.top_k(probs, TOP_K)
        gate_v = gate_v / jnp.sum(gate_v, axis=-1, keepdims=True)
        ef = gate_i.reshape(-1)
        gf = gate_v.reshape(-1)
        oh = jax.nn.one_hot(ef, E, dtype=x2.dtype)
        pos = jnp.sum((jnp.cumsum(oh, axis=0) - oh) * oh, axis=1).astype(jnp.int32)
        keep = (pos < C).astype(x2.dtype)
        posc = jnp.minimum(pos, C - 1)
        tok = jnp.repeat(x2, TOP_K, axis=0) * keep[:, None]
        buf = jnp.zeros((E, C, H), x2.dtype).at[ef, posc].add(tok)
        h = jax.nn.gelu(jnp.einsum('ech,ehf->ecf', buf, w1) + b1[:, None, :])
        y = jnp.einsum('ecf,efh->ech', h, w2) + b2[:, None, :]
        ys = y[ef, posc] * (gf * keep)[:, None]
        moe_out = ys.reshape(T, TOP_K, H).sum(axis=1).reshape(B, S, H)
        return x + moe_out

    def _L1_gnn_ref(x, edge_index, W_l, b_l, W_r, gamma, beta):
        import jax, jax.numpy as jnp
        import numpy as np
        N_NODES = 6250
        N_EDGES = 100000
        D_IN = 512
        D_OUT = 512
        EPS = 1e-05
        N = x.shape[0]
        src = edge_index[0]
        dst = edge_index[1]
        agg = jax.ops.segment_sum(x[src], dst, num_segments=N)
        deg = jax.ops.segment_sum(jnp.ones_like(dst, jnp.float32), dst, num_segments=N)
        mean_nb = agg / jnp.maximum(deg, 1.0)[:, None]
        h = mean_nb @ W_l.T + b_l + x @ W_r.T
        h = jax.nn.relu(h)
        mu = jnp.mean(h, axis=0)
        var = jnp.mean((h - mu) ** 2, axis=0)
        out = (h - mu) * jax.lax.rsqrt(var + EPS) * gamma + beta
        return out

    def _L1_ffn_ref(x, Wr, W1, b1, W2, b2):
        import jax, jax.numpy as jnp
        import numpy as np
        NUM_EXPERTS = 8
        TOP_K = 2
        B, S, D = x.shape
        E = Wr.shape[1]
        flat = x.reshape(B * S, D)
        logits = flat @ Wr
        top_vals, top_idx = jax.lax.top_k(logits, TOP_K)
        top_w = jax.nn.softmax(top_vals, axis=-1)
        N = flat.shape[0]
        gates = jnp.zeros((N, E), dtype=flat.dtype).at[jnp.arange(N)[:, None], top_idx].add(top_w)
        out = jnp.zeros_like(flat)
        for e in range(E):
            hdn = jax.nn.gelu(flat @ W1[e] + b1[e], approximate=False)
            y = hdn @ W2[e] + b2[e]
            out = out + gates[:, e:e + 1] * y
        return out.reshape(B, S, D)
    edge_index = jnp.stack([src, dst])
    x = x + _L0_gnn_ref(_layernorm(x, axis=-1), L0_gnn_W, src, dst, edge_weight)
    x = x + _L0_ffn_ref(_layernorm(x, axis=-1)[None], L0_ffn_ln1_g, L0_ffn_ln1_b, L0_ffn_wq, L0_ffn_wk, L0_ffn_wv, L0_ffn_wo, L0_ffn_ln2_g, L0_ffn_ln2_b, L0_ffn_wr, L0_ffn_w1, L0_ffn_b1, L0_ffn_w2, L0_ffn_b2)[0]
    x = x + _L1_gnn_ref(_layernorm(x, axis=-1), edge_index, L1_gnn_W_l, L1_gnn_b_l, L1_gnn_W_r, L1_gnn_gamma, L1_gnn_beta)
    x = x + _L1_ffn_ref(_layernorm(x, axis=-1)[None], L1_ffn_Wr, L1_ffn_W1, L1_ffn_b1, L1_ffn_W2, L1_ffn_b2)[0]
    return x

_drawn_inputs = setup_inputs


def setup_inputs(seed=0):
    import zlib

    import numpy as np

    out = dict(_drawn_inputs(seed))
    spreads = {'L0_ffn_ln1_g': (1.0, 0.6),
     'L0_ffn_ln1_b': (0.0, 0.8),
     'L0_ffn_ln2_g': (1.0, 0.6),
     'L0_ffn_ln2_b': (0.0, 0.693),
     'L0_ffn_b1': (0.0, 0.8),
     'L0_ffn_b2': (0.0, 1.273),
     'L1_gnn_b_l': (0.0, 0.283),
     'L1_gnn_gamma': (1.0, 0.6),
     'L1_gnn_beta': (0.0, 0.763)}
    factors = {'L0_ffn_wq': 8.0,
     'L0_ffn_wk': 8.0,
     'L0_ffn_wv': 5.617,
     'L0_ffn_wo': 5.369,
     'L0_ffn_w1': 3.182,
     'L0_ffn_w2': 2.985,
     'L1_ffn_Wr': 3.904,
     'L1_ffn_W1': 3.613,
     'L1_ffn_b1': 50.776,
     'L1_ffn_W2': 3.459,
     'L1_ffn_b2': 37.336}
    for name, (base, spread) in spreads.items():
        noise = np.random.default_rng([zlib.crc32(name.encode()), seed]).standard_normal(out[name].shape)
        drawn = base * np.exp(spread * noise) if base else spread * noise
        out[name] = jnp.asarray(drawn.astype(out[name].dtype))
    for name, factor in factors.items():
        out[name] = (out[name] * factor).astype(out[name].dtype)
    return out
```

```python
from contextlib import ExitStack

import concourse.bass as bass
from concourse import mybir

F32 = mybir.dt.float32
BF16 = mybir.dt.bfloat16
I16 = mybir.dt.int16
U16 = mybir.dt.uint16
I32 = mybir.dt.int32
U32 = mybir.dt.uint32
ALU = mybir.AluOpType
ACT = mybir.ActivationFunctionType
AX = mybir.AxisListType

N = 1250
D = 512
P = 125
NT = N // P
KD = D // 128
EPS = 1e-5
GROUPS = [(0, 4), (4, 4), (8, 2)]
CHUNKS = [(0, 417), (417, 417), (834, 416)]

EDGES = 41250
EC = 125
NCH = EDGES // EC
CR = 110
CJ = NCH // CR
WD = 25
NW = N // WD
NWP = 128
WC = NT * WD
SLOTS = 4

NH = 8
DH = D // NH
SCALE = DH ** -0.5

TOP = 2
E0, F0 = 64, 256
CAP = 2 * (N * TOP // E0)
E1, F1 = 8, 256
BR = 128
NB = (N * TOP + E1 * (BR - 1)) // BR
BLOCKS = -(-N // BR)
OUTSIDE = float(1 << 20)


class Named:
    pass


class Chain:

    def __init__(self, engine, semaphore, at):
        self.engine, self.semaphore, self.at = engine, semaphore, at

    def __call__(self, instruction):
        self.at[0] += 1
        instruction.then_inc(self.semaphore, 1)
        self.engine.wait_ge(self.semaphore, self.at[0])


class Carve:

    def __init__(self, region, start=0):
        self.region, self.at = region, start

    def __call__(self, parts, cols, dtype=F32):
        size = mybir.dt.size(dtype)
        words = -(-cols * size // 4)
        view = self.region[:, self.at:self.at + words]
        self.at += words
        assert self.at <= self.region.shape[1], (self.at, self.region.shape)
        if dtype != F32:
            view = view.bitcast(dtype)
        return view[:parts, :cols]



TURNS = len(GROUPS) * KD


def transpose_rows(pe, T, rows, ready, S, use):
    for g, (t0, n) in enumerate(GROUPS):
        if ready is not None:
            pe.wait_ge(ready, t0 + n)
        for k in range(KD):
            j = g * KD + k
            if j >= 8:
                pe.wait_ge(S.tiles_copied, use * TURNS + j - 7)
            for t in range(t0, t0 + n):
                last = pe.transpose(T.ps[:, j % 8, (t - t0) * P:(t - t0 + 1) * P],
                                    rows[:, t, k * 128:(k + 1) * 128], T.ident[:P, :P])
            last.then_inc(S.tiles_turned, 1)


def copy_transposed(act, T, out, S, use):
    for g, (t0, n) in enumerate(GROUPS):
        for k in range(KD):
            j = g * KD + k
            act.wait_ge(S.tiles_turned, use * TURNS + j + 1)
            act.activation(out[:, k, t0 * P:(t0 + n) * P], T.ps[:, j % 8, 0:n * P], ACT.Copy)\
               .then_inc(S.tiles_copied, 1)


def row_moments(dve, link, T, rows, t, var_ready):
    link(dve.bn_stats(T.stats[:], rows[:, t, :]))
    link(dve.bn_aggr(T.moments[:, t, :], T.stats[:]))
    dve.tensor_scalar(T.spread[:, t:t + 1], T.moments[:, t, 1:2], EPS, None, ALU.add).then_inc(var_ready, 1)


def row_roots(act, T, var_ready, std_ready, base=0):
    for t in range(NT):
        act.wait_ge(var_ready, base + t + 1)
        act.activation(T.std[:, t:t + 1], T.spread[:, t:t + 1], ACT.Sqrt).then_inc(std_ready, 1)


def normalize(dve, link, T, out, rows, t, gain=None, shift=None):
    link(dve.reciprocal(T.rstd[:, t:t + 1], T.std[:, t:t + 1]))
    if gain is None:
        return dve.tensor_scalar(out[:, t, :], rows[:, t, :], T.moments[:, t, 0:1], T.rstd[:, t:t + 1],
                                 ALU.subtract, ALU.mult)
    link(dve.scalar_tensor_tensor(out=out[:, t, :], in0=rows[:, t, :], scalar=T.moments[:, t, 0:1], in1=gain,
                                  op0=ALU.subtract, op1=ALU.mult))
    return dve.scalar_tensor_tensor(out=out[:, t, :], in0=out[:, t, :], scalar=T.rstd[:, t:t + 1], in1=shift,
                                    op0=ALU.mult, op1=ALU.add)


def rows_of(region, width=D):
    return region[:P, 0:NT * width].rearrange("p (t d) -> p t d", t=NT)


def feats_of(region):
    return region[:, 0:KD * N].rearrange("p (k n) -> p k n", k=KD)



def constants(nc, T, S, A):
    with nc.Block() as block:

        @block.gpsimd
        def _(pool):
            pool.memset(T.ident[:], 0.0).then_inc(S.const_pool, 1)
            pool.memset(T.before[:], 1.0).then_inc(S.const_pool, 1)
            pool.wait_ge(S.const_pool, 2)
            pool.affine_select(out=T.ident[:], in_=T.ident[:], compare_op=ALU.not_equal, fill=1.0, base=0,
                               pattern=[[-1, 128]], channel_multiplier=1)
            pool.affine_select(out=T.before[:], in_=T.before[:], compare_op=ALU.is_gt, fill=0.0, base=0,
                               pattern=[[1, P]], channel_multiplier=-1)
            exact = dict(allow_small_or_imprecise_dtypes=True)
            pool.iota(T.lo_iota[:], [[1, P]], base=0, channel_multiplier=0, **exact)
            pool.iota(T.cell_iota[:, 0, :], [[N, NT], [1, WD]], base=0, channel_multiplier=0, **exact)
            pool.iota(T.win_first[:], [[WD, NWP]], base=0, channel_multiplier=0, **exact)
            pool.iota(T.chunk_id[:], [[1, CJ]], base=0, channel_multiplier=CJ, **exact)
            pool.iota(T.expert_iota[:], [[1, E0]], base=0, channel_multiplier=0, **exact)
            pool.iota(T.block_iota[:], [[1, NB]], base=0, channel_multiplier=0, **exact)
            pool.iota(T.row_starts[:], [[BR, BLOCKS]], base=0, channel_multiplier=0, **exact)
            pool.iota(T.token_id[:], [[P, NT]], base=0, channel_multiplier=1, **exact)
            pool.iota(T.zero_ids[:], [[0, E0]], base=0, channel_multiplier=0, **exact)

        @block.vector
        def _(dve):
            dve.memset(T.zeros_bf[:], 0.0)
            dve.memset(T.win_range[:], 0.0)
            dve.memset(T.ones_bf[:], 1.0)
            dve.memset(T.ones[:], 1.0)

        @block.sync
        def _(sp):
            sp.dma_start(T.x[0:120], A.x.rearrange("(t p) d -> p t d", t=NT)[0:120]).then_inc(S.x_loaded, 16)
            sp.dma_start(T.x[120:P], A.x.rearrange("(t p) d -> p t d", t=NT)[120:P]).then_inc(S.x_loaded, 16)
            sp.dma_start(T.w_a, A.L0_gnn_W.rearrange("(k p) n -> p k n", k=KD)).then_inc(S.w0_loaded, 16)
            sp.dma_start(T.dst_i, A.dst.rearrange("(p j e) -> p j e", j=CJ, e=EC)).then_inc(S.edges_loaded, 16)
            sp.dma_start(T.src_i, A.src.rearrange("(p j e) -> p j e", j=CJ, e=EC)).then_inc(S.edges_loaded, 16)
            sp.dma_start(T.wgt, A.edge_weight.rearrange("(p j e) -> p j e", j=CJ, e=EC)).then_inc(S.edges_loaded, 16)
            sp.dma_start(T.w_b, A.L0_ffn_wq.rearrange("(k p) n -> p k n", k=KD)).then_inc(S.wq_loaded, 16)
            for i, v in enumerate((A.L0_ffn_ln1_g, A.L0_ffn_ln1_b, A.L0_ffn_ln2_g, A.L0_ffn_ln2_b)):
                sp.dma_start(T.affine[:, i, :], v.rearrange("(o d) -> o d", o=1).to_broadcast([P, D]))\
                  .then_inc(S.affine_loaded, 16)


def first_projection(nc, T, S, A):
    with nc.Block() as block:

        @block.vector
        def _(dve):
            link = Chain(dve, S.dve_chain, T.dve_at)
            dve.wait_ge(S.x_loaded, 32)
            for t in range(NT):
                row_moments(dve, link, T, T.x, t, S.z_var)
            for t in range(NT):
                dve.wait_ge(S.z_std, t + 1)
                normalize(dve, link, T, T.rows_a, T.x, t).then_inc(S.z_rows, 1)

        @block.scalar
        def _(act):
            row_roots(act, T, S.z_var, S.z_std)
            copy_transposed(act, T, T.feats, S, 0)
            for t in range(NT):
                act.wait_ge(S.z_done, t + 1)
                act.activation(T.rows_a[:, t, :], T.ps[:P, t % 8, :], ACT.Copy).then_inc(S.z_copied, 1)

        @block.tensor
        def _(pe):
            transpose_rows(pe, T, T.rows_a, S.z_rows, S, 0)
            pe.wait_ge(S.tiles_copied, 1 * TURNS)
            pe.wait_ge(S.w0_loaded, 16)
            for t in range(NT):
                if t >= 8:
                    pe.wait_ge(S.z_copied, t - 7)
                for k in range(KD):
                    last = pe.matmul(T.ps[:P, t % 8, :], T.feats[:, k, t * P:(t + 1) * P], T.w_a[:, k, :],
                                     start=(k == 0), stop=(k == KD - 1))
                last.then_inc(S.z_done, 1)


def adjacency(nc, T, S, A):
    with nc.Block() as block:

        @block.vector
        def _(dve):
            link = Chain(dve, S.dve_chain, T.dve_at)
            dve.wait_ge(S.edges_loaded, 48)
            dve.tensor_copy(T.dst_f, T.dst_i)
            link(dve.tensor_copy(T.src_f, T.src_i))
            link(dve.tensor_scalar(T.hi_f, T.src_f, float(P), None, ALU.is_ge))
            for k in range(2, NT):
                link(dve.scalar_tensor_tensor(out=T.hi_f, in0=T.src_f, scalar=float(k * P), in1=T.hi_f,
                                              op0=ALU.is_ge, op1=ALU.add))
            dve.scalar_tensor_tensor(out=T.prep[:, 0], in0=T.hi_f, scalar=-float(P), in1=T.src_f,
                                     op0=ALU.mult, op1=ALU.add)
            dve.scalar_tensor_tensor(out=T.prep[:, 1], in0=T.hi_f, scalar=float(N), in1=T.dst_f,
                                     op0=ALU.mult, op1=ALU.add)
            link(dve.tensor_copy(T.part_bf, T.wgt))
            link(dve.tensor_copy(T.prep[:, 2], T.part_bf))
            link(dve.tensor_tensor(T.wgt, T.wgt, T.prep[:, 2], ALU.subtract))
            link(dve.tensor_copy(T.part_bf, T.wgt))
            link(dve.tensor_copy(T.prep[:, 3], T.part_bf))
            dve.tensor_tensor(T.prep[:, 4], T.wgt, T.prep[:, 3], ALU.subtract)
            dve.tensor_reduce(T.ch_min, T.dst_f, AX.X, ALU.min)
            link(dve.tensor_reduce(T.ch_max, T.dst_f, AX.X, ALU.max))
            win = T.win_first[:].unsqueeze(1).to_broadcast([CR, CJ, NWP])
            link(dve.tensor_scalar(T.ch_min, T.ch_min, float(WD - 1), None, ALU.subtract))
            dve.tensor_tensor(T.hit, win, T.ch_min.unsqueeze(2).to_broadcast([CR, CJ, NWP]), ALU.is_ge)
            link(dve.tensor_tensor(T.hit2, win, T.ch_max.unsqueeze(2).to_broadcast([CR, CJ, NWP]), ALU.is_le))
            link(dve.tensor_tensor(T.hit, T.hit, T.hit2, ALU.mult))
            dve.tensor_scalar(T.ch_min, T.chunk_id[:], float(NCH), None, ALU.subtract)
            link(dve.tensor_scalar(T.ch_max, T.chunk_id[:], 1.0, None, ALU.add))
            dve.tensor_tensor(T.hit2, T.hit, T.ch_min.unsqueeze(2).to_broadcast([CR, CJ, NWP]), ALU.mult)
            dve.tensor_tensor(T.hit, T.hit, T.ch_max.unsqueeze(2).to_broadcast([CR, CJ, NWP]), ALU.mult)\
               .then_inc(S.prep_done, 1)
            dve.wait_ge(S.prep_transposed, 1)
            for a, column in enumerate((T.lo_col, T.cell_col, T.w1_col, T.w2_col, T.w3_col)):
                dve.tensor_copy(column.rearrange("q (p j) -> q p j", j=CJ),
                                T.ps[:P, a, 0:NCH].rearrange("q (j p) -> q p j", j=CJ))
            dve.tensor_reduce(T.win_range[:, 0:1], T.ps[:, 5, 0:NCH], AX.X, ALU.min)
            link(dve.tensor_reduce(T.win_range[:, 1:2], T.ps[:, 6, 0:NCH], AX.X, ALU.max))
            link(dve.tensor_scalar(T.win_range[:, 0:1], T.win_range[:, 0:1], -1.0, float(NCH), ALU.min, ALU.add))
            link(dve.tensor_scalar(T.win_end[:], T.win_range[:, 0:1], 1.0, None, ALU.add))
            dve.tensor_tensor(T.win_range[:, 1:2], T.win_range[:, 1:2], T.win_end[:], ALU.max).then_inc(S.range_ready, 1)
            dve.wait_ge(S.range_transposed, 1)
            dve.tensor_copy(T.ranges[:], T.ps[0:2, 7, 0:NWP]).then_inc(S.ranges_ready, 1)
            dve.wait_ge(S.ranges_ready, 1)

            visit = dve.alloc_register("dve_visit")
            slot = dve.alloc_register("dve_slot")
            dve.reg_mov(visit, 1)
            dve.reg_mov(slot, 0)
            with dve.Fori(0, NW // 2) as pair:
                for par in range(2):
                    w = pair * 2 + par
                    first = dve.value_load(T.ranges[0:1, bass.ds(w, 1)], min_val=0, max_val=NCH - 1)
                    end = dve.value_load(T.ranges[1:2, bass.ds(w, 1)], min_val=1, max_val=NCH)
                    with dve.Fori(first, end) as c:
                        s = dve.snap(slot, min_val=0, max_val=SLOTS - 1)
                        dve.wait_ge(S.slot_free, visit)
                        cells = T.onehot_cell[:, bass.ds(s * 4, 1), :]
                        dve.tensor_scalar(cells, T.cell_iota[:, par, :], T.cell_col[:, bass.ds(c, 1)], None,
                                          ALU.is_equal).then_inc(S.count_ready, 1)
                        dve.tensor_scalar(T.onehot_src[:, bass.ds(s, 1), :], T.lo_iota[:],
                                          T.lo_col[:, bass.ds(c, 1)], None, ALU.is_equal)
                        dve.wait_ge(S.count_ready, visit)
                        for part, column in ((1, T.w1_col), (2, T.w2_col)):
                            last = dve.tensor_scalar(T.onehot_cell[:, bass.ds(s * 4 + part, 1), :], cells,
                                                     column[:, bass.ds(c, 1)], None, ALU.mult)
                        last.then_inc(S.parts_ready, 1)
                        dve.reg_add(visit, visit, 1)
                        dve.reg_add(slot, slot, 1)
                        dve.reg_alu(slot, slot, SLOTS - 1, ALU.bitwise_and)
                    dve.tensor_scalar(T.cell_iota[:, 1 - par, :], T.cell_iota[:, par, :], float(WD), None, ALU.add)\
                       .then_inc(S.window_moved, 1)
                    dve.wait_ge(S.window_moved, w + 1)

        @block.scalar
        def _(act):
            act.wait_ge(S.ranges_ready, 1)
            visit = act.alloc_register("act_visit")
            slot = act.alloc_register("act_slot")
            act.reg_mov(visit, 1)
            act.reg_mov(slot, 0)
            act.preload_act_table(ACT.Copy)
            act.sem_inc(S.bank_free, 2)
            with act.Fori(0, NW // 2) as pair:
                for par in range(2):
                    w = pair * 2 + par
                    first = act.value_load(T.ranges[0:1, bass.ds(w, 1)], min_val=0, max_val=NCH - 1)
                    end = act.value_load(T.ranges[1:2, bass.ds(w, 1)], min_val=1, max_val=NCH)
                    with act.Fori(first, end) as c:
                        s = act.snap(slot, min_val=0, max_val=SLOTS - 1)
                        act.wait_ge(S.count_ready, visit)
                        act.activation(T.onehot_cell[:, bass.ds(s * 4 + 3, 1), :], T.onehot_cell[:, bass.ds(s * 4, 1), :],
                                       ACT.Copy, scale=T.w3_col[:, bass.ds(c, 1)]).then_inc(S.low_ready, 1)
                        act.reg_add(visit, visit, 1)
                        act.reg_add(slot, slot, 1)
                        act.reg_alu(slot, slot, SLOTS - 1, ALU.bitwise_and)
                    act.wait_ge(S.window_done, w + 1)
                    act.activation(T.ct[:, :, bass.ds(w * WD, WD)],
                                   T.ps[:P, par, 0:WC].rearrange("p (k d) -> p k d", k=NT), ACT.Copy)
                    act.activation(T.at[:, :, bass.ds(w * WD, WD)],
                                   T.ps[:P, par, WC:2 * WC].rearrange("p (k d) -> p k d", k=NT), ACT.Copy)\
                        .then_inc(S.bank_free, 1)

        @block.tensor
        def _(pe):
            pe.wait_ge(S.prep_done, 1)
            for a in range(5):
                for j in range(CJ):
                    pe.transpose(T.ps[:P, a, j * CR:(j + 1) * CR], T.prep[:, a, j, :], T.ident[:CR, :CR])
            for bank, source in ((5, T.hit2), (6, T.hit)):
                for j in range(CJ):
                    last = pe.transpose(T.ps[:, bank, j * CR:(j + 1) * CR], source[:, j, :], T.ident[:CR, :CR])
            last.then_inc(S.prep_transposed, 1)
            pe.wait_ge(S.range_ready, 1)
            pe.transpose(T.ps[:, 7, 0:NWP], T.win_range[:], T.ident[:]).then_inc(S.range_transposed, 1)
            pe.wait_ge(S.ranges_ready, 1)
            visit = pe.alloc_register("pe_visit")
            slot = pe.alloc_register("pe_slot")
            pe.reg_mov(visit, 1)
            pe.reg_mov(slot, 0)
            pe.sem_inc(S.slot_free, SLOTS)
            with pe.Fori(0, NW // 2) as pair:
                for par in range(2):
                    w = pair * 2 + par
                    first = pe.value_load(T.ranges[0:1, bass.ds(w, 1)], min_val=0, max_val=NCH - 1)
                    end = pe.value_load(T.ranges[1:2, bass.ds(w, 1)], min_val=1, max_val=NCH)
                    pe.wait_ge(S.bank_free, w + 1)
                    pe.matmul(T.ps[:P, par, 0:2 * WC], T.zeros_bf[:, 0:P], T.zeros_bf[:, 0:2 * WC],
                              start=True, stop=False, skip_group_check=True)
                    with pe.Fori(first, end):
                        s = pe.snap(slot, min_val=0, max_val=SLOTS - 1)
                        pe.wait_ge(S.parts_ready, visit)
                        src = T.onehot_src[:, bass.ds(s, 1), :].rearrange("e o p -> e (o p)")
                        pe.matmul(T.ps[:P, par, 0:2 * WC], src,
                                  T.onehot_cell[:, bass.ds(s * 4, 2), :].rearrange("e a c -> e (a c)"),
                                  start=False, stop=False, skip_group_check=True)
                        pe.matmul(T.ps[:P, par, WC:2 * WC], src,
                                  T.onehot_cell[:, bass.ds(s * 4 + 2, 1), :].rearrange("e a c -> e (a c)"),
                                  start=False, stop=False, skip_group_check=True)
                        pe.wait_ge(S.low_ready, visit)
                        pe.matmul(T.ps[:P, par, WC:2 * WC], src,
                                  T.onehot_cell[:, bass.ds(s * 4 + 3, 1), :].rearrange("e a c -> e (a c)"),
                                  start=False, stop=False, skip_group_check=True).then_inc(S.slot_free, 1)
                        pe.reg_add(visit, visit, 1)
                        pe.reg_add(slot, slot, 1)
                        pe.reg_alu(slot, slot, SLOTS - 1, ALU.bitwise_and)
                    pe.matmul(T.ps[:P, par, 0:2 * WC], T.zeros_bf[:, 0:P], T.zeros_bf[:, 0:2 * WC],
                              start=False, stop=True, skip_group_check=True).then_inc(S.window_done, 1)



def choose(dve, link, T, experts, chosen, gap_ready):
    for t in range(NT):
        last = dve.max(T.top[:, t, :], T.logits[:, t, 0:experts])
    link(last)
    dve.tensor_tensor(T.gap[:], T.top[:, :, 1], T.top[:, :, 0], ALU.subtract).then_inc(gap_ready, 1)
    for t in range(NT):
        last = dve.max_index(T.top_i[:, t, :], T.top[:, t, :], T.logits[:, t, 0:experts])
    link(last)
    link(dve.tensor_copy(T.expert[:], T.top_i[:, :, 0:TOP]))
    which = T.expert_iota[:, 0:experts].unsqueeze(1).to_broadcast([P, NT, experts])
    for j in range(TOP):
        last = dve.tensor_tensor(T.onehot[:, j, :, 0:experts], which,
                                 T.expert[:, :, j].unsqueeze(2).to_broadcast([P, NT, experts]), ALU.is_equal)
    link(last)
    dve.tensor_tensor(T.onehot[:, TOP, :, 0:experts], T.onehot[:, 0, :, 0:experts], T.onehot[:, 1, :, 0:experts],
                      ALU.add).then_inc(chosen, 1)


def gates(dve, link, T):
    link(dve.tensor_scalar(T.gate[:, :, 0], T.gap[:], 1.0, None, ALU.add))
    link(dve.reciprocal(T.gate[:, :, 0], T.gate[:, :, 0]))
    link(dve.tensor_tensor(T.gate[:, :, 1], T.gate[:, :, 0], T.gap[:], ALU.mult))


def count_before(pe, T, experts):
    for t in range(NT):
        out = T.ps[:P, 2 + t // 5, t % 5 * experts:(t % 5 + 1) * experts]
        for u in range(t):
            pe.matmul(out, T.ones_bf[:, 0:P], T.onehot[:, TOP, u, 0:experts], start=(u == 0), stop=False)
        last = pe.matmul(out, T.before[:], T.onehot[:, TOP, t, 0:experts], start=(t == 0), stop=True)
    return last


def positions(dve, link, T, experts):
    for j in range(TOP):
        for b in range(2):
            last = dve.tensor_tensor(T.picked[:, 5 * b:5 * b + 5, 0:experts], T.onehot[:, j, 5 * b:5 * b + 5, 0:experts],
                                     T.ps[:P, 2 + b, 0:5 * experts].rearrange("p (t e) -> p t e", t=5), ALU.mult)
        link(last)
        link(dve.tensor_reduce(T.position[:, :, j], T.picked[:, :, 0:experts], AX.X, ALU.add))


def gate_rows(dve, link, T, experts, ready):
    link(dve.memset(T.gate_rows[:], 0.0))
    for j in range(TOP):
        link(dve.tensor_tensor(T.picked[:, :, 0:experts], T.onehot[:, j, :, 0:experts],
                               T.gate[:, :, j].unsqueeze(2).to_broadcast([P, NT, experts]), ALU.mult))
        last = dve.tensor_tensor(T.gate_rows[:, :, 0:experts], T.gate_rows[:, :, 0:experts], T.picked[:, :, 0:experts], ALU.add)
        if j < TOP - 1:
            link(last)
    last.then_inc(ready, 1)


def fill_table(pool, T, table, size, filled):
    for t in range(NT):
        for j in range(TOP):
            pool.indirect_dma_start(table, bass.IndirectOffsetOnAxis(ap=T.address_i[:, t, j:j + 1], axis=0),
                                    T.token_id[:, t:t + 1], None, bounds_check=size - 1, oob_is_err=False)\
                .then_inc(filled, 16)


def first_convolution(nc, T, S, A):
    with nc.Block() as block:

        @block.sync
        def _(sp):
            sp.dma_start(T.w_a, A.L0_ffn_wk.rearrange("(k p) n -> p k n", k=KD)).then_inc(S.wk_loaded, 16)

        @block.tensor
        def _(pe):
            for t in range(NT):
                if t >= 8:
                    pe.wait_ge(S.agg_used, t - 7)
                for k in range(NT):
                    last = pe.matmul(T.ps[:P, t % 8, :], T.at[:, k, t * P:(t + 1) * P], T.rows_a[:, k, :],
                                     start=(k == 0), stop=(k == NT - 1))
                last.then_inc(S.agg_done, 1)
            pe.wait_ge(S.agg_used, NT)
            transpose_rows(pe, T, T.rows_c, S.attn_rows, S, 1)

        @block.vector
        def _(dve):
            link = Chain(dve, S.dve_chain, T.dve_at)

            def residual(t):
                dve.wait_ge(S.agg_done, t + 1)
                dve.scalar_tensor_tensor(out=T.x[:, t, :], in0=T.ps[:P, t % 8, :], scalar=0.0, in1=T.x[:, t, :],
                                         op0=ALU.max, op1=ALU.add).then_inc(S.agg_used, 1)
                dve.wait_ge(S.agg_used, t + 1)
                row_moments(dve, link, T, T.x, t, S.xf_var)

            def ffn_input(t):
                dve.wait_ge(S.xf_std, 2 * t + 1)
                link(normalize(dve, link, T, T.rows_b, T.x, t))
                row_moments(dve, link, T, T.rows_b, t, S.xf_var)
                dve.wait_ge(S.xf_std, 2 * t + 2)
                normalize(dve, link, T, T.rows_c, T.rows_b, t, T.affine[:, 0, :], T.affine[:, 1, :])\
                    .then_inc(S.attn_rows, 1)

            dve.wait_ge(S.affine_loaded, 64)
            for t in range(NT):
                residual(t)
                ffn_input(t)

        @block.scalar
        def _(act):
            for t in range(NT):
                for half in range(2):
                    act.wait_ge(S.xf_var, 2 * t + half + 1)
                    act.activation(T.std[:, t:t + 1], T.spread[:, t:t + 1], ACT.Sqrt).then_inc(S.xf_std, 1)
            copy_transposed(act, T, T.feats, S, 1)


def projections(nc, T, S, A):
    with nc.Block() as block:

        @block.sync
        def _(sp):
            sp.dma_start(T.w_v, A.L0_ffn_wv.rearrange("(k p) n -> p k n", k=KD)).then_inc(S.wv_loaded, 16)

        @block.tensor
        def _(pe):
            j = 0
            for weights, loaded in ((T.w_b, S.wq_loaded), (T.w_a, S.wk_loaded)):
                pe.wait_ge(loaded, 16)
                for m in range(KD):
                    for c0, n in CHUNKS:
                        if j >= 8:
                            pe.wait_ge(S.proj_copied, j - 7)
                        for k in range(KD):
                            last = pe.matmul(T.ps[:, j % 8, 0:n], weights[:, k, m * 128:(m + 1) * 128],
                                             T.feats[:, k, c0:c0 + n], start=(k == 0), stop=(k == KD - 1))
                        last.then_inc(S.proj_done, 1)
                        j += 1
            pe.wait_ge(S.wv_loaded, 16)
            for t in range(NT):
                pe.wait_ge(S.proj_copied, j - 7)
                for k in range(KD):
                    last = pe.matmul(T.ps[:P, j % 8, :], T.feats[:, k, t * P:(t + 1) * P], T.w_v[:, k, :],
                                     start=(k == 0), stop=(k == KD - 1))
                last.then_inc(S.proj_done, 1)
                j += 1

        @block.scalar
        def _(act):
            j = 0
            for out in (T.qt, T.kt):
                for m in range(KD):
                    for c0, n in CHUNKS:
                        act.wait_ge(S.proj_done, j + 1)
                        act.activation(out[:, m, c0:c0 + n], T.ps[:, j % 8, 0:n], ACT.Copy).then_inc(S.proj_copied, 1)
                        j += 1
            for t in range(NT):
                act.wait_ge(S.proj_done, j + 1)
                act.activation(T.v[:, t, :], T.ps[:P, j % 8, :], ACT.Copy).then_inc(S.proj_copied, 1)
                j += 1


def attention(nc, T, S, A):
    steps = [(h, t) for h in range(NH) for t in range(NT)]
    LAST = N - CHUNKS[0][1]
    starts = [0, CHUNKS[0][1], LAST]
    CW = CHUNKS[0][1]
    twice = 2 * CW - LAST
    TURNED = (7, 6, 7)

    with nc.Block() as block:

        @block.sync
        def _(sp):
            sp.dma_start(T.w_b, A.L0_ffn_wo.rearrange("(k p) n -> p k n", k=KD)).then_inc(S.wo_loaded, 16)
            sp.dma_start(T.w_r, A.L0_ffn_wr.rearrange("(k p) e -> p k e", k=KD)).then_inc(S.wr_loaded, 16)

        @block.tensor
        def _(pe):
            def scores(n):
                h, t = steps[n]
                b, m = DH * (h % 2), h // 2
                if n >= 2:
                    pe.wait_ge(S.exp_done, n - 1)
                for c, c0 in enumerate(starts):
                    last = pe.matmul(T.ps[:P, 3 * (n % 2) + c, 0:CW], T.qt[b:b + DH, m, t * P:(t + 1) * P],
                                     T.kt[b:b + DH, m, c0:c0 + CW], start=True, stop=True)
                last.then_inc(S.scores_done, 1)

            def turn(n):
                pe.wait_ge(S.exp_done, n + 1)
                for g, (t0, k) in enumerate(GROUPS):
                    if g == 1 and n >= 1:
                        pe.wait_ge(S.out_copied, n)
                    if g == 2:
                        pe.wait_ge(S.probs_copied, 3 * n + 1)
                    for t in range(t0, t0 + k):
                        last = pe.transpose(T.ps[:P, TURNED[g], (t - t0) * P:(t - t0 + 1) * P],
                                            T.probs[:, n % 2, t * P:(t + 1) * P], T.ident[:P, :P])
                    last.then_inc(S.probs_turned, 1)

            def values(n):
                h, _ = steps[n]
                pe.wait_ge(S.probs_copied, 3 * n + 3)
                for k in range(NT):
                    last = pe.matmul(T.ps[:P, 6, 0:DH], T.probs_t[:, n % 2, k * P:(k + 1) * P],
                                     T.v[:, k, h * DH:(h + 1) * DH], start=(k == 0), stop=(k == NT - 1))
                last.then_inc(S.values_done, 1)

            for n in range(len(steps) + 2):
                if n < len(steps):
                    scores(n)
                if n >= 2:
                    values(n - 2)
                if 1 <= n <= len(steps):
                    turn(n - 1)

        @block.scalar
        def _(act):
            for n in range(len(steps)):
                act.wait_ge(S.max_ready, n + 1)
                if n >= 2:
                    act.wait_ge(S.probs_turned, 3 * n - 3)
                s = 3 * (n % 2)
                act.activation(T.probs[:, n % 2, 0:2 * CW].rearrange("q (c k) -> q c k", c=2), T.ps[:P, s:s + 2, 0:CW],
                               ACT.Exp, bias=T.neg_max[:, n % 4:n % 4 + 1], scale=SCALE,
                               accum_out=T.sums[:, n % 4, 0:1])
                act.activation(T.probs[:, n % 2, 2 * CW:N], T.ps[:P, s + 2, twice:CW],
                               ACT.Exp, bias=T.neg_max[:, n % 4:n % 4 + 1], scale=SCALE,
                               accum_out=T.sums[:, n % 4, 1:2]).then_inc(S.exp_done, 1)

        @block.vector
        def _(dve):
            link = Chain(dve, S.dve_chain, T.dve_at)

            def maxima(n):
                s = 3 * (n % 2)
                dve.wait_ge(S.scores_done, n + 1)
                link(dve.tensor_reduce(T.row_max[:, n % 4:n % 4 + 1], T.ps[:P, s:s + 3, 0:CW], AX.XY, ALU.max))
                dve.tensor_scalar(T.neg_max[:, n % 4:n % 4 + 1], T.row_max[:, n % 4:n % 4 + 1], -SCALE, None, ALU.mult)\
                   .then_inc(S.max_ready, 1)

            def output(n):
                h, t = steps[n]
                dve.wait_ge(S.exp_done, n + 1)
                link(dve.tensor_tensor(T.total[:, n % 2:n % 2 + 1], T.sums[:, n % 4, 0:1], T.sums[:, n % 4, 1:2], ALU.add))
                link(dve.reciprocal(T.total[:, n % 2:n % 2 + 1], T.total[:, n % 2:n % 2 + 1]))
                dve.wait_ge(S.values_done, n + 1)
                dve.tensor_scalar(T.o[:, t, h * DH:(h + 1) * DH], T.ps[:P, 6, 0:DH],
                                  T.total[:, n % 2:n % 2 + 1], None, ALU.mult).then_inc(S.out_copied, 1)

            def turned(n):
                for g, (t0, k) in enumerate(GROUPS):
                    j = 3 * n + g
                    dve.wait_ge(S.probs_turned, j + 1)
                    dve.tensor_copy(T.probs_t[:, n % 2, t0 * P:(t0 + k) * P], T.ps[:P, TURNED[g], 0:k * P])\
                       .then_inc(S.probs_copied, 1)

            for n in range(len(steps) + 2):
                if n < len(steps):
                    maxima(n)
                if n >= 2:
                    output(n - 2)
                if 1 <= n <= len(steps):
                    turned(n - 1)


def first_router(nc, T, S, A):
    with nc.Block() as block:

        @block.tensor
        def _(pe):
            transpose_rows(pe, T, T.o, None, S, 2)
            pe.wait_ge(S.tiles_copied, 3 * TURNS)
            pe.wait_ge(S.wo_loaded, 16)
            for t in range(NT):
                if t >= 8:
                    pe.wait_ge(S.wo_used, t - 7)
                for k in range(KD):
                    last = pe.matmul(T.ps[:P, t % 8, :], T.ot[:, k, t * P:(t + 1) * P], T.w_b[:, k, :],
                                     start=(k == 0), stop=(k == KD - 1))
                last.then_inc(S.wo_done, 1)
            pe.wait_ge(S.wo_used, NT)
            transpose_rows(pe, T, T.rows_a, S.x2_rows, S, 3)
            pe.wait_ge(S.tiles_copied, 4 * TURNS)
            pe.wait_ge(S.wr_loaded, 16)
            for t in range(NT):
                for k in range(KD):
                    last = pe.matmul(T.ps[:P, t // 5, t % 5 * E0:(t % 5 + 1) * E0], T.feats[:, k, t * P:(t + 1) * P],
                                     T.w_r[:, k, :], start=(k == 0), stop=(k == KD - 1))
            last.then_inc(S.logits_done, 1)
            pe.wait_ge(S.chosen, 1)
            count_before(pe, T, E0).then_inc(S.counted, 1)
            pe.wait_ge(S.gates_ready, 1)
            for t in range(NT):
                last = pe.transpose(T.ps[:, 4 + t // 4, t % 4 * P:(t % 4 + 1) * P], T.gate_rows[:, t, :], T.ident[:P, :P])
            last.then_inc(S.gates_turned, 1)

        @block.scalar
        def _(act):
            copy_transposed(act, T, T.ot, S, 2)
            row_roots(act, T, S.x2_var, S.x2_std)
            copy_transposed(act, T, T.feats, S, 3)
            act.wait_ge(S.logits_done, 1)
            for b in range(2):
                act.activation(T.logits[:, 5 * b:5 * b + 5, 0:E0],
                               T.ps[:P, b, 0:5 * E0].rearrange("p (t e) -> p t e", t=5), ACT.Copy).then_inc(S.logits_ready, 1)
            act.wait_ge(S.gap_ready, 1)
            act.activation(T.gap[:], T.gap[:], ACT.Exp).then_inc(S.gap_exp, 1)
            act.wait_ge(S.gates_turned, 1)
            for b in range(3):
                n = min(4, NT - 4 * b)
                act.activation(T.gates_t[:, 4 * b * P:(4 * b + n) * P], T.ps[:E0, 4 + b, 0:n * P], ACT.Copy)\
                   .then_inc(S.gates_t_ready, 1)

        @block.vector
        def _(dve):
            link = Chain(dve, S.dve_chain, T.dve_at)
            for t in range(NT):
                dve.wait_ge(S.wo_done, t + 1)
                dve.tensor_tensor(T.rows_b[:, t, :], T.ps[:P, t % 8, :], T.rows_b[:, t, :], ALU.add).then_inc(S.wo_used, 1)
                dve.wait_ge(S.wo_used, t + 1)
                row_moments(dve, link, T, T.rows_b, t, S.x2_var)
                dve.tensor_tensor(T.x[:, t, :], T.x[:, t, :], T.rows_b[:, t, :], ALU.add)
                dve.wait_ge(S.x2_std, t + 1)
                normalize(dve, link, T, T.rows_a, T.rows_b, t, T.affine[:, 2, :], T.affine[:, 3, :])\
                    .then_inc(S.x2_rows, 1)
            dve.wait_ge(S.logits_ready, 2)
            choose(dve, link, T, E0, S.chosen, S.gap_ready)
            dve.wait_ge(S.gap_exp, 1)
            gates(dve, link, T)
            dve.wait_ge(S.counted, 1)
            positions(dve, link, T, E0)
            keep, at, last = T.keep, T.address, T.scratch
            link(dve.tensor_scalar(keep[:], T.position[:], float(CAP), None, ALU.is_lt))
            link(dve.tensor_tensor(T.gate[:], T.gate[:], keep[:], ALU.mult))
            link(dve.scalar_tensor_tensor(out=at[:], in0=T.position[:], scalar=float(E0), in1=T.expert[:],
                                          op0=ALU.mult, op1=ALU.add))
            link(dve.tensor_scalar(keep[:], keep[:], -OUTSIDE, OUTSIDE, ALU.mult, ALU.add))
            link(dve.tensor_tensor(at[:], at[:], keep[:], ALU.add))
            dve.tensor_copy(T.address_i[:], at[:]).then_inc(S.addresses_ready, 1)
            link(dve.tensor_scalar(last[:], T.position[:], float(CAP - 1), None, ALU.min))
            link(dve.scalar_tensor_tensor(out=last[:], in0=T.expert[:], scalar=float(CAP), in1=last[:],
                                          op0=ALU.mult, op1=ALU.add))
            dve.tensor_copy(T.row_i[:], last[:]).then_inc(S.rows_ready, 1)
            gate_rows(dve, link, T, E0, S.gates_ready)

        @block.sync
        def _(sp):
            sp.dma_start(A.table0.rearrange("(c e) o -> c (e o)", e=E0), T.zero_ids[:CAP, :]).then_inc(S.table0_clear, 16)
            sp.wait_ge(S.x2_rows, NT)
            sp.dma_start(A.rows0.rearrange("(t p) d -> p t d", t=NT), T.rows_a).then_inc(S.rows0_stored, 16)
            sp.wait_ge(S.table0_filled, 16 * NT * TOP)
            sp.dma_start(T.ids[:CAP, 0:E0], A.table0.rearrange("(c e) o -> c (e o)", e=E0)).then_inc(S.ids0_loaded, 16)
            sp.wait_ge(S.ids0_loaded, 16)
            sp.wait_ge(S.rows0_stored, 16)

        @block.gpsimd
        def _(pool):
            pool.wait_ge(S.table0_clear, 16)
            pool.wait_ge(S.addresses_ready, 1)
            fill_table(pool, T, A.table0, CAP * E0, S.table0_filled)


def wait_count(engine, semaphore, q, per, n):
    if not isinstance(q, int) or per * q + n > 0:
        engine.wait_ge(semaphore, q * per + n)


def gather_rows(pool, T, rows, slots, parts, count, ids_ready, turned, loaded):
    def column(q, r):
        pool.tensor_copy(T.ex_ids[:parts, r % 4:r % 4 + 1], T.ids[:parts, bass.ds(q * 4 + r, 1)]).then_inc(ids_ready, 1)

    def gather(q, r, last=False):
        wait_count(pool, turned, q, 4, r - 1)
        pool.wait_ge(ids_ready, q * 4 + (r + 1))
        if not last:
            column(q, r + 1)
        pool.indirect_dma_start(slots[:parts, r % 2, :], None, rows,
                                bass.IndirectOffsetOnAxis(ap=T.ex_ids[:parts, r % 4:r % 4 + 1], axis=0))\
            .then_inc(loaded[r % 2], 16)

    loops = (count - 1) // 4
    column(0, 0)
    for r in range(4):
        gather(0, r)
    with pool.Fori(1, loops) as q:
        for r in range(4):
            gather(q, r)
    for r in range(count - 4 * loops):
        gather(loops, r, 4 * loops + r == count - 1)


def first_experts(nc, T, S, A):
    WS = 4
    FK = F0 // 128
    LOOPS = (E0 - 2) // WS

    def experts(engine, step):
        for r in range(2):
            step(0, r)
        with engine.Fori(0, LOOPS) as q:
            for r in range(2, 2 + WS):
                step(q, r)
        for r in range(2, 2 + (E0 - 2) % WS):
            step(LOOPS, r)

    def is_last(q, r):
        return isinstance(q, int) and WS * q + r == E0 - 1

    with nc.Block() as block:

        @block.sync
        def _(sp):
            def load(e, slot):
                sp.dma_start(T.ew1[:, slot], A.L0_ffn_w1[bass.ds(e, 1)].rearrange("o (k p) f -> p (o k) f", k=KD))\
                  .then_inc(S.ew_loaded[slot], 16)
                sp.dma_start(T.ew2[:, slot], A.L0_ffn_w2[bass.ds(e, 1)].rearrange("o (k p) n -> p (o k) n", k=FK))\
                  .then_inc(S.ew_loaded[slot], 16)

            sp.dma_start(T.eb1_rows, A.L0_ffn_b1).then_inc(S.columns_loaded, 16)
            for i, v in enumerate((A.L1_gnn_b_l, A.L1_gnn_gamma, A.L1_gnn_beta)):
                sp.dma_start(T.feature_rows[i * KD:(i + 1) * KD], v.rearrange("(m p) -> m p", m=KD)).then_inc(S.columns_loaded, 16)
            for slot in range(WS):
                load(slot, slot)
            with sp.Fori(0, E0 // WS - 1) as q:
                for slot in range(WS):
                    sp.wait_ge(S.ey_done, q * WS + (slot + 1))
                    load(q * WS + (slot + WS), slot)

        @block.gpsimd
        def _(pool):
            gather_rows(pool, T, A.rows0, T.ex, CAP, E0, S.ex_ids_ready, S.ex_turned, S.ex_loaded)

        @block.tensor
        def _(pe):
            def turn(q, r):
                wait_count(pe, S.ex_loaded[r % 2], q, 8 * WS, 16 * (r // 2 + 1))
                wait_count(pe, S.ex_turned_copied, q, WS, r - 1)
                for k in range(KD):
                    last = pe.transpose(T.ps[:, r % 2, k * CAP:(k + 1) * CAP], T.ex[:CAP, r % 2, k * 128:(k + 1) * 128],
                                        T.ident[:CAP, :CAP])
                last.then_inc(S.ex_turned, 1)

            def hidden(q, r):
                wait_count(pe, S.ex_turned_copied, q, WS, r + 1)
                wait_count(pe, S.ew_loaded[r % WS], q, 32, 32 * (r // WS + 1))
                wait_count(pe, S.eh_ready, q, WS, r - 1)
                for f in range(FK):
                    for k in range(KD):
                        last = pe.matmul(T.ps[:, 2 + r % 2, f * CAP:(f + 1) * CAP],
                                         T.ew1[:, r % WS, k, f * 128:(f + 1) * 128], T.ex_t[:, r % 2, k, :],
                                         start=(k == 0), stop=(k == KD - 1))
                last.then_inc(S.eh_done, 1)

            def output(q, r):
                wait_count(pe, S.eh_ready, q, WS, r + 1)
                wait_count(pe, S.ey_copied, q, WS, r - 1)
                for f in range(FK):
                    last = pe.matmul(T.ps[:CAP, 4 + r % 2, :], T.eh[:, r % 2, f, :], T.ew2[:, r % WS, f, :],
                                     start=(f == 0), stop=(f == FK - 1))
                last.then_inc(S.ey_done, 1)

            def step(q, r):
                hidden(q, r)
                if not isinstance(q, int) or WS * q + r > 0:
                    output(q, r - 1)
                if not is_last(q, r):
                    turn(q, r + 1)

            pe.wait_ge(S.columns_loaded, 64)
            for f in range(FK):
                pe.transpose(T.ps[:, 7, f * E0:(f + 1) * E0], T.eb1_rows[:, f * 128:(f + 1) * 128], T.ident[:E0, :E0])
            pe.transpose(T.ps[:, 6, 0:3 * KD], T.feature_rows, T.ident[:3 * KD, :3 * KD]).then_inc(S.columns_turned, 1)
            turn(0, 0)
            experts(pe, step)
            output(LOOPS, (E0 - 1) - WS * LOOPS)

        @block.scalar
        def _(act):
            act.wait_ge(S.columns_turned, 1)
            act.activation(T.feature[:], T.ps[:, 6, 0:3 * KD].rearrange("p (i m) -> p i m", m=KD), ACT.Copy)
            act.activation(T.eb1, T.ps[:, 7, 0:FK * E0].rearrange("p (f e) -> p f e", f=FK), ACT.Copy).then_inc(S.eb1_ready, 1)
            act.preload_act_table(ACT.Gelu_apprx_tanh)
            act.wait_ge(S.eb1_ready, 1)

            def store(q, r):
                wait_count(act, S.ey_copied, q, WS, r + 1)
                act.dma_start(A.y0[bass.ds(q * WS + r, 1)].rearrange("o c d -> (o c) d"), T.ey[:CAP, r % 2, :])\
                   .then_inc(S.ey_stored[r % 2], 16)

            def step(q, r):
                wait_count(act, S.eh_done, q, WS, r + 1)
                wait_count(act, S.ey_done, q, WS, r - 1)
                for f in range(FK):
                    last = act.activation(T.eh[:, r % 2, f, :], T.ps[:, 2 + r % 2, f * CAP:(f + 1) * CAP],
                                          ACT.Gelu_apprx_tanh, bias=T.eb1[:, f, bass.ds(q * WS + r, 1)])
                last.then_inc(S.eh_ready, 1)
                if not isinstance(q, int) or WS * q + r > 0:
                    store(q, r - 1)

            experts(act, step)
            store(LOOPS, (E0 - 1) - WS * LOOPS)
            for slot in range(2):
                act.wait_ge(S.ey_stored[slot], 8 * E0)

        @block.vector
        def _(dve):
            def turned(q, r):
                wait_count(dve, S.ex_turned, q, WS, r + 1)
                wait_count(dve, S.eh_done, q, WS, r - 1)
                dve.tensor_copy(T.ex_t[:, r % 2], T.ps[:, r % 2, 0:KD * CAP].rearrange("p (k c) -> p k c", k=KD))\
                   .then_inc(S.ex_turned_copied, 1)

            def output(q, r):
                wait_count(dve, S.ey_done, q, WS, r + 1)
                wait_count(dve, S.ey_stored[r % 2], q, 8 * WS, 16 * (r // 2))
                dve.tensor_copy(T.ey[:CAP, r % 2, :], T.ps[:CAP, 4 + r % 2, :]).then_inc(S.ey_copied, 1)

            def step(q, r):
                if not isinstance(q, int) or WS * q + r > 0:
                    output(q, r - 1)
                if not is_last(q, r):
                    turned(q, r + 1)

            turned(0, 0)
            experts(dve, step)
            output(LOOPS, (E0 - 1) - WS * LOOPS)


def second_convolution(nc, T, S, A):
    with nc.Block() as block:

        @block.gpsimd
        def _(pool):
            for t in range(NT):
                for j, rows in enumerate((T.rows_a, T.rows_c)):
                    pool.indirect_dma_start(rows[:, t, :], None, A.y0.rearrange("e c d -> (e c) d"),
                                            bass.IndirectOffsetOnAxis(ap=T.row_i[:, t, j:j + 1], axis=0))\
                        .then_inc(S.y_gathered[t], 16)

        @block.sync
        def _(sp):
            sp.dma_start(T.b2_rows, A.L0_ffn_b2).then_inc(S.b2_loaded, 16)
            sp.dma_start(T.w_a, A.L1_gnn_W_l.rearrange("(m p) n -> p m n", m=KD)).then_inc(S.wl_loaded, 16)
            sp.dma_start(T.w_b, A.L1_gnn_W_r.rearrange("(m p) n -> p m n", m=KD)).then_inc(S.wl_loaded, 16)

        @block.tensor
        def _(pe):
            pe.wait_ge(S.wl_loaded, 32)
            for i, w in enumerate((T.w_a, T.w_b)):
                for k in range(KD):
                    for m in range(KD):
                        last = pe.transpose(T.ps[:, 4 * i + k, m * 128:(m + 1) * 128], w[:, m, k * 128:(k + 1) * 128],
                                            T.ident[:])
                    last.then_inc(S.wl_turned, 1)
            pe.wait_ge(S.wl_copied, 2 * KD)
            pe.wait_ge(S.b2_loaded, 16)
            for t in range(NT):
                if t >= 8:
                    pe.wait_ge(S.moe_added, t - 7)
                pe.matmul(T.ps[:P, t % 8, :], T.gates_t[:, t * P:(t + 1) * P], T.b2_rows, start=True, stop=True)\
                  .then_inc(S.bias_done, 1)
            pe.wait_ge(S.moe_added, NT)
            transpose_rows(pe, T, T.rows_a, S.conv_rows, S, 4)
            pe.wait_ge(S.tiles_copied, 5 * TURNS)
            pe.wait_ge(S.ct_ready, 2)
            for c, (c0, n) in enumerate(CHUNKS):
                for k in range(NT):
                    last = pe.matmul(T.ps[:, c, 0:n], T.ones[:P, :], T.ct_f[:, k, c0:c0 + n], start=(k == 0), stop=(k == NT - 1))
            last.then_inc(S.degrees_done, 1)
            for m in range(KD):
                for c, (c0, n) in enumerate(CHUNKS):
                    j = 3 * m + c
                    if j >= 5:
                        pe.wait_ge(S.means_ready, j - 4)
                    for k in range(NT):
                        last = pe.matmul(T.ps[:, 3 + j % 5, 0:n], T.rows_a[:, k, m * 128:(m + 1) * 128],
                                         T.ct_f[:, k, c0:c0 + n], start=(k == 0), stop=(k == NT - 1))
                    last.then_inc(S.sums_done, 1)
            pe.wait_ge(S.means_ready, KD * 3)
            for m in range(KD):
                for c, (c0, n) in enumerate(CHUNKS):
                    j = 3 * m + c
                    if j >= 8:
                        pe.wait_ge(S.conv_relu, j - 7)
                    for k in range(KD):
                        pe.matmul(T.ps[:, j % 8, 0:n], T.wl_t[:, 0, k, m * 128:(m + 1) * 128], T.means[:, k, c0:c0 + n],
                                  start=(k == 0), stop=False)
                    for k in range(KD):
                        last = pe.matmul(T.ps[:, j % 8, 0:n], T.wl_t[:, 1, k, m * 128:(m + 1) * 128],
                                         T.feats[:, k, c0:c0 + n], start=False, stop=(k == KD - 1))
                    last.then_inc(S.conv_done, 1)
            pe.wait_ge(S.conv_relu, KD * 3)
            pe.wait_ge(S.conv_normed, KD)
            for t in range(NT):
                if t >= 8:
                    pe.wait_ge(S.conv_added, t - 7)
                for m in range(KD):
                    last = pe.transpose(T.ps[:P, t % 8, m * 128:(m + 1) * 128], T.conv[:, m, t * P:(t + 1) * P], T.ident[:])
                last.then_inc(S.conv_turned, 1)

        @block.scalar
        def _(act):
            for i in range(2):
                for k in range(KD):
                    act.wait_ge(S.wl_turned, 4 * i + k + 1)
                    act.activation(T.wl_t[:, i, k, :], T.ps[:, 4 * i + k, :], ACT.Copy).then_inc(S.wl_copied, 1)
            act.activation(T.ct_f[:, 0:NT // 2], T.ct[:, 0:NT // 2], ACT.Copy).then_inc(S.ct_ready, 1)
            act.activation(T.ct_f[:, NT // 2:NT], T.ct[:, NT // 2:NT], ACT.Copy).then_inc(S.ct_ready, 1)
            row_roots(act, T, S.conv_var, S.conv_std)
            copy_transposed(act, T, T.feats, S, 4)
            for m in range(KD):
                for c, (c0, n) in enumerate(CHUNKS):
                    j = 3 * m + c
                    act.wait_ge(S.conv_done, j + 1)
                    act.activation(T.conv[:, m, c0:c0 + n], T.ps[:, j % 8, 0:n], ACT.Relu, bias=T.feature[:, 0, m:m + 1])\
                       .then_inc(S.conv_relu, 1)
            act.wait_ge(S.bn_var, 1)
            act.activation(T.bn_std[:], T.bn_std[:], ACT.Sqrt).then_inc(S.bn_root, 1)
            act.wait_ge(S.bn_ready, 1)
            for m in range(KD):
                act.activation(T.conv[:, m, :], T.conv[:, m, :], ACT.Identity, bias=T.bn_shift[:, m:m + 1],
                               scale=T.bn_scale[:, m:m + 1]).then_inc(S.conv_normed, 1)

        @block.vector
        def _(dve):
            link = Chain(dve, S.dve_chain, T.dve_at)
            for t in range(NT):
                dve.wait_ge(S.y_gathered[t], 32)
                dve.wait_ge(S.bias_done, t + 1)
                for j, rows in enumerate((T.rows_a, T.rows_c)):
                    link(dve.scalar_tensor_tensor(out=T.x[:, t, :], in0=rows[:, t, :], scalar=T.gate[:, t, j:j + 1],
                                                  in1=T.x[:, t, :], op0=ALU.mult, op1=ALU.add))
                dve.tensor_tensor(T.x[:, t, :], T.ps[:P, t % 8, :], T.x[:, t, :], ALU.add).then_inc(S.moe_added, 1)
                dve.wait_ge(S.moe_added, t + 1)
                row_moments(dve, link, T, T.x, t, S.conv_var)
                dve.wait_ge(S.conv_std, t + 1)
                normalize(dve, link, T, T.rows_a, T.x, t).then_inc(S.conv_rows, 1)
            dve.wait_ge(S.degrees_done, 1)
            for c, (c0, n) in enumerate(CHUNKS):
                last = dve.tensor_scalar(T.rdeg[:, c0:c0 + n], T.ps[:, c, 0:n], 1.0, None, ALU.max)
            link(last)
            link(dve.reciprocal(T.rdeg[:], T.rdeg[:]))
            for m in range(KD):
                for c, (c0, n) in enumerate(CHUNKS):
                    j = 3 * m + c
                    dve.wait_ge(S.sums_done, j + 1)
                    dve.tensor_tensor(T.means[:, m, c0:c0 + n], T.ps[:, 3 + j % 5, 0:n], T.rdeg[:, c0:c0 + n], ALU.mult)\
                       .then_inc(S.means_ready, 1)
            for m in range(KD):
                for c, (c0, n) in enumerate(CHUNKS):
                    dve.wait_ge(S.conv_relu, 3 * m + c + 1)
                    last = dve.bn_stats(T.bn_parts[:, m, c, :], T.conv[:, m, c0:c0 + n])
            link(last)
            for m in range(KD):
                last = dve.bn_aggr(T.bn_moments[:, m, :], T.bn_parts[:, m].rearrange("p c s -> p (c s)"))
            link(last)
            dve.tensor_scalar(T.bn_std[:], T.bn_moments[:, :, 1], EPS, None, ALU.add).then_inc(S.bn_var, 1)
            dve.wait_ge(S.bn_root, 1)
            link(dve.reciprocal(T.bn_scale[:], T.bn_std[:]))
            link(dve.tensor_tensor(T.bn_scale[:], T.bn_scale[:], T.feature[:, 1, :], ALU.mult))
            link(dve.tensor_tensor(T.bn_shift[:], T.bn_moments[:, :, 0], T.bn_scale[:], ALU.mult))
            dve.tensor_tensor(T.bn_shift[:], T.feature[:, 2, :], T.bn_shift[:], ALU.subtract).then_inc(S.bn_ready, 1)
            for t in range(NT):
                dve.wait_ge(S.conv_turned, t + 1)
                dve.tensor_tensor(T.x[:, t, :], T.ps[:P, t % 8, :], T.x[:, t, :], ALU.add).then_inc(S.conv_added, 1)


def second_router(nc, T, S, A):
    with nc.Block() as block:

        @block.sync
        def _(sp):
            sp.dma_start(A.table1.rearrange("(r b) o -> r (b o)", b=NB), T.zero_ids[:, 0:NB]).then_inc(S.table1_clear, 16)
            sp.dma_start(T.w_r1, A.L1_ffn_Wr.rearrange("(k p) e -> p k e", k=KD)).then_inc(S.wr1_loaded, 16)
            sp.dma_start(T.b2_rows1, A.L1_ffn_b2).then_inc(S.b21_loaded, 16)
            sp.wait_ge(S.f_rows, NT)
            sp.dma_start(A.rows1.rearrange("(t p) d -> p t d", t=NT)[0:120], T.rows_b[0:120]).then_inc(S.rows1_stored, 16)
            sp.dma_start(A.rows1.rearrange("(t p) d -> p t d", t=NT)[120:P], T.rows_b[120:P]).then_inc(S.rows1_stored, 16)
            sp.dma_start(T.w1, A.L1_ffn_W1.rearrange("e (k p) f -> p e k f", k=KD)).then_inc(S.w12_loaded, 16)
            sp.dma_start(T.w2, A.L1_ffn_W2.rearrange("e (k p) n -> p e k n", k=F1 // 128)).then_inc(S.w12_loaded, 16)
            sp.dma_start(T.b1, A.L1_ffn_b1.rearrange("(o e) f -> o (e f)", o=1).to_broadcast([BR, E1 * F1]))\
              .then_inc(S.b11_loaded, 16)
            sp.wait_ge(S.table1_filled, 16 * NT * TOP)
            sp.dma_start(T.ids[:, 0:NB], A.table1.rearrange("(r b) o -> r (b o)", b=NB)).then_inc(S.ids1_loaded, 16)
            sp.wait_ge(S.ids1_loaded, 16)
            sp.wait_ge(S.rows1_stored, 32)

        @block.tensor
        def _(pe):
            transpose_rows(pe, T, T.rows_b, S.f_rows, S, 5)
            pe.wait_ge(S.tiles_copied, 6 * TURNS)
            pe.wait_ge(S.wr1_loaded, 16)
            for t in range(NT):
                for k in range(KD):
                    last = pe.matmul(T.ps[:P, 0, t * E1:(t + 1) * E1], T.feats[:, k, t * P:(t + 1) * P], T.w_r1[:, k, :],
                                     start=(k == 0), stop=(k == KD - 1))
            last.then_inc(S.logits1_done, 1)
            pe.wait_ge(S.chosen, 2)
            for t in range(NT):
                pe.matmul(T.ps[:, 1, 0:E1], T.ones_bf[:, 0:BR], T.onehot[:, TOP, t, 0:E1], start=(t == 0), stop=(t == NT - 1))
            count_before(pe, T, E1).then_inc(S.counted, 1)
            pe.wait_ge(S.gates_ready, 2)
            for t in range(NT):
                last = pe.transpose(T.ps[:, 4 + t // 4, t % 4 * P:(t % 4 + 1) * P], T.gate_rows[:, t, :], T.ident[:P, :P])
            last.then_inc(S.gates_turned, 1)

        @block.scalar
        def _(act):
            row_roots(act, T, S.f_var, S.f_std)
            copy_transposed(act, T, T.feats, S, 5)
            act.wait_ge(S.logits1_done, 1)
            act.activation(T.logits[:, :, 0:E1], T.ps[:P, 0, 0:NT * E1].rearrange("p (t e) -> p t e", t=NT), ACT.Copy)\
               .then_inc(S.logits1_ready, 1)
            act.wait_ge(S.gap_ready, 2)
            act.activation(T.gap[:], T.gap[:], ACT.Exp).then_inc(S.gap_exp, 1)
            act.wait_ge(S.gates_turned, 2)
            for b in range(3):
                n = min(4, NT - 4 * b)
                act.activation(T.gates_t1[:, 4 * b * P:(4 * b + n) * P], T.ps[:E1, 4 + b, 0:n * P], ACT.Copy)

        @block.vector
        def _(dve):
            link = Chain(dve, S.dve_chain, T.dve_at)
            for t in range(NT):
                row_moments(dve, link, T, T.x, t, S.f_var)
            for t in range(NT):
                dve.wait_ge(S.f_std, t + 1)
                normalize(dve, link, T, T.rows_b, T.x, t).then_inc(S.f_rows, 1)
            dve.wait_ge(S.logits1_ready, 1)
            choose(dve, link, T, E1, S.chosen, S.gap_ready)
            dve.wait_ge(S.gap_exp, 2)
            gates(dve, link, T)
            dve.wait_ge(S.counted, 2)
            positions(dve, link, T, E1)
            link(dve.tensor_copy(T.totals[:], T.ps[:, 1, 0:E1]))
            link(dve.tensor_tensor(T.below[:], T.row_starts[:].unsqueeze(1).to_broadcast([BR, E1, BLOCKS]),
                                   T.totals[:].unsqueeze(2).to_broadcast([BR, E1, BLOCKS]), ALU.is_lt))
            dve.memset(T.first_block[:, 0:1], 0.0)
            link(dve.tensor_reduce(T.totals[:], T.below[:], AX.X, ALU.add))
            for e in range(E1):
                link(dve.tensor_tensor(T.first_block[:, e + 1:e + 2], T.first_block[:, e:e + 1], T.totals[:, e:e + 1], ALU.add))
            link(dve.tensor_tensor(T.ended[:], T.block_iota[:].unsqueeze(2).to_broadcast([BR, NB, E1]),
                                   T.first_block[:, 1:E1 + 1].unsqueeze(1).to_broadcast([BR, NB, E1]), ALU.is_ge))
            link(dve.tensor_reduce(T.block_expert_f[:], T.ended[:], AX.X, ALU.add))
            dve.tensor_scalar(T.block_expert[:], T.block_expert_f[:], float(E1 - 1), None, ALU.min)
            within, row, at = T.keep, T.scratch, T.address
            choices = T.position[:].rearrange("p t j -> p (t j)")
            link(dve.tensor_tensor(T.past[:], T.row_starts[:P, 1:].unsqueeze(1).to_broadcast([P, NT * TOP, BLOCKS - 1]),
                                   choices.unsqueeze(2).to_broadcast([P, NT * TOP, BLOCKS - 1]), ALU.is_le))
            link(dve.tensor_reduce(within[:].rearrange("p t j -> p (t j)"), T.past[:], AX.X, ALU.add))
            link(dve.scalar_tensor_tensor(out=row[:], in0=within[:], scalar=-float(BR), in1=T.position[:],
                                          op0=ALU.mult, op1=ALU.add))
            for j in range(TOP):
                link(dve.tensor_tensor(T.picked[:, :, 0:E1], T.onehot[:, j, :, 0:E1],
                                       T.first_block[:P, 0:E1].unsqueeze(1).to_broadcast([P, NT, E1]), ALU.mult))
                link(dve.tensor_reduce(at[:, :, j], T.picked[:, :, 0:E1], AX.X, ALU.add))
            link(dve.tensor_tensor(within[:], within[:], at[:], ALU.add))
            link(dve.scalar_tensor_tensor(out=at[:], in0=row[:], scalar=float(NB), in1=within[:], op0=ALU.mult, op1=ALU.add))
            dve.tensor_copy(T.address_i[:], at[:]).then_inc(S.addresses_ready, 1)
            link(dve.scalar_tensor_tensor(out=row[:], in0=within[:], scalar=float(BR), in1=row[:], op0=ALU.mult, op1=ALU.add))
            dve.tensor_copy(T.row_i[:], row[:])
            gate_rows(dve, link, T, E1, S.gates_ready)

        @block.gpsimd
        def _(pool):
            pool.wait_ge(S.table1_clear, 16)
            pool.wait_ge(S.addresses_ready, 2)
            fill_table(pool, T, A.table1, BR * NB, S.table1_filled)


def second_experts(nc, T, S, A):
    FK = F1 // 128
    LOOPS = (NB - 2) // 2

    def blocks(engine, step):
        for r in range(2):
            step(0, r)
        with engine.Fori(0, LOOPS) as q:
            for r in range(2, 4):
                step(q, r)
        for r in range(2, 2 + (NB - 2) % 2):
            step(LOOPS, r)

    def is_first(q, r):
        return isinstance(q, int) and 2 * q + r == 0

    def is_last(q, r):
        return isinstance(q, int) and 2 * q + r == NB - 1

    def expert_of(engine, q, r):
        return engine.value_load(T.block_expert[0:1, bass.ds(q * 2 + r, 1)], min_val=0, max_val=E1 - 1)

    end = (LOOPS, NB - 1 - 2 * LOOPS)

    with nc.Block() as block:

        @block.gpsimd
        def _(pool):
            gather_rows(pool, T, A.rows1, T.rx, BR, NB, S.rx_ids_ready, S.rx_turned, S.rx_loaded)

        @block.tensor
        def _(pe):
            def turn(q, r):
                wait_count(pe, S.rx_loaded[r % 2], q, 16, 16 * (r // 2 + 1))
                wait_count(pe, S.rx_copied, q, 2, r - 1)
                for k in range(KD):
                    last = pe.transpose(T.ps[:, r % 2, k * BR:(k + 1) * BR], T.rx[:, r % 2, k * 128:(k + 1) * 128], T.ident[:])
                last.then_inc(S.rx_turned, 1)

            def hidden(q, r):
                e = expert_of(pe, q, r)
                wait_count(pe, S.rx_copied, q, 2, r + 1)
                wait_count(pe, S.rh_summed, q, 2, r - 1)
                for k in range(KD):
                    last = pe.matmul(T.ps[:, 2 + r % 2, 0:F1], T.rx_t[:, r % 2, k, :],
                                     T.w1[:, bass.ds(e, 1), k, :].rearrange("p o f -> p (o f)"),
                                     start=(k == 0), stop=(k == KD - 1))
                last.then_inc(S.rh_done, 1)

            def turn_hidden(q, r):
                wait_count(pe, S.rh_ready, q, 2, r + 1)
                wait_count(pe, S.rh_copied, q, 2, r - 1)
                for f in range(FK):
                    last = pe.transpose(T.ps[:, 4 + r % 2, f * BR:(f + 1) * BR], T.rh[:, r % 2, f * 128:(f + 1) * 128], T.ident[:])
                last.then_inc(S.rh_turned, 1)

            def output(q, r):
                e = expert_of(pe, q, r)
                wait_count(pe, S.rh_copied, q, 2, r + 1)
                wait_count(pe, S.ry_copied, q, 2, r - 1)
                for f in range(FK):
                    last = pe.matmul(T.ps[:, 6 + r % 2, :], T.rh_t[:, r % 2, f, :],
                                     T.w2[:, bass.ds(e, 1), f, :].rearrange("p o n -> p (o n)"),
                                     start=(f == 0), stop=(f == FK - 1))
                last.then_inc(S.ry_done, 1)

            def step(q, r):
                if not is_first(q, r):
                    turn_hidden(q, r - 1)
                hidden(q, r)
                if not is_first(q, r):
                    output(q, r - 1)
                if not is_last(q, r):
                    turn(q, r + 1)

            pe.wait_ge(S.w12_loaded, 32)
            turn(0, 0)
            blocks(pe, step)
            turn_hidden(*end)
            output(*end)

        @block.scalar
        def _(act):
            def hidden(q, r):
                wait_count(act, S.rh_summed, q, 2, r + 1)
                wait_count(act, S.rh_turned, q, 2, r - 1)
                act.activation(T.rh[:, r % 2, :], T.rh_sum[:, r % 2, :], ACT.Gelu).then_inc(S.rh_ready, 1)

            def turned(q, r):
                wait_count(act, S.rh_turned, q, 2, r + 1)
                wait_count(act, S.ry_done, q, 2, r - 1)
                act.activation(T.rh_t[:, r % 2], T.ps[:, 4 + r % 2, 0:F1].rearrange("p (f c) -> p f c", f=FK), ACT.Copy)\
                   .then_inc(S.rh_copied, 1)

            def store(q, r):
                wait_count(act, S.ry_copied, q, 2, r + 1)
                act.dma_start(A.y1[bass.ds(q * 2 + r, 1)].rearrange("o c d -> (o c) d"), T.ry[:, r % 2, :])\
                   .then_inc(S.ry_stored[r % 2], 16)

            def step(q, r):
                if not is_first(q, r):
                    turned(q, r - 1)
                hidden(q, r)
                if not is_first(q, r):
                    store(q, r - 1)

            act.preload_act_table(ACT.Gelu)
            blocks(act, step)
            turned(*end)
            store(*end)
            for slot in range(2):
                act.wait_ge(S.ry_stored[slot], 16 * ((NB + 1 - slot) // 2))

        @block.vector
        def _(dve):
            def turned(q, r):
                wait_count(dve, S.rx_turned, q, 2, r + 1)
                wait_count(dve, S.rh_done, q, 2, r - 1)
                dve.tensor_copy(T.rx_t[:, r % 2], T.ps[:, r % 2, :].rearrange("p (k c) -> p k c", k=KD)).then_inc(S.rx_copied, 1)

            def hidden(q, r):
                e = expert_of(dve, q, r)
                wait_count(dve, S.rh_done, q, 2, r + 1)
                wait_count(dve, S.rh_ready, q, 2, r - 1)
                dve.tensor_tensor(T.rh_sum[:, r % 2, :], T.ps[:, 2 + r % 2, 0:F1],
                                  T.b1_of[:, bass.ds(e, 1), :].rearrange("p o f -> p (o f)"), ALU.add).then_inc(S.rh_summed, 1)

            def output(q, r):
                wait_count(dve, S.ry_done, q, 2, r + 1)
                wait_count(dve, S.ry_stored[r % 2], q, 16, 16 * (r // 2))
                dve.tensor_copy(T.ry[:, r % 2, :], T.ps[:, 6 + r % 2, :]).then_inc(S.ry_copied, 1)

            def step(q, r):
                hidden(q, r)
                if not is_first(q, r):
                    output(q, r - 1)
                if not is_last(q, r):
                    turned(q, r + 1)

            dve.wait_ge(S.b11_loaded, 16)
            turned(0, 0)
            blocks(dve, step)
            output(*end)


def finish(nc, T, S, A):
    with nc.Block() as block:

        @block.gpsimd
        def _(pool):
            for t in range(NT):
                for j, rows in enumerate((T.rows_a, T.rows_d)):
                    pool.indirect_dma_start(rows[:, t, :], None, A.y1.rearrange("b c d -> (b c) d"),
                                            bass.IndirectOffsetOnAxis(ap=T.row_i[:, t, j:j + 1], axis=0))\
                        .then_inc(S.y_gathered[t], 16)

        @block.tensor
        def _(pe):
            pe.wait_ge(S.b21_loaded, 16)
            for t in range(NT):
                if t >= 8:
                    pe.wait_ge(S.out_ready, t - 7)
                pe.matmul(T.ps[:P, t % 8, :], T.gates_t1[:, t * P:(t + 1) * P], T.b2_rows1, start=True, stop=True)\
                  .then_inc(S.bias1_done, 1)

        @block.vector
        def _(dve):
            link = Chain(dve, S.dve_chain, T.dve_at)
            for t in range(NT):
                dve.wait_ge(S.y_gathered[t], 64)
                dve.wait_ge(S.bias1_done, t + 1)
                for j, rows in enumerate((T.rows_a, T.rows_d)):
                    link(dve.scalar_tensor_tensor(out=T.x[:, t, :], in0=rows[:, t, :], scalar=T.gate[:, t, j:j + 1],
                                                  in1=T.x[:, t, :], op0=ALU.mult, op1=ALU.add))
                dve.tensor_tensor(T.x[:, t, :], T.ps[:P, t % 8, :], T.x[:, t, :], ALU.add).then_inc(S.out_ready, 1)

        @block.sync
        def _(sp):
            for t in range(NT):
                sp.wait_ge(S.out_ready, t + 1)
                for p0, p1 in ((0, 120), (120, P)):
                    sp.dma_start(A.out[t * P + p0:t * P + p1], T.x[p0:p1, t, :]).then_inc(S.out_stored, 16)
            sp.wait_ge(S.out_stored, 32 * NT)



def semaphores_by_name(semaphores):
    S = Named()
    S.tiles_copied, S.tiles_turned = semaphores("tiles_copied tiles_turned")
    S.const_pool, S.x_loaded, S.w0_loaded = semaphores("const_pool x_loaded w0_loaded")
    S.edges_loaded, S.wq_loaded, S.affine_loaded = semaphores("edges_loaded wq_loaded affine_loaded")
    S.dve_chain, S.z_var, S.z_std = semaphores("dve_chain z_var z_std")
    S.z_rows, S.z_done, S.z_copied = semaphores("z_rows z_done z_copied")
    S.prep_done, S.prep_transposed, S.range_ready = semaphores("prep_done prep_transposed range_ready")
    S.range_transposed, S.ranges_ready, S.slot_free = semaphores("range_transposed ranges_ready slot_free")
    S.count_ready, S.parts_ready, S.window_moved = semaphores("count_ready parts_ready window_moved")
    S.bank_free, S.low_ready, S.window_done = semaphores("bank_free low_ready window_done")
    S.wk_loaded, S.agg_used, S.agg_done = semaphores("wk_loaded agg_used agg_done")
    S.attn_rows, S.xf_var, S.xf_std = semaphores("attn_rows xf_var xf_std")
    S.wv_loaded, S.proj_copied, S.proj_done = semaphores("wv_loaded proj_copied proj_done")
    S.wo_loaded, S.wr_loaded, S.exp_done = semaphores("wo_loaded wr_loaded exp_done")
    S.scores_done, S.out_copied, S.probs_copied = semaphores("scores_done out_copied probs_copied")
    S.probs_turned, S.values_done, S.max_ready = semaphores("probs_turned values_done max_ready")
    S.wo_used, S.wo_done, S.x2_rows = semaphores("wo_used wo_done x2_rows")
    S.logits_done, S.chosen, S.counted = semaphores("logits_done chosen counted")
    S.gates_ready, S.gates_turned, S.x2_var = semaphores("gates_ready gates_turned x2_var")
    S.x2_std, S.logits_ready, S.gap_ready = semaphores("x2_std logits_ready gap_ready")
    S.gap_exp, S.gates_t_ready, S.addresses_ready = semaphores("gap_exp gates_t_ready addresses_ready")
    S.rows_ready, S.table0_clear, S.rows0_stored = semaphores("rows_ready table0_clear rows0_stored")
    S.table0_filled, S.ids0_loaded = semaphores("table0_filled ids0_loaded")
    S.columns_loaded, S.ey_done, S.ex_ids_ready = semaphores("columns_loaded ey_done ex_ids_ready")
    S.ex_turned, S.ex_turned_copied, S.eh_ready = semaphores("ex_turned ex_turned_copied eh_ready")
    S.eh_done, S.ey_copied, S.columns_turned = semaphores("eh_done ey_copied columns_turned")
    S.eb1_ready, S.b2_loaded, S.wl_loaded = semaphores("eb1_ready b2_loaded wl_loaded")
    S.wl_turned, S.wl_copied, S.moe_added = semaphores("wl_turned wl_copied moe_added")
    S.bias_done, S.conv_rows, S.ct_ready = semaphores("bias_done conv_rows ct_ready")
    S.degrees_done, S.means_ready, S.sums_done = semaphores("degrees_done means_ready sums_done")
    S.conv_relu, S.conv_done, S.conv_normed = semaphores("conv_relu conv_done conv_normed")
    S.conv_added, S.conv_turned, S.conv_var = semaphores("conv_added conv_turned conv_var")
    S.conv_std, S.bn_var, S.bn_root = semaphores("conv_std bn_var bn_root")
    [S.bn_ready] = semaphores("bn_ready")
    S.ew_loaded = semaphores(" ".join(f"ew_loaded{i}" for i in range(4)))
    S.ex_loaded = semaphores(" ".join(f"ex_loaded{i}" for i in range(2)))
    S.ey_stored = semaphores(" ".join(f"ey_stored{i}" for i in range(2)))
    S.y_gathered = semaphores(" ".join(f"y_gathered{i}" for i in range(NT)))
    S.table1_clear, S.wr1_loaded, S.b21_loaded = semaphores("table1_clear wr1_loaded b21_loaded")
    S.f_rows, S.rows1_stored, S.w12_loaded = semaphores("f_rows rows1_stored w12_loaded")
    S.b11_loaded, S.table1_filled, S.ids1_loaded = semaphores("b11_loaded table1_filled ids1_loaded")
    S.logits1_done, S.f_var, S.f_std = semaphores("logits1_done f_var f_std")
    S.logits1_ready, S.rx_ids_ready, S.rx_turned = semaphores("logits1_ready rx_ids_ready rx_turned")
    S.rx_copied, S.rh_summed, S.rh_done = semaphores("rx_copied rh_summed rh_done")
    S.rh_ready, S.rh_copied, S.rh_turned = semaphores("rh_ready rh_copied rh_turned")
    S.ry_copied, S.ry_done, S.out_ready = semaphores("ry_copied ry_done out_ready")
    S.bias1_done, S.out_stored = semaphores("bias1_done out_stored")
    S.rx_loaded = semaphores(" ".join(f"rx_loaded{i}" for i in range(2)))
    S.ry_stored = semaphores(" ".join(f"ry_stored{i}" for i in range(2)))
    return S


def program(nc, A):
    with ExitStack() as stack:
        def sbuf(name, shape, dtype=F32):
            return stack.enter_context(nc.sbuf_tensor("b_" + name, shape, dtype))[:]

        def semaphores(names):
            return [stack.enter_context(nc.semaphore(name)) for name in names.split()]

        S = semaphores_by_name(semaphores)
        A.table0 = nc.dram_tensor("table0", [CAP * E0, 1], I32).ap()
        A.rows0 = nc.dram_tensor("rows0", [N, D], F32).ap()
        A.y0 = nc.dram_tensor("y0", [E0, CAP, D], F32).ap()
        A.table1 = nc.dram_tensor("table1", [BR * NB, 1], I32).ap()
        A.rows1 = nc.dram_tensor("rows1", [N, D], F32).ap()
        A.y1 = nc.dram_tensor("y1", [NB, BR, D], F32).ap()

        T = Named()
        T.dve_at = [0]
        T.ps = stack.enter_context(nc.psum_tensor("ps", [128, 8, 512], F32))

        T.x = sbuf("x", [P, NT, D])
        T.ident = sbuf("ident", [128, 128])
        T.before = sbuf("before", [P, P], BF16)
        T.ones_bf = sbuf("ones_bf", [P, 128], BF16)
        T.ones = sbuf("ones", [128, 128])
        T.zeros_bf = sbuf("zeros_bf", [P, 512], BF16)
        T.expert_iota = sbuf("expert_iota", [P, E0])
        T.block_iota = sbuf("block_iota", [BR, NB])
        T.row_starts = sbuf("row_starts", [BR, BLOCKS])
        T.token_id = sbuf("token_id", [P, NT], I32)
        T.zero_ids = sbuf("zero_ids", [128, E0], I32)
        T.ids = sbuf("ids", [128, E0], I32)
        T.ex_ids = sbuf("ex_ids", [128, 4], I32)
        T.stats = sbuf("stats", [P, 6])
        T.moments = sbuf("moments", [P, NT, 2])
        T.spread, T.std, T.rstd, T.gap = (sbuf(n, [P, NT]) for n in ("spread", "std", "rstd", "gap"))
        T.row_max, T.neg_max = (sbuf(n, [P, 4]) for n in ("row_max", "neg_max"))
        T.sums = sbuf("sums", [P, 4, 2])
        T.total = sbuf("total", [P, 2])
        T.top = sbuf("top", [P, NT, 8])
        T.top_i = sbuf("top_i", [P, NT, 8], U32)
        T.expert, T.gate, T.position, T.keep, T.address, T.scratch = (
            sbuf(n, [P, NT, TOP]) for n in ("expert", "gate", "position", "keep", "address", "scratch"))
        T.address_i, T.row_i = (sbuf(n, [P, NT, TOP], I32) for n in ("address_i", "row_i"))
        T.feature_rows = sbuf("feature_rows", [3 * KD, 128])
        T.feature = sbuf("feature", [128, 3, KD])
        T.bn_parts = sbuf("bn_parts", [128, KD, 3, 6])
        T.bn_moments = sbuf("bn_moments", [128, KD, 2])
        T.bn_std, T.bn_scale, T.bn_shift = (sbuf(n, [128, KD]) for n in ("bn_std", "bn_scale", "bn_shift"))
        T.w_r = sbuf("w_r", [128, KD, E0])
        T.lo_iota = sbuf("lo_iota", [P, P], I16)
        T.cell_iota = sbuf("cell_iota", [P, 2, WC], I16)
        T.win_first = sbuf("win_first", [CR, NWP], I16)
        T.chunk_id = sbuf("chunk_id", [CR, CJ])
        T.win_range = sbuf("win_range", [128, 128])
        T.win_end = sbuf("win_end", [128, 1])
        T.ranges = sbuf("ranges", [2, NWP], I32)
        T.w_r1 = sbuf("w_r1", [128, KD, E1])
        T.totals = sbuf("totals", [BR, E1])
        T.first_block = sbuf("first_block", [BR, E1 + 1])
        T.block_expert_f = sbuf("block_expert_f", [BR, NB])
        T.block_expert = sbuf("block_expert", [BR, NB], I32)

        w_a, w_b = (sbuf(n, [128, KD, D]) for n in ("w_a", "w_b"))
        affine = sbuf("affine", [P, 4 * D])
        r1, r2, r5, r6 = (sbuf(n, [128, NT * D]) for n in ("r1", "r2", "r5", "r6"))
        r34 = sbuf("r34", [128, NT * N + NT * N // 2])
        T.w_a, T.w_b = w_a, w_b
        T.rows_a, T.rows_b, T.rows_c, T.rows_d = (rows_of(r) for r in (r1, r5, r6, r2))
        T.feats = feats_of(r2)

        T.at = r34[:P, 0:NT * N].rearrange("p (k n) -> p k n", k=NT)
        T.ct = r34[:P, NT * N:].bitcast(U16).rearrange("p (k n) -> p k n", k=NT)
        cut = Carve(r5)
        T.dst_i, T.src_i = (cut(CR, CJ * EC, I32).rearrange("p (j e) -> p j e", j=CJ) for _ in range(2))
        T.wgt, T.dst_f, T.src_f, T.hi_f = (cut(CR, CJ * EC).rearrange("p (j e) -> p j e", j=CJ) for _ in range(4))
        T.part_bf = cut(CR, CJ * EC, BF16).rearrange("p (j e) -> p j e", j=CJ)
        T.prep = cut(CR, 5 * CJ * EC).rearrange("p (a j e) -> p a j e", a=5, j=CJ)
        T.hit = cut(CR, CJ * NWP).rearrange("p (j w) -> p j w", j=CJ)
        cut = Carve(r6)
        T.hit2 = cut(CR, CJ * NWP).rearrange("p (j w) -> p j w", j=CJ)
        T.ch_min, T.ch_max = cut(CR, CJ), cut(CR, CJ)
        T.lo_col, T.cell_col, T.w1_col, T.w2_col, T.w3_col = (cut(EC, NCH) for _ in range(5))
        T.onehot_src = cut(EC, SLOTS * P, BF16).rearrange("e (s p) -> e s p", s=SLOTS)
        T.onehot_cell = cut(EC, 4 * SLOTS * WC, BF16).rearrange("e (a c) -> e a c", a=4 * SLOTS)
        T.affine = affine[:].rearrange("p (a d) -> p a d", a=4)

        constants(nc, T, S, A)
        first_projection(nc, T, S, A)
        adjacency(nc, T, S, A)
        first_convolution(nc, T, S, A)

        cut = Carve(r34[:, 0:NT * N])
        T.qt, T.kt = (cut(128, KD * N).rearrange("p (k n) -> p k n", k=KD) for _ in range(2))
        T.probs = cut(P, 2 * N).rearrange("p (s n) -> p s n", s=2)
        T.w_v = r6[:, 0:KD * D].rearrange("p (k d) -> p k d", k=KD)
        T.probs_t = r6[:P, 0:2 * N].rearrange("p (s n) -> p s n", s=2)
        T.v, T.o, T.ot = rows_of(r1), rows_of(r2), feats_of(r6)
        projections(nc, T, S, A)
        attention(nc, T, S, A)

        def router(cut, experts):
            T.logits, T.picked = (cut(P, NT * experts).rearrange("p (t e) -> p t e", t=NT) for _ in range(2))
            T.onehot = cut(P, (TOP + 1) * NT * experts, BF16).rearrange("p (j t e) -> p j t e", j=TOP + 1, t=NT)
            T.gate_rows = cut(P, NT * 128).rearrange("p (t e) -> p t e", t=NT)

        router(Carve(r34[:, 0:NT * N]), E0)
        T.gates_t, T.b2_rows = affine[:E0, 0:N], affine[:E0, N:N + D]
        first_router(nc, T, S, A)

        cut = Carve(r34[:, 0:NT * N])
        T.ew1 = cut(128, 4 * KD * F0).rearrange("p (s k f) -> p s k f", s=4, k=KD)
        T.ew2 = cut(128, 4 * F0 // 128 * D).rearrange("p (s k n) -> p s k n", s=4, k=F0 // 128)
        T.ex = cut(128, 2 * D).rearrange("p (s d) -> p s d", s=2)
        T.ex_t = cut(128, 2 * KD * CAP).rearrange("p (s k c) -> p s k c", s=2, k=KD)
        T.eh = cut(128, 2 * F0 // 128 * CAP).rearrange("p (s f c) -> p s f c", s=2, f=F0 // 128)
        T.ey = cut(128, 2 * D).rearrange("p (s d) -> p s d", s=2)
        T.eb1_rows = cut(E0, F0)
        T.eb1 = cut(128, F0 // 128 * E0).rearrange("p (f e) -> p f e", f=F0 // 128)
        first_experts(nc, T, S, A)

        T.ct_f = r34[:P, 0:NT * N].rearrange("p (k n) -> p k n", k=NT)
        T.rdeg = r34[:, NT * N:NT * N + N]
        T.wl_t = r5[:, 0:2 * KD * D].rearrange("p (i k d) -> p i k d", i=2, k=KD)
        T.means, T.conv = feats_of(r6), feats_of(r1)
        second_convolution(nc, T, S, A)

        cut = Carve(r34)
        T.w1 = cut(128, E1 * KD * F1).rearrange("p (e k f) -> p e k f", e=E1, k=KD)
        T.w2 = cut(128, E1 * F1 // 128 * D).rearrange("p (e k n) -> p e k n", e=E1, k=F1 // 128)
        router(cut, E1)
        T.gates_t1, T.b2_rows1 = affine[:E1, 0:N], affine[:E1, N:N + D]
        T.b1 = r6[:, 0:E1 * F1]
        cut = Carve(r6, E1 * F1)
        T.below = cut(BR, E1 * BLOCKS).rearrange("p (e k) -> p e k", e=E1)
        T.ended = cut(BR, NB * E1).rearrange("p (b e) -> p b e", b=NB)
        T.past = cut(P, NT * TOP * (BLOCKS - 1)).rearrange("p (c k) -> p c k", c=NT * TOP)
        second_router(nc, T, S, A)

        T.b1_of = T.b1.rearrange("p (e f) -> p e f", e=E1)
        cut = Carve(r1)
        T.rx = cut(128, 2 * D).rearrange("p (s d) -> p s d", s=2)
        T.rx_t = cut(128, 2 * KD * BR).rearrange("p (s k c) -> p s k c", s=2, k=KD)
        T.rh_sum, T.rh = (cut(128, 2 * F1).rearrange("p (s f) -> p s f", s=2) for _ in range(2))
        T.rh_t = cut(128, 2 * F1).rearrange("p (s f c) -> p s f c", s=2, f=F1 // 128)
        T.ry = cut(128, 2 * D).rearrange("p (s d) -> p s d", s=2)
        second_experts(nc, T, S, A)
        finish(nc, T, S, A)



NAMES = ["x", "src", "dst", "edge_weight", "L0_gnn_W", "L0_ffn_ln1_g", "L0_ffn_ln1_b", "L0_ffn_wq", "L0_ffn_wk",
         "L0_ffn_wv", "L0_ffn_wo", "L0_ffn_ln2_g", "L0_ffn_ln2_b", "L0_ffn_wr", "L0_ffn_w1", "L0_ffn_b1", "L0_ffn_w2",
         "L0_ffn_b2", "L1_gnn_W_l", "L1_gnn_b_l", "L1_gnn_W_r", "L1_gnn_gamma", "L1_gnn_beta", "L1_ffn_Wr", "L1_ffn_W1",
         "L1_ffn_b1", "L1_ffn_W2", "L1_ffn_b2"]


def by_name(places, out):
    A = Named()
    (A.x, A.src, A.dst, A.edge_weight, A.L0_gnn_W, A.L0_ffn_ln1_g, A.L0_ffn_ln1_b, A.L0_ffn_wq, A.L0_ffn_wk,
     A.L0_ffn_wv, A.L0_ffn_wo, A.L0_ffn_ln2_g, A.L0_ffn_ln2_b, A.L0_ffn_wr, A.L0_ffn_w1, A.L0_ffn_b1, A.L0_ffn_w2,
     A.L0_ffn_b2, A.L1_gnn_W_l, A.L1_gnn_b_l, A.L1_gnn_W_r, A.L1_gnn_gamma, A.L1_gnn_beta, A.L1_ffn_Wr, A.L1_ffn_W1,
     A.L1_ffn_b1, A.L1_ffn_W2, A.L1_ffn_b2) = [places[name] for name in NAMES]
    A.out = out
    return A


def kernel(**inputs):
    import numpy as np
    import concourse.bacc as bacc
    from concourse.bass_utils import run_bass_kernel_spmd

    nc = bacc.Bacc("TRN2", target_bir_lowering=False, num_devices=1)
    arrays, places = {}, {}
    for name in NAMES:
        arrays[name] = np.ascontiguousarray(inputs[name])
        places[name] = nc.dram_tensor(name, arrays[name].shape, mybir.dt.from_np(arrays[name].dtype),
                                      kind="ExternalInput").ap()
    out = nc.dram_tensor("out", [N, D], F32, kind="ExternalOutput").ap()
    program(nc, by_name(places, out))
    return run_bass_kernel_spmd(nc, [arrays], core_ids=[0]).results[0]["out"]
```

```python
from contextlib import ExitStack

import concourse.bass as bass
from concourse import mybir

F32 = mybir.dt.float32
BF16 = mybir.dt.bfloat16
I16 = mybir.dt.int16
U16 = mybir.dt.uint16
I32 = mybir.dt.int32
U32 = mybir.dt.uint32
ALU = mybir.AluOpType
ACT = mybir.ActivationFunctionType
AX = mybir.AxisListType

N = 1250
D = 512
P = 125
NT = N // P
KD = D // 128
EPS = 1e-5
GROUPS = [(0, 4), (4, 4), (8, 2)]
CHUNKS = [(0, 417), (417, 417), (834, 416)]

EDGES = 41250
EC = 125
CJ = 3
NCH = EDGES // EC
NG = NCH // CJ
WD = 16
WINDOWS = -(-N // WD)
WC = NT * WD
UNROLL = 22

NH = 8
DH = D // NH
SCALE = DH ** -0.5

TOP = 2
E0, F0 = 64, 256
CAP = 2 * (N * TOP // E0)
E1, F1 = 8, 256
BR = 128
NB = (N * TOP + E1 * (BR - 1)) // BR
BLOCKS = -(-N // BR)
OUTSIDE = float(1 << 20)


class Named:
    pass


class Chain:

    def __init__(self, engine, semaphore, at):
        self.engine, self.semaphore, self.at = engine, semaphore, at

    def __call__(self, instruction):
        self.at[0] += 1
        instruction.then_inc(self.semaphore, 1)
        self.engine.wait_ge(self.semaphore, self.at[0])


class Carve:

    def __init__(self, region, start=0):
        self.region, self.at = region, start

    def __call__(self, parts, cols, dtype=F32):
        size = mybir.dt.size(dtype)
        words = -(-cols * size // 4)
        view = self.region[:, self.at:self.at + words]
        self.at += words
        assert self.at <= self.region.shape[1], (self.at, self.region.shape)
        if dtype != F32:
            view = view.bitcast(dtype)
        return view[:parts, :cols]



TURNS = len(GROUPS) * KD


def transpose_rows(pe, T, rows, ready, S, use):
    for g, (t0, n) in enumerate(GROUPS):
        if ready is not None:
            pe.wait_ge(ready, t0 + n)
        for k in range(KD):
            j = g * KD + k
            if j >= 8:
                pe.wait_ge(S.tiles_copied, use * TURNS + j - 7)
            for t in range(t0, t0 + n):
                last = pe.transpose(T.ps[:, j % 8, (t - t0) * P:(t - t0 + 1) * P],
                                    rows[:, t, k * 128:(k + 1) * 128], T.ident[:P, :P])
            last.then_inc(S.tiles_turned, 1)


def copy_transposed(act, T, out, S, use):
    for g, (t0, n) in enumerate(GROUPS):
        for k in range(KD):
            j = g * KD + k
            act.wait_ge(S.tiles_turned, use * TURNS + j + 1)
            act.activation(out[:, k, t0 * P:(t0 + n) * P], T.ps[:, j % 8, 0:n * P], ACT.Copy)\
               .then_inc(S.tiles_copied, 1)


def row_moments(dve, link, T, rows, t, var_ready):
    link(dve.bn_stats(T.stats[:], rows[:, t, :]))
    link(dve.bn_aggr(T.moments[:, t, :], T.stats[:]))
    dve.tensor_scalar(T.spread[:, t:t + 1], T.moments[:, t, 1:2], EPS, None, ALU.add).then_inc(var_ready, 1)


def row_roots(act, T, var_ready, std_ready, base=0):
    for t in range(NT):
        act.wait_ge(var_ready, base + t + 1)
        act.activation(T.std[:, t:t + 1], T.spread[:, t:t + 1], ACT.Sqrt).then_inc(std_ready, 1)


def normalize(dve, link, T, out, rows, t, gain=None, shift=None):
    link(dve.reciprocal(T.rstd[:, t:t + 1], T.std[:, t:t + 1]))
    if gain is None:
        return dve.tensor_scalar(out[:, t, :], rows[:, t, :], T.moments[:, t, 0:1], T.rstd[:, t:t + 1],
                                 ALU.subtract, ALU.mult)
    link(dve.scalar_tensor_tensor(out=out[:, t, :], in0=rows[:, t, :], scalar=T.moments[:, t, 0:1], in1=gain,
                                  op0=ALU.subtract, op1=ALU.mult))
    return dve.scalar_tensor_tensor(out=out[:, t, :], in0=out[:, t, :], scalar=T.rstd[:, t:t + 1], in1=shift,
                                    op0=ALU.mult, op1=ALU.add)


def rows_of(region, width=D):
    return region[:P, 0:NT * width].rearrange("p (t d) -> p t d", t=NT)


def feats_of(region):
    return region[:, 0:KD * N].rearrange("p (k n) -> p k n", k=KD)



def constants(nc, T, S, A):
    with nc.Block() as block:

        @block.gpsimd
        def _(pool):
            pool.memset(T.ident[:], 0.0).then_inc(S.const_pool, 1)
            pool.memset(T.before[:], 1.0).then_inc(S.const_pool, 1)
            pool.wait_ge(S.const_pool, 2)
            pool.affine_select(out=T.ident[:], in_=T.ident[:], compare_op=ALU.not_equal, fill=1.0, base=0,
                               pattern=[[-1, 128]], channel_multiplier=1)
            pool.affine_select(out=T.before[:], in_=T.before[:], compare_op=ALU.is_gt, fill=0.0, base=0,
                               pattern=[[1, P]], channel_multiplier=-1)
            exact = dict(allow_small_or_imprecise_dtypes=True)
            pool.iota(T.lo_iota[:], [[1, P]], base=0, channel_multiplier=0, **exact)
            pool.iota(T.cell_iota[:], [[1, WC]], base=0, channel_multiplier=0, **exact)
            pool.iota(T.win_starts[:], [[WD, WINDOWS]], base=0, channel_multiplier=0, **exact)
            pool.iota(T.expert_iota[:], [[1, E0]], base=0, channel_multiplier=0, **exact)
            pool.iota(T.block_iota[:], [[1, NB]], base=0, channel_multiplier=0, **exact)
            pool.iota(T.row_starts[:], [[BR, BLOCKS]], base=0, channel_multiplier=0, **exact)
            pool.iota(T.token_id[:], [[P, NT]], base=0, channel_multiplier=1, **exact)
            pool.iota(T.zero_ids[:], [[0, E0]], base=0, channel_multiplier=0, **exact)

        @block.vector
        def _(dve):
            dve.memset(T.ones_bf[:], 1.0)
            dve.memset(T.ones[:], 1.0)

        @block.sync
        def _(sp):
            sp.dma_start(T.x[0:120], A.x.rearrange("(t p) d -> p t d", t=NT)[0:120]).then_inc(S.x_loaded, 16)
            sp.dma_start(T.x[120:P], A.x.rearrange("(t p) d -> p t d", t=NT)[120:P]).then_inc(S.x_loaded, 16)
            sp.dma_start(T.w_a, A.L0_gnn_W.rearrange("(k p) n -> p k n", k=KD)).then_inc(S.w0_loaded, 16)
            sp.dma_start(T.dst_i, A.dst.rearrange("(p j e) -> p j e", j=CJ, e=EC)).then_inc(S.edges_loaded, 16)
            sp.dma_start(T.src_i, A.src.rearrange("(p j e) -> p j e", j=CJ, e=EC)).then_inc(S.edges_loaded, 16)
            sp.dma_start(T.wgt, A.edge_weight.rearrange("(p j e) -> p j e", j=CJ, e=EC)).then_inc(S.edges_loaded, 16)
            sp.dma_start(T.w_b, A.L0_ffn_wq.rearrange("(k p) n -> p k n", k=KD)).then_inc(S.wq_loaded, 16)
            for i, v in enumerate((A.L0_ffn_ln1_g, A.L0_ffn_ln1_b, A.L0_ffn_ln2_g, A.L0_ffn_ln2_b)):
                sp.dma_start(T.affine[:, i, :], v.rearrange("(o d) -> o d", o=1).to_broadcast([P, D]))\
                  .then_inc(S.affine_loaded, 16)


def first_projection(nc, T, S, A):
    with nc.Block() as block:

        @block.gpsimd
        def _(pool):
            pool.memset(T.at, 0.0)
            pool.memset(T.ct, 0.0)

        @block.vector
        def _(dve):
            link = Chain(dve, S.dve_chain, T.dve_at)
            dve.wait_ge(S.x_loaded, 32)
            for t in range(NT):
                row_moments(dve, link, T, T.x, t, S.z_var)
            for t in range(NT):
                dve.wait_ge(S.z_std, t + 1)
                normalize(dve, link, T, T.rows_a, T.x, t).then_inc(S.z_rows, 1)

        @block.scalar
        def _(act):
            row_roots(act, T, S.z_var, S.z_std)
            copy_transposed(act, T, T.feats, S, 0)
            for t in range(NT):
                act.wait_ge(S.z_done, t + 1)
                act.activation(T.rows_a[:, t, :], T.ps[:P, t % 8, :], ACT.Copy).then_inc(S.z_copied, 1)

        @block.tensor
        def _(pe):
            transpose_rows(pe, T, T.rows_a, S.z_rows, S, 0)
            pe.wait_ge(S.tiles_copied, 1 * TURNS)
            pe.wait_ge(S.w0_loaded, 16)
            for t in range(NT):
                if t >= 8:
                    pe.wait_ge(S.z_copied, t - 7)
                for k in range(KD):
                    last = pe.matmul(T.ps[:P, t % 8, :], T.feats[:, k, t * P:(t + 1) * P], T.w_a[:, k, :],
                                     start=(k == 0), stop=(k == KD - 1))
                last.then_inc(S.z_done, 1)


def adjacency(nc, T, S, A):
    LAST = N - WD

    def visits(engine, name, body, before=None):
        count = engine.alloc_register(name + "_passes")
        seen = engine.alloc_register(name + "_visits")
        engine.reg_load(count, T.passes[0:1, 0:1])
        engine.reg_mov(seen, 0)
        with engine.Fori(0, engine.snap(count, min_val=1, max_val=WINDOWS)) as r:
            if before:
                before(r)
            with engine.Fori(0, NG // UNROLL) as q:
                body(q, engine.snap(seen, min_val=0, max_val=NG * WINDOWS))
                engine.reg_add(seen, seen, UNROLL)

    def column(columns, g, width):
        return columns[:, bass.ds(g, 1), :].rearrange("e o j -> e (o j)").unsqueeze(2).to_broadcast([EC, CJ, width])

    def window(engine, sums, g):
        base = engine.value_load(T.base_row[0:1, bass.ds(g, 1)], min_val=0, max_val=LAST)
        return sums[:, :, bass.ds(base, WD)]

    def products(bank):
        return T.ps[:P, bank, 0:WC].rearrange("p (k d) -> p k d", k=NT)

    with nc.Block() as block:

        @block.vector
        def _(dve):
            link = Chain(dve, S.dve_chain, T.dve_at)
            dve.wait_ge(S.edges_loaded, 48)
            dve.tensor_copy(T.dst_f, T.dst_i)
            link(dve.tensor_copy(T.src_f, T.src_i))
            link(dve.tensor_scalar(T.hi_f, T.src_f, float(P), None, ALU.is_ge))
            for k in range(2, NT):
                link(dve.scalar_tensor_tensor(out=T.hi_f, in0=T.src_f, scalar=float(k * P), in1=T.hi_f,
                                              op0=ALU.is_ge, op1=ALU.add))
            dve.scalar_tensor_tensor(out=T.lo_row, in0=T.hi_f, scalar=-float(P), in1=T.src_f, op0=ALU.mult, op1=ALU.add)
            dve.tensor_reduce(T.group_min, T.dst_f, AX.XY, ALU.min)
            link(dve.tensor_reduce(T.group_max, T.dst_f, AX.XY, ALU.max))
            link(dve.tensor_scalar(T.group_min, T.group_min, float(LAST), None, ALU.min))
            dve.tensor_scalar(T.base_rows, T.ones[:NG, :], T.group_min, None, ALU.mult)
            link(dve.tensor_tensor(T.group_max, T.group_max, T.group_min, ALU.subtract))
            link(dve.tensor_scalar(T.further, T.win_starts[:], T.group_max, None, ALU.is_le))
            link(dve.tensor_reduce(T.group_max, T.further, AX.X, ALU.add))
            dve.sem_inc(S.prep_done, 1)
            dve.wait_ge(S.prep_transposed, 1)
            for a, columns in enumerate((T.lo_col, T.hi_col, T.dst_col, T.w_col)):
                dve.tensor_copy(columns, T.ps[:P, a, 0:NCH].rearrange("q (j p) -> q p j", p=NG))
            dve.tensor_copy(T.base_all, T.ps[:P, 4, 0:NG])
            link(dve.tensor_reduce(T.further[0:1, 0:1], T.ps[0:1, 5, 0:NG], AX.X, ALU.max))
            link(dve.tensor_copy(T.passes[:], T.further[0:1, 0:1]))
            link(dve.tensor_scalar(T.hi_col, T.hi_col, float(WD), 1.0, ALU.mult, ALU.add))
            dve.sem_inc(S.columns_ready, 1)

            def next_pass(r):
                every = T.base_all.unsqueeze(2).to_broadcast([EC, NG, CJ])
                dve.wait_ge(S.at_added, r * NG + 2)
                dve.wait_ge(S.ct_added, r * NG + 2)
                steps = [
                    lambda: dve.tensor_tensor(T.rel_col, T.dst_col, every, ALU.subtract),
                    lambda: dve.tensor_scalar(T.base_now, T.base_all, float(LAST), None, ALU.min),
                    lambda: dve.tensor_scalar(T.valid_col, T.rel_col, 0.0, None, ALU.is_ge),
                    lambda: dve.scalar_tensor_tensor(out=T.valid_col, in0=T.rel_col, scalar=float(WD), in1=T.valid_col,
                                                     op0=ALU.is_lt, op1=ALU.mult),
                    lambda: dve.tensor_tensor(T.cell_col, T.dst_col, T.base_now.unsqueeze(2).to_broadcast([EC, NG, CJ]),
                                              ALU.subtract),
                    lambda: dve.tensor_tensor(T.cell_col, T.cell_col, T.hi_col, ALU.add),
                    lambda: dve.tensor_tensor(T.cell_col, T.cell_col, T.valid_col, ALU.mult),
                    lambda: dve.tensor_scalar(T.cell_col, T.cell_col, 1.0, None, ALU.subtract),
                    lambda: dve.tensor_scalar(T.base_all, T.base_all, float(WD), None, ALU.add),
                    lambda: dve.tensor_copy(T.base_row[:], T.base_now[0:1, :]),
                ]
                for i, step in enumerate(steps):
                    if i > 0:
                        dve.wait_ge(S.pass_step, r * len(steps) + i)
                    step().then_inc(S.pass_step, 1)
    
            def add_counts(q, i, seen):
                dve.wait_ge(S.products_done, seen + (i + 3))
                sums = window(dve, T.ct, q * UNROLL + i)
                dve.wait_ge(S.ct_added, seen + (i + 2))
                dve.tensor_tensor(sums, sums, products(i % 2), ALU.add).then_inc(S.ct_added, 1)

            def body(q, seen):
                for i in range(UNROLL):
                    g, b = q * UNROLL + i, i % 2
                    dve.wait_ge(S.products_done, seen + (i + 1))
                    dve.tensor_tensor(T.sources[:, b], T.lo_iota[:].unsqueeze(1).to_broadcast([EC, CJ, P]),
                                      column(T.lo_col, g, P), ALU.is_equal).then_inc(S.sources_ready, 1)
                    dve.tensor_tensor(T.cells[:, b], T.cell_iota[:].unsqueeze(1).to_broadcast([EC, CJ, WC]),
                                      column(T.cell_col, g, WC), ALU.is_equal).then_inc(S.cells_ready, 1)
                    if i >= 2:
                        add_counts(q, i - 2, seen)
                for i in range(UNROLL - 2, UNROLL):
                    add_counts(q, i, seen)

            dve.sem_inc(S.ct_added, 2)
            visits(dve, "dve", body, next_pass)

        @block.gpsimd
        def _(pool):
            def body(q, seen):
                for i in range(UNROLL):
                    pool.wait_ge(S.weights_copied, seen + (i + 3))
                    sums = window(pool, T.at, q * UNROLL + i)
                    pool.wait_ge(S.at_added, seen + (i + 2))
                    pool.tensor_tensor(sums, sums, T.copied[:, i % 2, :].rearrange("p (k d) -> p k d", k=NT), ALU.add)\
                        .then_inc(S.at_added, 1)

            pool.sem_inc(S.at_added, 2)
            pool.wait_ge(S.columns_ready, 1)
            visits(pool, "pool", body)

        @block.scalar
        def _(act):
            def copy_weights(i, seen):
                act.wait_ge(S.products_done, seen + (i + 3))
                act.wait_ge(S.at_added, seen + (i + 1))
                act.activation(T.copied[:, i % 2, :], T.ps[:P, 2 + i % 2, 0:WC], ACT.Copy).then_inc(S.weights_copied, 1)

            def body(q, seen):
                for i in range(UNROLL):
                    act.wait_ge(S.sources_ready, seen + (i + 1))
                    for j in range(CJ):
                        last = act.activation(T.weighted[:, i % 2, j, :], T.sources[:, i % 2, j, :], ACT.Copy,
                                              scale=T.w_col[:, bass.ds(q * UNROLL + i, 1), j])
                    last.then_inc(S.weighted_ready, 1)
                    if i > 0:
                        copy_weights(i - 1, seen)
                copy_weights(UNROLL - 1, seen)

            act.sem_inc(S.weights_copied, 2)
            act.wait_ge(S.columns_ready, 1)
            act.preload_act_table(ACT.Copy)
            visits(act, "act", body)

        @block.tensor
        def _(pe):
            def body(q, seen):
                for i in range(UNROLL):
                    b = i % 2
                    pe.wait_ge(S.ct_added, seen + (i + 1))
                    pe.wait_ge(S.weights_copied, seen + (i + 1))
                    pe.wait_ge(S.cells_ready, seen + (i + 1))
                    for j in range(CJ):
                        pe.matmul(T.ps[:P, b, 0:WC], T.sources_bf[:, b, j, :, 1], T.cells_bf[:, b, j, :, 1],
                                  start=(j == 0), stop=(j == CJ - 1))
                    pe.wait_ge(S.weighted_ready, seen + (i + 1))
                    for j in range(CJ):
                        last = pe.matmul(T.ps[:P, 2 + b, 0:WC], T.weighted[:, b, j, :], T.cells[:, b, j, :],
                                         start=(j == 0), stop=(j == CJ - 1))
                    last.then_inc(S.products_done, 1)

            pe.wait_ge(S.prep_done, 1)
            for a, rows in enumerate((T.lo_row, T.hi_f, T.dst_f, T.wgt)):
                for j in range(CJ):
                    pe.transpose(T.ps[:P, a, j * NG:(j + 1) * NG], rows[:, j, :], T.ident[:NG, :NG])
            pe.transpose(T.ps[:, 4, 0:NG], T.base_rows, T.ident[:NG, :NG])
            pe.transpose(T.ps[0:1, 5, 0:NG], T.group_max, T.ident[:NG, :NG]).then_inc(S.prep_transposed, 1)
            pe.wait_ge(S.columns_ready, 1)
            pe.sem_inc(S.products_done, 2)
            visits(pe, "pe", body)



def choose(dve, link, T, experts, chosen, gap_ready):
    for t in range(NT):
        last = dve.max(T.top[:, t, :], T.logits[:, t, 0:experts])
    link(last)
    dve.tensor_tensor(T.gap[:], T.top[:, :, 1], T.top[:, :, 0], ALU.subtract).then_inc(gap_ready, 1)
    for t in range(NT):
        last = dve.max_index(T.top_i[:, t, :], T.top[:, t, :], T.logits[:, t, 0:experts])
    link(last)
    link(dve.tensor_copy(T.expert[:], T.top_i[:, :, 0:TOP]))
    which = T.expert_iota[:, 0:experts].unsqueeze(1).to_broadcast([P, NT, experts])
    for j in range(TOP):
        last = dve.tensor_tensor(T.onehot[:, j, :, 0:experts], which,
                                 T.expert[:, :, j].unsqueeze(2).to_broadcast([P, NT, experts]), ALU.is_equal)
    link(last)
    dve.tensor_tensor(T.onehot[:, TOP, :, 0:experts], T.onehot[:, 0, :, 0:experts], T.onehot[:, 1, :, 0:experts],
                      ALU.add).then_inc(chosen, 1)


def gates(dve, link, T):
    link(dve.tensor_scalar(T.gate[:, :, 0], T.gap[:], 1.0, None, ALU.add))
    link(dve.reciprocal(T.gate[:, :, 0], T.gate[:, :, 0]))
    link(dve.tensor_tensor(T.gate[:, :, 1], T.gate[:, :, 0], T.gap[:], ALU.mult))


def count_before(pe, T, experts):
    for t in range(NT):
        out = T.ps[:P, 2 + t // 5, t % 5 * experts:(t % 5 + 1) * experts]
        for u in range(t):
            pe.matmul(out, T.ones_bf[:, 0:P], T.onehot[:, TOP, u, 0:experts], start=(u == 0), stop=False)
        last = pe.matmul(out, T.before[:], T.onehot[:, TOP, t, 0:experts], start=(t == 0), stop=True)
    return last


def positions(dve, link, T, experts):
    for j in range(TOP):
        for b in range(2):
            last = dve.tensor_tensor(T.picked[:, 5 * b:5 * b + 5, 0:experts], T.onehot[:, j, 5 * b:5 * b + 5, 0:experts],
                                     T.ps[:P, 2 + b, 0:5 * experts].rearrange("p (t e) -> p t e", t=5), ALU.mult)
        link(last)
        link(dve.tensor_reduce(T.position[:, :, j], T.picked[:, :, 0:experts], AX.X, ALU.add))


def gate_rows(dve, link, T, experts, ready):
    link(dve.memset(T.gate_rows[:], 0.0))
    for j in range(TOP):
        link(dve.tensor_tensor(T.picked[:, :, 0:experts], T.onehot[:, j, :, 0:experts],
                               T.gate[:, :, j].unsqueeze(2).to_broadcast([P, NT, experts]), ALU.mult))
        last = dve.tensor_tensor(T.gate_rows[:, :, 0:experts], T.gate_rows[:, :, 0:experts], T.picked[:, :, 0:experts], ALU.add)
        if j < TOP - 1:
            link(last)
    last.then_inc(ready, 1)


def fill_table(pool, T, table, size, filled):
    for t in range(NT):
        for j in range(TOP):
            pool.indirect_dma_start(table, bass.IndirectOffsetOnAxis(ap=T.address_i[:, t, j:j + 1], axis=0),
                                    T.token_id[:, t:t + 1], None, bounds_check=size - 1, oob_is_err=False)\
                .then_inc(filled, 16)


def first_convolution(nc, T, S, A):
    with nc.Block() as block:

        @block.sync
        def _(sp):
            sp.dma_start(T.w_a, A.L0_ffn_wk.rearrange("(k p) n -> p k n", k=KD)).then_inc(S.wk_loaded, 16)

        @block.tensor
        def _(pe):
            for t in range(NT):
                if t >= 8:
                    pe.wait_ge(S.agg_used, t - 7)
                for k in range(NT):
                    last = pe.matmul(T.ps[:P, t % 8, :], T.at[:, k, t * P:(t + 1) * P], T.rows_a[:, k, :],
                                     start=(k == 0), stop=(k == NT - 1))
                last.then_inc(S.agg_done, 1)
            pe.wait_ge(S.agg_used, NT)
            transpose_rows(pe, T, T.rows_c, S.attn_rows, S, 1)

        @block.vector
        def _(dve):
            link = Chain(dve, S.dve_chain, T.dve_at)

            def residual(t):
                dve.wait_ge(S.agg_done, t + 1)
                dve.scalar_tensor_tensor(out=T.x[:, t, :], in0=T.ps[:P, t % 8, :], scalar=0.0, in1=T.x[:, t, :],
                                         op0=ALU.max, op1=ALU.add).then_inc(S.agg_used, 1)
                dve.wait_ge(S.agg_used, t + 1)
                row_moments(dve, link, T, T.x, t, S.xf_var)

            def ffn_input(t):
                dve.wait_ge(S.xf_std, 2 * t + 1)
                link(normalize(dve, link, T, T.rows_b, T.x, t))
                row_moments(dve, link, T, T.rows_b, t, S.xf_var)
                dve.wait_ge(S.xf_std, 2 * t + 2)
                normalize(dve, link, T, T.rows_c, T.rows_b, t, T.affine[:, 0, :], T.affine[:, 1, :])\
                    .then_inc(S.attn_rows, 1)

            dve.wait_ge(S.affine_loaded, 64)
            for t in range(NT):
                residual(t)
                ffn_input(t)

        @block.scalar
        def _(act):
            for t in range(NT):
                for half in range(2):
                    act.wait_ge(S.xf_var, 2 * t + half + 1)
                    act.activation(T.std[:, t:t + 1], T.spread[:, t:t + 1], ACT.Sqrt).then_inc(S.xf_std, 1)
            copy_transposed(act, T, T.feats, S, 1)


def projections(nc, T, S, A):
    with nc.Block() as block:

        @block.sync
        def _(sp):
            sp.dma_start(T.w_v, A.L0_ffn_wv.rearrange("(k p) n -> p k n", k=KD)).then_inc(S.wv_loaded, 16)

        @block.tensor
        def _(pe):
            j = 0
            for weights, loaded in ((T.w_b, S.wq_loaded), (T.w_a, S.wk_loaded)):
                pe.wait_ge(loaded, 16)
                for m in range(KD):
                    for c0, n in CHUNKS:
                        if j >= 8:
                            pe.wait_ge(S.proj_copied, j - 7)
                        for k in range(KD):
                            last = pe.matmul(T.ps[:, j % 8, 0:n], weights[:, k, m * 128:(m + 1) * 128],
                                             T.feats[:, k, c0:c0 + n], start=(k == 0), stop=(k == KD - 1))
                        last.then_inc(S.proj_done, 1)
                        j += 1

        @block.scalar
        def _(act):
            j = 0
            for out in (T.qt, T.kt):
                for m in range(KD):
                    for c0, n in CHUNKS:
                        act.wait_ge(S.proj_done, j + 1)
                        act.activation(out[:, m, c0:c0 + n], T.ps[:, j % 8, 0:n], ACT.Copy).then_inc(S.proj_copied, 1)
                        j += 1


def attention(nc, T, S, A):
    steps = [(h, t) for h in range(NH) for t in range(NT)]
    LAST = N - CHUNKS[0][1]
    starts = [0, CHUNKS[0][1], LAST]
    CW = CHUNKS[0][1]
    twice = 2 * CW - LAST
    TURNED = (7, 6, 7)

    with nc.Block() as block:

        @block.sync
        def _(sp):
            sp.dma_start(T.w_b, A.L0_ffn_wo.rearrange("(k p) n -> p k n", k=KD)).then_inc(S.wo_loaded, 16)
            sp.dma_start(T.w_r, A.L0_ffn_wr.rearrange("(k p) e -> p k e", k=KD)).then_inc(S.wr_loaded, 16)

        @block.tensor
        def _(pe):
            def scores(n, c):
                h, t = steps[n]
                b, m = DH * (h % 2), h // 2
                if c == 0 and n >= 2:
                    pe.wait_ge(S.exp_done, n - 1)
                last = pe.matmul(T.ps[:P, 3 * (n % 2) + c, 0:CW], T.qt[b:b + DH, m, t * P:(t + 1) * P],
                                 T.kt[b:b + DH, m, starts[c]:starts[c] + CW], start=True, stop=True)
                if c == 2:
                    last.then_inc(S.scores_done, 1)

            def turn(n, g):
                t0, k = GROUPS[g]
                if g == 0:
                    pe.wait_ge(S.exp_done, n + 1)
                    if n >= 1:
                        pe.wait_ge(S.probs_copied, 3 * n)
                elif g == 1 and n >= 2:
                    pe.wait_ge(S.out_copied, n - 1)
                elif g == 2:
                    pe.wait_ge(S.probs_copied, 3 * n + 1)
                for t in range(t0, t0 + k):
                    last = pe.transpose(T.ps[:P, TURNED[g], (t - t0) * P:(t - t0 + 1) * P],
                                        T.probs[:, n % 2, t * P:(t + 1) * P], T.ident[:P, :P])
                last.then_inc(S.probs_turned, 1)

            def values(n):
                h, _ = steps[n]
                pe.wait_ge(S.probs_copied, 3 * n + (5 if n + 1 < len(steps) else 3))
                if n + 1 == len(steps):
                    pe.wait_ge(S.out_copied, n)
                for k in range(NT):
                    last = pe.matmul(T.ps[:P, 6, 0:DH], T.probs_t[:, n % 2, k * P:(k + 1) * P],
                                     T.v[:, k, h * DH:(h + 1) * DH], start=(k == 0), stop=(k == NT - 1))
                last.then_inc(S.values_done, 1)

            def value_rows():
                pe.wait_ge(S.wv_loaded, 16)
                for t in range(NT):
                    if t >= 2:
                        pe.wait_ge(S.v_copied, t - 1)
                    for k in range(KD):
                        last = pe.matmul(T.ps[:P, 6 + t % 2, :], T.feats[:, k, t * P:(t + 1) * P], T.w_v[:, k, :],
                                         start=(k == 0), stop=(k == KD - 1))
                    last.then_inc(S.v_done, 1)
                pe.wait_ge(S.v_copied, NT)

            for n in range(len(steps) + 3):
                turns = 2 <= n < len(steps) + 2
                if n == 2:
                    value_rows()
                for part in range(3):
                    if turns:
                        turn(n - 2, part)
                    if n < len(steps):
                        scores(n, part)
                if n >= 3:
                    values(n - 3)

        @block.scalar
        def _(act):
            for n in range(len(steps)):
                act.wait_ge(S.max_ready, n + 1)
                if n >= 2:
                    act.wait_ge(S.probs_turned, 3 * n - 3)
                s = 3 * (n % 2)
                act.activation(T.probs[:, n % 2, 0:2 * CW].rearrange("q (c k) -> q c k", c=2), T.ps[:P, s:s + 2, 0:CW],
                               ACT.Exp, bias=T.neg_max[:, n % 4:n % 4 + 1], scale=SCALE,
                               accum_out=T.sums[:, n % 4, 0:1])
                act.activation(T.probs[:, n % 2, 2 * CW:N], T.ps[:P, s + 2, twice:CW],
                               ACT.Exp, bias=T.neg_max[:, n % 4:n % 4 + 1], scale=SCALE,
                               accum_out=T.sums[:, n % 4, 1:2]).then_inc(S.exp_done, 1)

        @block.vector
        def _(dve):
            link = Chain(dve, S.dve_chain, T.dve_at)

            def maxima(n):
                s = 3 * (n % 2)
                dve.wait_ge(S.scores_done, n + 1)
                link(dve.tensor_reduce(T.row_max[:, n % 4:n % 4 + 1], T.ps[:P, s:s + 3, 0:CW], AX.XY, ALU.max))
                dve.tensor_scalar(T.neg_max[:, n % 4:n % 4 + 1], T.row_max[:, n % 4:n % 4 + 1], -SCALE, None, ALU.mult)\
                   .then_inc(S.max_ready, 1)

            def output(n):
                h, t = steps[n]
                dve.wait_ge(S.exp_done, n + 1)
                link(dve.tensor_tensor(T.total[:, n % 2:n % 2 + 1], T.sums[:, n % 4, 0:1], T.sums[:, n % 4, 1:2], ALU.add))
                link(dve.reciprocal(T.total[:, n % 2:n % 2 + 1], T.total[:, n % 2:n % 2 + 1]))
                dve.wait_ge(S.values_done, n + 1)
                dve.tensor_scalar(T.o[:, t, h * DH:(h + 1) * DH], T.ps[:P, 6, 0:DH],
                                  T.total[:, n % 2:n % 2 + 1], None, ALU.mult).then_inc(S.out_copied, 1)

            def turned(n):
                for g, (t0, k) in enumerate(GROUPS):
                    dve.wait_ge(S.probs_turned, 3 * n + g + 1)
                    dve.tensor_copy(T.probs_t[:, n % 2, t0 * P:(t0 + k) * P], T.ps[:P, TURNED[g], 0:k * P])\
                       .then_inc(S.probs_copied, 1)

            for n in range(len(steps) + 3):
                if n == 2:
                    for t in range(NT):
                        dve.wait_ge(S.v_done, t + 1)
                        dve.tensor_copy(T.v[:, t, :], T.ps[:P, 6 + t % 2, :]).then_inc(S.v_copied, 1)
                if 2 <= n < len(steps) + 2:
                    turned(n - 2)
                if n < len(steps):
                    maxima(n)
                if n >= 3:
                    output(n - 3)


def first_router(nc, T, S, A):
    with nc.Block() as block:

        @block.tensor
        def _(pe):
            transpose_rows(pe, T, T.o, None, S, 2)
            pe.wait_ge(S.tiles_copied, 3 * TURNS)
            pe.wait_ge(S.wo_loaded, 16)
            for t in range(NT):
                if t >= 8:
                    pe.wait_ge(S.wo_used, t - 7)
                for k in range(KD):
                    last = pe.matmul(T.ps[:P, t % 8, :], T.ot[:, k, t * P:(t + 1) * P], T.w_b[:, k, :],
                                     start=(k == 0), stop=(k == KD - 1))
                last.then_inc(S.wo_done, 1)
            pe.wait_ge(S.wo_used, NT)
            transpose_rows(pe, T, T.rows_a, S.x2_rows, S, 3)
            pe.wait_ge(S.tiles_copied, 4 * TURNS)
            pe.wait_ge(S.wr_loaded, 16)
            for t in range(NT):
                for k in range(KD):
                    last = pe.matmul(T.ps[:P, t // 5, t % 5 * E0:(t % 5 + 1) * E0], T.feats[:, k, t * P:(t + 1) * P],
                                     T.w_r[:, k, :], start=(k == 0), stop=(k == KD - 1))
            last.then_inc(S.logits_done, 1)
            pe.wait_ge(S.chosen, 1)
            count_before(pe, T, E0).then_inc(S.counted, 1)
            pe.wait_ge(S.gates_ready, 1)
            for t in range(NT):
                last = pe.transpose(T.ps[:, 4 + t // 4, t % 4 * P:(t % 4 + 1) * P], T.gate_rows[:, t, :], T.ident[:P, :P])
            last.then_inc(S.gates_turned, 1)

        @block.scalar
        def _(act):
            copy_transposed(act, T, T.ot, S, 2)
            row_roots(act, T, S.x2_var, S.x2_std)
            copy_transposed(act, T, T.feats, S, 3)
            act.wait_ge(S.logits_done, 1)
            for b in range(2):
                act.activation(T.logits[:, 5 * b:5 * b + 5, 0:E0],
                               T.ps[:P, b, 0:5 * E0].rearrange("p (t e) -> p t e", t=5), ACT.Copy).then_inc(S.logits_ready, 1)
            act.wait_ge(S.gap_ready, 1)
            act.activation(T.gap[:], T.gap[:], ACT.Exp).then_inc(S.gap_exp, 1)
            act.wait_ge(S.gates_turned, 1)
            for b in range(3):
                n = min(4, NT - 4 * b)
                act.activation(T.gates_t[:, 4 * b * P:(4 * b + n) * P], T.ps[:E0, 4 + b, 0:n * P], ACT.Copy)\
                   .then_inc(S.gates_t_ready, 1)

        @block.vector
        def _(dve):
            link = Chain(dve, S.dve_chain, T.dve_at)
            for t in range(NT):
                dve.wait_ge(S.wo_done, t + 1)
                dve.tensor_tensor(T.rows_b[:, t, :], T.ps[:P, t % 8, :], T.rows_b[:, t, :], ALU.add).then_inc(S.wo_used, 1)
                dve.wait_ge(S.wo_used, t + 1)
                row_moments(dve, link, T, T.rows_b, t, S.x2_var)
                dve.tensor_tensor(T.x[:, t, :], T.x[:, t, :], T.rows_b[:, t, :], ALU.add)
                dve.wait_ge(S.x2_std, t + 1)
                normalize(dve, link, T, T.rows_a, T.rows_b, t, T.affine[:, 2, :], T.affine[:, 3, :])\
                    .then_inc(S.x2_rows, 1)
            dve.wait_ge(S.logits_ready, 2)
            choose(dve, link, T, E0, S.chosen, S.gap_ready)
            dve.wait_ge(S.gap_exp, 1)
            gates(dve, link, T)
            dve.wait_ge(S.counted, 1)
            positions(dve, link, T, E0)
            keep, at, last = T.keep, T.address, T.scratch
            link(dve.tensor_scalar(keep[:], T.position[:], float(CAP), None, ALU.is_lt))
            link(dve.tensor_tensor(T.gate[:], T.gate[:], keep[:], ALU.mult))
            link(dve.scalar_tensor_tensor(out=at[:], in0=T.position[:], scalar=float(E0), in1=T.expert[:],
                                          op0=ALU.mult, op1=ALU.add))
            link(dve.tensor_scalar(keep[:], keep[:], -OUTSIDE, OUTSIDE, ALU.mult, ALU.add))
            link(dve.tensor_tensor(at[:], at[:], keep[:], ALU.add))
            dve.tensor_copy(T.address_i[:], at[:]).then_inc(S.addresses_ready, 1)
            link(dve.tensor_scalar(last[:], T.position[:], float(CAP - 1), None, ALU.min))
            link(dve.scalar_tensor_tensor(out=last[:], in0=T.expert[:], scalar=float(CAP), in1=last[:],
                                          op0=ALU.mult, op1=ALU.add))
            dve.tensor_copy(T.row_i[:], last[:]).then_inc(S.rows_ready, 1)
            gate_rows(dve, link, T, E0, S.gates_ready)

        @block.sync
        def _(sp):
            sp.dma_start(A.table0.rearrange("(c e) o -> c (e o)", e=E0), T.zero_ids[:CAP, :]).then_inc(S.table0_clear, 16)
            sp.wait_ge(S.x2_rows, NT)
            sp.dma_start(A.rows0.rearrange("(t p) d -> p t d", t=NT), T.rows_a).then_inc(S.rows0_stored, 16)
            sp.wait_ge(S.table0_filled, 16 * NT * TOP)
            sp.dma_start(T.ids[:CAP, 0:E0], A.table0.rearrange("(c e) o -> c (e o)", e=E0)).then_inc(S.ids0_loaded, 16)
            sp.wait_ge(S.ids0_loaded, 16)
            sp.wait_ge(S.rows0_stored, 16)

        @block.gpsimd
        def _(pool):
            pool.wait_ge(S.table0_clear, 16)
            pool.wait_ge(S.addresses_ready, 1)
            fill_table(pool, T, A.table0, CAP * E0, S.table0_filled)


def wait_count(engine, semaphore, q, per, n):
    if not isinstance(q, int) or per * q + n > 0:
        engine.wait_ge(semaphore, q * per + n)


def gather_rows(pool, T, rows, slots, parts, count, ids_ready, turned, loaded):
    def column(q, r):
        pool.tensor_copy(T.ex_ids[:parts, r % 4:r % 4 + 1], T.ids[:parts, bass.ds(q * 4 + r, 1)]).then_inc(ids_ready, 1)

    def gather(q, r, last=False):
        wait_count(pool, turned, q, 4, r - 1)
        pool.wait_ge(ids_ready, q * 4 + (r + 1))
        if not last:
            column(q, r + 1)
        pool.indirect_dma_start(slots[:parts, r % 2, :], None, rows,
                                bass.IndirectOffsetOnAxis(ap=T.ex_ids[:parts, r % 4:r % 4 + 1], axis=0))\
            .then_inc(loaded[r % 2], 16)

    loops = (count - 1) // 4
    column(0, 0)
    for r in range(4):
        gather(0, r)
    with pool.Fori(1, loops) as q:
        for r in range(4):
            gather(q, r)
    for r in range(count - 4 * loops):
        gather(loops, r, 4 * loops + r == count - 1)


def first_experts(nc, T, S, A):
    WS = 4
    FK = F0 // 128
    LOOPS = (E0 - 2) // WS

    def experts(engine, step):
        for r in range(2):
            step(0, r)
        with engine.Fori(0, LOOPS) as q:
            for r in range(2, 2 + WS):
                step(q, r)
        for r in range(2, 2 + (E0 - 2) % WS):
            step(LOOPS, r)

    def is_last(q, r):
        return isinstance(q, int) and WS * q + r == E0 - 1

    with nc.Block() as block:

        @block.sync
        def _(sp):
            def load(e, slot):
                sp.dma_start(T.ew1[:, slot], A.L0_ffn_w1[bass.ds(e, 1)].rearrange("o (k p) f -> p (o k) f", k=KD))\
                  .then_inc(S.ew_loaded[slot], 16)
                sp.dma_start(T.ew2[:, slot], A.L0_ffn_w2[bass.ds(e, 1)].rearrange("o (k p) n -> p (o k) n", k=FK))\
                  .then_inc(S.ew_loaded[slot], 16)

            sp.dma_start(T.eb1_rows, A.L0_ffn_b1).then_inc(S.columns_loaded, 16)
            for i, v in enumerate((A.L1_gnn_b_l, A.L1_gnn_gamma, A.L1_gnn_beta)):
                sp.dma_start(T.feature_rows[i * KD:(i + 1) * KD], v.rearrange("(m p) -> m p", m=KD)).then_inc(S.columns_loaded, 16)
            for slot in range(WS):
                load(slot, slot)
            with sp.Fori(0, E0 // WS - 1) as q:
                for slot in range(WS):
                    sp.wait_ge(S.ey_done, q * WS + (slot + 1))
                    load(q * WS + (slot + WS), slot)

        @block.gpsimd
        def _(pool):
            gather_rows(pool, T, A.rows0, T.ex, CAP, E0, S.ex_ids_ready, S.ex_turned, S.ex_loaded)

        @block.tensor
        def _(pe):
            def turn(q, r):
                wait_count(pe, S.ex_loaded[r % 2], q, 8 * WS, 16 * (r // 2 + 1))
                wait_count(pe, S.ex_turned_copied, q, WS, r - 1)
                for k in range(KD):
                    last = pe.transpose(T.ps[:, r % 2, k * CAP:(k + 1) * CAP], T.ex[:CAP, r % 2, k * 128:(k + 1) * 128],
                                        T.ident[:CAP, :CAP])
                last.then_inc(S.ex_turned, 1)

            def hidden(q, r):
                wait_count(pe, S.ex_turned_copied, q, WS, r + 1)
                wait_count(pe, S.ew_loaded[r % WS], q, 32, 32 * (r // WS + 1))
                wait_count(pe, S.eh_ready, q, WS, r - 1)
                for f in range(FK):
                    for k in range(KD):
                        last = pe.matmul(T.ps[:, 2 + r % 2, f * CAP:(f + 1) * CAP],
                                         T.ew1[:, r % WS, k, f * 128:(f + 1) * 128], T.ex_t[:, r % 2, k, :],
                                         start=(k == 0), stop=(k == KD - 1))
                last.then_inc(S.eh_done, 1)

            def output(q, r):
                wait_count(pe, S.eh_ready, q, WS, r + 1)
                wait_count(pe, S.ey_copied, q, WS, r - 1)
                for f in range(FK):
                    last = pe.matmul(T.ps[:CAP, 4 + r % 2, :], T.eh[:, r % 2, f, :], T.ew2[:, r % WS, f, :],
                                     start=(f == 0), stop=(f == FK - 1))
                last.then_inc(S.ey_done, 1)

            def step(q, r):
                hidden(q, r)
                if not is_last(q, r):
                    turn(q, r + 1)
                if not isinstance(q, int) or WS * q + r > 0:
                    output(q, r - 1)

            pe.wait_ge(S.columns_loaded, 64)
            for f in range(FK):
                pe.transpose(T.ps[:, 7, f * E0:(f + 1) * E0], T.eb1_rows[:, f * 128:(f + 1) * 128], T.ident[:E0, :E0])
            pe.transpose(T.ps[:, 6, 0:3 * KD], T.feature_rows, T.ident[:3 * KD, :3 * KD]).then_inc(S.columns_turned, 1)
            turn(0, 0)
            experts(pe, step)
            output(LOOPS, (E0 - 1) - WS * LOOPS)

        @block.scalar
        def _(act):
            act.wait_ge(S.columns_turned, 1)
            act.activation(T.feature[:], T.ps[:, 6, 0:3 * KD].rearrange("p (i m) -> p i m", m=KD), ACT.Copy)
            act.activation(T.eb1, T.ps[:, 7, 0:FK * E0].rearrange("p (f e) -> p f e", f=FK), ACT.Copy).then_inc(S.eb1_ready, 1)
            act.preload_act_table(ACT.Gelu_apprx_tanh)
            act.wait_ge(S.eb1_ready, 1)

            def store(q, r):
                wait_count(act, S.ey_copied, q, WS, r + 1)
                act.dma_start(A.y0[bass.ds(q * WS + r, 1)].rearrange("o c d -> (o c) d"), T.ey[:CAP, r % 2, :])\
                   .then_inc(S.ey_stored[r % 2], 16)

            def step(q, r):
                wait_count(act, S.eh_done, q, WS, r + 1)
                wait_count(act, S.ey_done, q, WS, r - 1)
                for f in range(FK):
                    last = act.activation(T.eh[:, r % 2, f, :], T.ps[:, 2 + r % 2, f * CAP:(f + 1) * CAP],
                                          ACT.Gelu_apprx_tanh, bias=T.eb1[:, f, bass.ds(q * WS + r, 1)])
                last.then_inc(S.eh_ready, 1)
                if not isinstance(q, int) or WS * q + r > 0:
                    store(q, r - 1)

            experts(act, step)
            store(LOOPS, (E0 - 1) - WS * LOOPS)
            for slot in range(2):
                act.wait_ge(S.ey_stored[slot], 8 * E0)

        @block.vector
        def _(dve):
            def turned(q, r):
                wait_count(dve, S.ex_turned, q, WS, r + 1)
                wait_count(dve, S.eh_done, q, WS, r - 1)
                dve.tensor_copy(T.ex_t[:, r % 2], T.ps[:, r % 2, 0:KD * CAP].rearrange("p (k c) -> p k c", k=KD))\
                   .then_inc(S.ex_turned_copied, 1)

            def output(q, r):
                wait_count(dve, S.ey_done, q, WS, r + 1)
                wait_count(dve, S.ey_stored[r % 2], q, 8 * WS, 16 * (r // 2))
                dve.tensor_copy(T.ey[:CAP, r % 2, :], T.ps[:CAP, 4 + r % 2, :]).then_inc(S.ey_copied, 1)

            def step(q, r):
                if not is_last(q, r):
                    turned(q, r + 1)
                if not isinstance(q, int) or WS * q + r > 0:
                    output(q, r - 1)

            turned(0, 0)
            experts(dve, step)
            output(LOOPS, (E0 - 1) - WS * LOOPS)


def second_convolution(nc, T, S, A):
    with nc.Block() as block:

        @block.gpsimd
        def _(pool):
            for t in range(NT):
                for j, rows in enumerate((T.rows_a, T.rows_c)):
                    pool.indirect_dma_start(rows[:, t, :], None, A.y0.rearrange("e c d -> (e c) d"),
                                            bass.IndirectOffsetOnAxis(ap=T.row_i[:, t, j:j + 1], axis=0))\
                        .then_inc(S.y_gathered[t], 16)

        @block.sync
        def _(sp):
            sp.dma_start(T.b2_rows, A.L0_ffn_b2).then_inc(S.b2_loaded, 16)
            sp.dma_start(T.w_a, A.L1_gnn_W_l.rearrange("(m p) n -> p m n", m=KD)).then_inc(S.wl_loaded, 16)
            sp.dma_start(T.w_b, A.L1_gnn_W_r.rearrange("(m p) n -> p m n", m=KD)).then_inc(S.wl_loaded, 16)

        @block.tensor
        def _(pe):
            pe.wait_ge(S.wl_loaded, 32)
            for i, w in enumerate((T.w_a, T.w_b)):
                for k in range(KD):
                    for m in range(KD):
                        last = pe.transpose(T.ps[:, 4 * i + k, m * 128:(m + 1) * 128], w[:, m, k * 128:(k + 1) * 128],
                                            T.ident[:])
                    last.then_inc(S.wl_turned, 1)
            pe.wait_ge(S.wl_copied, 2 * KD)
            pe.wait_ge(S.ct_ready, 2)
            for c, (c0, n) in enumerate(CHUNKS):
                for k in range(NT):
                    last = pe.matmul(T.ps[:, c, 0:n], T.ones[:P, :], T.ct_f[:, k, c0:c0 + n], start=(k == 0), stop=(k == NT - 1))
            last.then_inc(S.degrees_done, 1)
            pe.wait_ge(S.b2_loaded, 16)
            pe.wait_ge(S.degrees_copied, 1)
            for t in range(NT):
                if t >= 8:
                    pe.wait_ge(S.moe_added, t - 7)
                pe.matmul(T.ps[:P, t % 8, :], T.gates_t[:, t * P:(t + 1) * P], T.b2_rows, start=True, stop=True)\
                  .then_inc(S.bias_done, 1)
            pe.wait_ge(S.moe_added, NT)
            transpose_rows(pe, T, T.rows_a, S.conv_rows, S, 4)
            pe.wait_ge(S.tiles_copied, 5 * TURNS)
            for m in range(KD):
                for c, (c0, n) in enumerate(CHUNKS):
                    j = 3 * m + c
                    if j >= 5:
                        pe.wait_ge(S.means_ready, j - 4)
                    for k in range(NT):
                        last = pe.matmul(T.ps[:, 3 + j % 5, 0:n], T.rows_a[:, k, m * 128:(m + 1) * 128],
                                         T.ct_f[:, k, c0:c0 + n], start=(k == 0), stop=(k == NT - 1))
                    last.then_inc(S.sums_done, 1)
            pe.wait_ge(S.means_ready, KD * 3)
            for m in range(KD):
                for c, (c0, n) in enumerate(CHUNKS):
                    j = 3 * m + c
                    if j >= 8:
                        pe.wait_ge(S.conv_relu, j - 7)
                    for k in range(KD):
                        pe.matmul(T.ps[:, j % 8, 0:n], T.wl_t[:, 0, k, m * 128:(m + 1) * 128], T.means[:, k, c0:c0 + n],
                                  start=(k == 0), stop=False)
                    for k in range(KD):
                        last = pe.matmul(T.ps[:, j % 8, 0:n], T.wl_t[:, 1, k, m * 128:(m + 1) * 128],
                                         T.feats[:, k, c0:c0 + n], start=False, stop=(k == KD - 1))
                    last.then_inc(S.conv_done, 1)
            pe.wait_ge(S.conv_relu, KD * 3)
            pe.wait_ge(S.conv_normed, KD)
            for t in range(NT):
                if t >= 8:
                    pe.wait_ge(S.conv_added, t - 7)
                for m in range(KD):
                    last = pe.transpose(T.ps[:P, t % 8, m * 128:(m + 1) * 128], T.conv[:, m, t * P:(t + 1) * P], T.ident[:])
                last.then_inc(S.conv_turned, 1)

        @block.scalar
        def _(act):
            for i in range(2):
                for k in range(KD):
                    act.wait_ge(S.wl_turned, 4 * i + k + 1)
                    act.activation(T.wl_t[:, i, k, :], T.ps[:, 4 * i + k, :], ACT.Copy).then_inc(S.wl_copied, 1)
            act.activation(T.ct_f[:, 0:NT // 2], T.ct[:, 0:NT // 2], ACT.Copy).then_inc(S.ct_ready, 1)
            act.activation(T.ct_f[:, NT // 2:NT], T.ct[:, NT // 2:NT], ACT.Copy).then_inc(S.ct_ready, 1)
            row_roots(act, T, S.conv_var, S.conv_std)
            copy_transposed(act, T, T.feats, S, 4)
            for m in range(KD):
                for c, (c0, n) in enumerate(CHUNKS):
                    j = 3 * m + c
                    act.wait_ge(S.conv_done, j + 1)
                    act.activation(T.conv[:, m, c0:c0 + n], T.ps[:, j % 8, 0:n], ACT.Relu, bias=T.feature[:, 0, m:m + 1])\
                       .then_inc(S.conv_relu, 1)
            act.wait_ge(S.bn_var, 1)
            act.activation(T.bn_std[:], T.bn_std[:], ACT.Sqrt).then_inc(S.bn_root, 1)
            act.wait_ge(S.bn_ready, 1)
            for m in range(KD):
                act.activation(T.conv[:, m, :], T.conv[:, m, :], ACT.Identity, bias=T.bn_shift[:, m:m + 1],
                               scale=T.bn_scale[:, m:m + 1]).then_inc(S.conv_normed, 1)

        @block.vector
        def _(dve):
            link = Chain(dve, S.dve_chain, T.dve_at)
            dve.wait_ge(S.degrees_done, 1)
            for c, (c0, n) in enumerate(CHUNKS):
                last = dve.tensor_scalar(T.rdeg[:, c0:c0 + n], T.ps[:, c, 0:n], 1.0, None, ALU.max)
            last.then_inc(S.degrees_copied, 1)
            dve.wait_ge(S.degrees_copied, 1)
            link(dve.reciprocal(T.rdeg[:], T.rdeg[:]))
            for t in range(NT):
                dve.wait_ge(S.y_gathered[t], 32)
                dve.wait_ge(S.bias_done, t + 1)
                for j, rows in enumerate((T.rows_a, T.rows_c)):
                    link(dve.scalar_tensor_tensor(out=T.x[:, t, :], in0=rows[:, t, :], scalar=T.gate[:, t, j:j + 1],
                                                  in1=T.x[:, t, :], op0=ALU.mult, op1=ALU.add))
                dve.tensor_tensor(T.x[:, t, :], T.ps[:P, t % 8, :], T.x[:, t, :], ALU.add).then_inc(S.moe_added, 1)
                dve.wait_ge(S.moe_added, t + 1)
                row_moments(dve, link, T, T.x, t, S.conv_var)
                dve.wait_ge(S.conv_std, t + 1)
                normalize(dve, link, T, T.rows_a, T.x, t).then_inc(S.conv_rows, 1)
            for m in range(KD):
                for c, (c0, n) in enumerate(CHUNKS):
                    j = 3 * m + c
                    dve.wait_ge(S.sums_done, j + 1)
                    dve.tensor_tensor(T.means[:, m, c0:c0 + n], T.ps[:, 3 + j % 5, 0:n], T.rdeg[:, c0:c0 + n], ALU.mult)\
                       .then_inc(S.means_ready, 1)
            for m in range(KD):
                for c, (c0, n) in enumerate(CHUNKS):
                    dve.wait_ge(S.conv_relu, 3 * m + c + 1)
                    last = dve.bn_stats(T.bn_parts[:, m, c, :], T.conv[:, m, c0:c0 + n])
            link(last)
            for m in range(KD):
                last = dve.bn_aggr(T.bn_moments[:, m, :], T.bn_parts[:, m].rearrange("p c s -> p (c s)"))
            link(last)
            dve.tensor_scalar(T.bn_std[:], T.bn_moments[:, :, 1], EPS, None, ALU.add).then_inc(S.bn_var, 1)
            dve.wait_ge(S.bn_root, 1)
            link(dve.reciprocal(T.bn_scale[:], T.bn_std[:]))
            link(dve.tensor_tensor(T.bn_scale[:], T.bn_scale[:], T.feature[:, 1, :], ALU.mult))
            link(dve.tensor_tensor(T.bn_shift[:], T.bn_moments[:, :, 0], T.bn_scale[:], ALU.mult))
            dve.tensor_tensor(T.bn_shift[:], T.feature[:, 2, :], T.bn_shift[:], ALU.subtract).then_inc(S.bn_ready, 1)
            for t in range(NT):
                dve.wait_ge(S.conv_turned, t + 1)
                dve.tensor_tensor(T.x[:, t, :], T.ps[:P, t % 8, :], T.x[:, t, :], ALU.add).then_inc(S.conv_added, 1)


def second_router(nc, T, S, A):
    with nc.Block() as block:

        @block.sync
        def _(sp):
            sp.dma_start(A.table1.rearrange("(r b) o -> r (b o)", b=NB), T.zero_ids[:, 0:NB]).then_inc(S.table1_clear, 16)
            sp.dma_start(T.w_r1, A.L1_ffn_Wr.rearrange("(k p) e -> p k e", k=KD)).then_inc(S.wr1_loaded, 16)
            sp.dma_start(T.b2_rows1, A.L1_ffn_b2).then_inc(S.b21_loaded, 16)
            sp.dma_start(T.w1, A.L1_ffn_W1.rearrange("e (k p) f -> p e k f", k=KD)).then_inc(S.w12_loaded, 16)
            sp.dma_start(T.w2, A.L1_ffn_W2.rearrange("e (k p) n -> p e k n", k=F1 // 128)).then_inc(S.w12_loaded, 16)
            sp.dma_start(T.b1, A.L1_ffn_b1.rearrange("(o e) f -> o (e f)", o=1).to_broadcast([BR, E1 * F1]))\
              .then_inc(S.b11_loaded, 16)
            sp.wait_ge(S.f_rows, NT)
            sp.dma_start(A.rows1.rearrange("(t p) d -> p t d", t=NT)[0:120], T.rows_b[0:120]).then_inc(S.rows1_stored, 16)
            sp.dma_start(A.rows1.rearrange("(t p) d -> p t d", t=NT)[120:P], T.rows_b[120:P]).then_inc(S.rows1_stored, 16)
            sp.wait_ge(S.table1_filled, 16 * NT * TOP)
            sp.dma_start(T.ids[:, 0:NB], A.table1.rearrange("(r b) o -> r (b o)", b=NB)).then_inc(S.ids1_loaded, 16)
            sp.wait_ge(S.ids1_loaded, 16)
            sp.wait_ge(S.rows1_stored, 32)

        @block.tensor
        def _(pe):
            transpose_rows(pe, T, T.rows_b, S.f_rows, S, 5)
            pe.wait_ge(S.tiles_copied, 6 * TURNS)
            pe.wait_ge(S.wr1_loaded, 16)
            for t in range(NT):
                for k in range(KD):
                    last = pe.matmul(T.ps[:P, 0, t * E1:(t + 1) * E1], T.feats[:, k, t * P:(t + 1) * P], T.w_r1[:, k, :],
                                     start=(k == 0), stop=(k == KD - 1))
            last.then_inc(S.logits1_done, 1)
            pe.wait_ge(S.chosen, 2)
            for t in range(NT):
                pe.matmul(T.ps[:, 1, 0:E1], T.ones_bf[:, 0:BR], T.onehot[:, TOP, t, 0:E1], start=(t == 0), stop=(t == NT - 1))
            count_before(pe, T, E1).then_inc(S.counted, 1)
            pe.wait_ge(S.gates_ready, 2)
            for t in range(NT):
                last = pe.transpose(T.ps[:, 4 + t // 4, t % 4 * P:(t % 4 + 1) * P], T.gate_rows[:, t, :], T.ident[:P, :P])
            last.then_inc(S.gates_turned, 1)

        @block.scalar
        def _(act):
            row_roots(act, T, S.f_var, S.f_std)
            copy_transposed(act, T, T.feats, S, 5)
            act.wait_ge(S.logits1_done, 1)
            act.activation(T.logits[:, :, 0:E1], T.ps[:P, 0, 0:NT * E1].rearrange("p (t e) -> p t e", t=NT), ACT.Copy)\
               .then_inc(S.logits1_ready, 1)
            act.wait_ge(S.gap_ready, 2)
            act.activation(T.gap[:], T.gap[:], ACT.Exp).then_inc(S.gap_exp, 1)
            act.wait_ge(S.gates_turned, 2)
            for b in range(3):
                n = min(4, NT - 4 * b)
                act.activation(T.gates_t1[:, 4 * b * P:(4 * b + n) * P], T.ps[:E1, 4 + b, 0:n * P], ACT.Copy)

        @block.vector
        def _(dve):
            link = Chain(dve, S.dve_chain, T.dve_at)
            for t in range(NT):
                row_moments(dve, link, T, T.x, t, S.f_var)
            for t in range(NT):
                dve.wait_ge(S.f_std, t + 1)
                normalize(dve, link, T, T.rows_b, T.x, t).then_inc(S.f_rows, 1)
            dve.wait_ge(S.logits1_ready, 1)
            choose(dve, link, T, E1, S.chosen, S.gap_ready)
            dve.wait_ge(S.gap_exp, 2)
            gates(dve, link, T)
            dve.wait_ge(S.counted, 2)
            positions(dve, link, T, E1)
            link(dve.tensor_copy(T.totals[:], T.ps[:, 1, 0:E1]))
            link(dve.tensor_tensor(T.below[:], T.row_starts[:].unsqueeze(1).to_broadcast([BR, E1, BLOCKS]),
                                   T.totals[:].unsqueeze(2).to_broadcast([BR, E1, BLOCKS]), ALU.is_lt))
            dve.memset(T.first_block[:, 0:1], 0.0)
            link(dve.tensor_reduce(T.totals[:], T.below[:], AX.X, ALU.add))
            for e in range(E1):
                link(dve.tensor_tensor(T.first_block[:, e + 1:e + 2], T.first_block[:, e:e + 1], T.totals[:, e:e + 1], ALU.add))
            link(dve.tensor_tensor(T.ended[:], T.block_iota[:].unsqueeze(2).to_broadcast([BR, NB, E1]),
                                   T.first_block[:, 1:E1 + 1].unsqueeze(1).to_broadcast([BR, NB, E1]), ALU.is_ge))
            link(dve.tensor_reduce(T.block_expert_f[:], T.ended[:], AX.X, ALU.add))
            dve.tensor_scalar(T.block_expert[:], T.block_expert_f[:], float(E1 - 1), None, ALU.min)
            within, row, at = T.keep, T.scratch, T.address
            choices = T.position[:].rearrange("p t j -> p (t j)")
            link(dve.tensor_tensor(T.past[:], T.row_starts[:P, 1:].unsqueeze(1).to_broadcast([P, NT * TOP, BLOCKS - 1]),
                                   choices.unsqueeze(2).to_broadcast([P, NT * TOP, BLOCKS - 1]), ALU.is_le))
            link(dve.tensor_reduce(within[:].rearrange("p t j -> p (t j)"), T.past[:], AX.X, ALU.add))
            link(dve.scalar_tensor_tensor(out=row[:], in0=within[:], scalar=-float(BR), in1=T.position[:],
                                          op0=ALU.mult, op1=ALU.add))
            for j in range(TOP):
                link(dve.tensor_tensor(T.picked[:, :, 0:E1], T.onehot[:, j, :, 0:E1],
                                       T.first_block[:P, 0:E1].unsqueeze(1).to_broadcast([P, NT, E1]), ALU.mult))
                link(dve.tensor_reduce(at[:, :, j], T.picked[:, :, 0:E1], AX.X, ALU.add))
            link(dve.tensor_tensor(within[:], within[:], at[:], ALU.add))
            link(dve.scalar_tensor_tensor(out=at[:], in0=row[:], scalar=float(NB), in1=within[:], op0=ALU.mult, op1=ALU.add))
            dve.tensor_copy(T.address_i[:], at[:]).then_inc(S.addresses_ready, 1)
            link(dve.scalar_tensor_tensor(out=row[:], in0=within[:], scalar=float(BR), in1=row[:], op0=ALU.mult, op1=ALU.add))
            dve.tensor_copy(T.row_i[:], row[:])
            gate_rows(dve, link, T, E1, S.gates_ready)

        @block.gpsimd
        def _(pool):
            pool.wait_ge(S.table1_clear, 16)
            pool.wait_ge(S.addresses_ready, 2)
            fill_table(pool, T, A.table1, BR * NB, S.table1_filled)


def second_experts(nc, T, S, A):
    FK = F1 // 128
    LOOPS = (NB - 2) // 2

    def blocks(engine, step):
        for r in range(2):
            step(0, r)
        with engine.Fori(0, LOOPS) as q:
            for r in range(2, 4):
                step(q, r)
        for r in range(2, 2 + (NB - 2) % 2):
            step(LOOPS, r)

    def is_first(q, r):
        return isinstance(q, int) and 2 * q + r == 0

    def is_last(q, r):
        return isinstance(q, int) and 2 * q + r == NB - 1

    def expert_of(engine, q, r):
        return engine.value_load(T.block_expert[0:1, bass.ds(q * 2 + r, 1)], min_val=0, max_val=E1 - 1)

    end = (LOOPS, NB - 1 - 2 * LOOPS)

    with nc.Block() as block:

        @block.gpsimd
        def _(pool):
            gather_rows(pool, T, A.rows1, T.rx, BR, NB, S.rx_ids_ready, S.rx_turned, S.rx_loaded)

        @block.tensor
        def _(pe):
            def turn(q, r):
                wait_count(pe, S.rx_loaded[r % 2], q, 16, 16 * (r // 2 + 1))
                wait_count(pe, S.rx_copied, q, 2, r - 1)
                for k in range(KD):
                    last = pe.transpose(T.ps[:, r % 2, k * BR:(k + 1) * BR], T.rx[:, r % 2, k * 128:(k + 1) * 128], T.ident[:])
                last.then_inc(S.rx_turned, 1)

            def hidden(q, r):
                e = expert_of(pe, q, r)
                wait_count(pe, S.rx_copied, q, 2, r + 1)
                wait_count(pe, S.rh_summed, q, 2, r - 1)
                for k in range(KD):
                    last = pe.matmul(T.ps[:, 2 + r % 2, 0:F1], T.rx_t[:, r % 2, k, :],
                                     T.w1[:, bass.ds(e, 1), k, :].rearrange("p o f -> p (o f)"),
                                     start=(k == 0), stop=(k == KD - 1))
                last.then_inc(S.rh_done, 1)

            def turn_hidden(q, r):
                wait_count(pe, S.rh_ready, q, 2, r + 1)
                wait_count(pe, S.rh_copied, q, 2, r - 1)
                for f in range(FK):
                    last = pe.transpose(T.ps[:, 4 + r % 2, f * BR:(f + 1) * BR], T.rh[:, r % 2, f * 128:(f + 1) * 128], T.ident[:])
                last.then_inc(S.rh_turned, 1)

            def output(q, r):
                e = expert_of(pe, q, r)
                wait_count(pe, S.rh_copied, q, 2, r + 1)
                wait_count(pe, S.ry_copied, q, 2, r - 1)
                for f in range(FK):
                    last = pe.matmul(T.ps[:, 6 + r % 2, :], T.rh_t[:, r % 2, f, :],
                                     T.w2[:, bass.ds(e, 1), f, :].rearrange("p o n -> p (o n)"),
                                     start=(f == 0), stop=(f == FK - 1))
                last.then_inc(S.ry_done, 1)

            def step(q, r):
                if not is_first(q, r):
                    turn_hidden(q, r - 1)
                hidden(q, r)
                if not is_last(q, r):
                    turn(q, r + 1)
                if not is_first(q, r):
                    output(q, r - 1)

            pe.wait_ge(S.w12_loaded, 32)
            turn(0, 0)
            blocks(pe, step)
            turn_hidden(*end)
            output(*end)

        @block.scalar
        def _(act):
            def hidden(q, r):
                wait_count(act, S.rh_summed, q, 2, r + 1)
                wait_count(act, S.rh_turned, q, 2, r - 1)
                act.activation(T.rh[:, r % 2, :], T.rh_sum[:, r % 2, :], ACT.Gelu).then_inc(S.rh_ready, 1)

            def turned(q, r):
                wait_count(act, S.rh_turned, q, 2, r + 1)
                wait_count(act, S.ry_done, q, 2, r - 1)
                act.activation(T.rh_t[:, r % 2], T.ps[:, 4 + r % 2, 0:F1].rearrange("p (f c) -> p f c", f=FK), ACT.Copy)\
                   .then_inc(S.rh_copied, 1)

            def store(q, r):
                wait_count(act, S.ry_copied, q, 2, r + 1)
                act.dma_start(A.y1[bass.ds(q * 2 + r, 1)].rearrange("o c d -> (o c) d"), T.ry[:, r % 2, :])\
                   .then_inc(S.ry_stored[r % 2], 16)

            def step(q, r):
                if not is_first(q, r):
                    turned(q, r - 1)
                hidden(q, r)
                if not is_first(q, r):
                    store(q, r - 1)

            act.preload_act_table(ACT.Gelu)
            blocks(act, step)
            turned(*end)
            store(*end)
            for slot in range(2):
                act.wait_ge(S.ry_stored[slot], 16 * ((NB + 1 - slot) // 2))

        @block.vector
        def _(dve):
            def turned(q, r):
                wait_count(dve, S.rx_turned, q, 2, r + 1)
                wait_count(dve, S.rh_done, q, 2, r - 1)
                dve.tensor_copy(T.rx_t[:, r % 2], T.ps[:, r % 2, :].rearrange("p (k c) -> p k c", k=KD)).then_inc(S.rx_copied, 1)

            def hidden(q, r):
                e = expert_of(dve, q, r)
                wait_count(dve, S.rh_done, q, 2, r + 1)
                wait_count(dve, S.rh_ready, q, 2, r - 1)
                dve.tensor_tensor(T.rh_sum[:, r % 2, :], T.ps[:, 2 + r % 2, 0:F1],
                                  T.b1_of[:, bass.ds(e, 1), :].rearrange("p o f -> p (o f)"), ALU.add).then_inc(S.rh_summed, 1)

            def output(q, r):
                wait_count(dve, S.ry_done, q, 2, r + 1)
                wait_count(dve, S.ry_stored[r % 2], q, 16, 16 * (r // 2))
                dve.tensor_copy(T.ry[:, r % 2, :], T.ps[:, 6 + r % 2, :]).then_inc(S.ry_copied, 1)

            def step(q, r):
                hidden(q, r)
                if not is_last(q, r):
                    turned(q, r + 1)
                if not is_first(q, r):
                    output(q, r - 1)

            dve.wait_ge(S.b11_loaded, 16)
            turned(0, 0)
            blocks(dve, step)
            output(*end)


def finish(nc, T, S, A):
    with nc.Block() as block:

        @block.gpsimd
        def _(pool):
            for t in range(NT):
                for j, rows in enumerate((T.rows_a, T.rows_d)):
                    pool.indirect_dma_start(rows[:, t, :], None, A.y1.rearrange("b c d -> (b c) d"),
                                            bass.IndirectOffsetOnAxis(ap=T.row_i[:, t, j:j + 1], axis=0))\
                        .then_inc(S.y_gathered[t], 16)

        @block.tensor
        def _(pe):
            pe.wait_ge(S.b21_loaded, 16)
            for t in range(NT):
                if t >= 8:
                    pe.wait_ge(S.out_ready, t - 7)
                pe.matmul(T.ps[:P, t % 8, :], T.gates_t1[:, t * P:(t + 1) * P], T.b2_rows1, start=True, stop=True)\
                  .then_inc(S.bias1_done, 1)

        @block.vector
        def _(dve):
            link = Chain(dve, S.dve_chain, T.dve_at)
            for t in range(NT):
                dve.wait_ge(S.y_gathered[t], 64)
                dve.wait_ge(S.bias1_done, t + 1)
                for j, rows in enumerate((T.rows_a, T.rows_d)):
                    link(dve.scalar_tensor_tensor(out=T.x[:, t, :], in0=rows[:, t, :], scalar=T.gate[:, t, j:j + 1],
                                                  in1=T.x[:, t, :], op0=ALU.mult, op1=ALU.add))
                dve.tensor_tensor(T.x[:, t, :], T.ps[:P, t % 8, :], T.x[:, t, :], ALU.add).then_inc(S.out_ready, 1)

        @block.sync
        def _(sp):
            for t in range(NT):
                sp.wait_ge(S.out_ready, t + 1)
                for p0, p1 in ((0, 120), (120, P)):
                    sp.dma_start(A.out[t * P + p0:t * P + p1], T.x[p0:p1, t, :]).then_inc(S.out_stored, 16)
            sp.wait_ge(S.out_stored, 32 * NT)



def semaphores_by_name(semaphores):
    S = Named()
    S.tiles_copied, S.tiles_turned = semaphores("tiles_copied tiles_turned")
    S.const_pool, S.x_loaded, S.w0_loaded = semaphores("const_pool x_loaded w0_loaded")
    S.edges_loaded, S.wq_loaded, S.affine_loaded = semaphores("edges_loaded wq_loaded affine_loaded")
    S.dve_chain, S.z_var, S.z_std = semaphores("dve_chain z_var z_std")
    S.z_rows, S.z_done, S.z_copied = semaphores("z_rows z_done z_copied")
    S.prep_done, S.prep_transposed, S.columns_ready = semaphores("prep_done prep_transposed columns_ready")
    S.at_added, S.ct_added, S.pass_step = semaphores("at_added ct_added pass_step")
    S.products_done, S.sources_ready, S.cells_ready = semaphores("products_done sources_ready cells_ready")
    S.weights_copied, S.weighted_ready = semaphores("weights_copied weighted_ready")
    S.wk_loaded, S.agg_used, S.agg_done = semaphores("wk_loaded agg_used agg_done")
    S.attn_rows, S.xf_var, S.xf_std = semaphores("attn_rows xf_var xf_std")
    S.wv_loaded, S.proj_copied, S.proj_done = semaphores("wv_loaded proj_copied proj_done")
    S.wo_loaded, S.wr_loaded, S.exp_done = semaphores("wo_loaded wr_loaded exp_done")
    S.scores_done, S.probs_copied, S.out_copied = semaphores("scores_done probs_copied out_copied")
    S.probs_turned, S.values_done, S.v_copied = semaphores("probs_turned values_done v_copied")
    S.v_done, S.max_ready, S.wo_used = semaphores("v_done max_ready wo_used")
    S.wo_done, S.x2_rows, S.logits_done = semaphores("wo_done x2_rows logits_done")
    S.chosen, S.counted, S.gates_ready = semaphores("chosen counted gates_ready")
    S.gates_turned, S.x2_var, S.x2_std = semaphores("gates_turned x2_var x2_std")
    S.logits_ready, S.gap_ready, S.gap_exp = semaphores("logits_ready gap_ready gap_exp")
    S.gates_t_ready, S.addresses_ready, S.rows_ready = semaphores("gates_t_ready addresses_ready rows_ready")
    S.table0_clear, S.rows0_stored, S.table0_filled = semaphores("table0_clear rows0_stored table0_filled")
    [S.ids0_loaded] = semaphores("ids0_loaded")
    S.columns_loaded, S.ey_done, S.ex_ids_ready = semaphores("columns_loaded ey_done ex_ids_ready")
    S.ex_turned, S.ex_turned_copied, S.eh_ready = semaphores("ex_turned ex_turned_copied eh_ready")
    S.eh_done, S.ey_copied, S.columns_turned = semaphores("eh_done ey_copied columns_turned")
    S.eb1_ready, S.b2_loaded, S.wl_loaded = semaphores("eb1_ready b2_loaded wl_loaded")
    S.wl_turned, S.wl_copied, S.ct_ready = semaphores("wl_turned wl_copied ct_ready")
    S.degrees_done, S.degrees_copied, S.moe_added = semaphores("degrees_done degrees_copied moe_added")
    S.bias_done, S.conv_rows, S.means_ready = semaphores("bias_done conv_rows means_ready")
    S.sums_done, S.conv_relu, S.conv_done = semaphores("sums_done conv_relu conv_done")
    S.conv_normed, S.conv_added, S.conv_turned = semaphores("conv_normed conv_added conv_turned")
    S.conv_var, S.conv_std, S.bn_var = semaphores("conv_var conv_std bn_var")
    S.bn_root, S.bn_ready = semaphores("bn_root bn_ready")
    S.ew_loaded = semaphores(" ".join(f"ew_loaded{i}" for i in range(4)))
    S.ex_loaded = semaphores(" ".join(f"ex_loaded{i}" for i in range(2)))
    S.ey_stored = semaphores(" ".join(f"ey_stored{i}" for i in range(2)))
    S.y_gathered = semaphores(" ".join(f"y_gathered{i}" for i in range(NT)))
    S.table1_clear, S.wr1_loaded, S.b21_loaded = semaphores("table1_clear wr1_loaded b21_loaded")
    S.w12_loaded, S.b11_loaded, S.f_rows = semaphores("w12_loaded b11_loaded f_rows")
    S.rows1_stored, S.table1_filled, S.ids1_loaded = semaphores("rows1_stored table1_filled ids1_loaded")
    S.logits1_done, S.f_var, S.f_std = semaphores("logits1_done f_var f_std")
    S.logits1_ready, S.rx_ids_ready, S.rx_turned = semaphores("logits1_ready rx_ids_ready rx_turned")
    S.rx_copied, S.rh_summed, S.rh_done = semaphores("rx_copied rh_summed rh_done")
    S.rh_ready, S.rh_copied, S.rh_turned = semaphores("rh_ready rh_copied rh_turned")
    S.ry_copied, S.ry_done, S.out_ready = semaphores("ry_copied ry_done out_ready")
    S.bias1_done, S.out_stored = semaphores("bias1_done out_stored")
    S.rx_loaded = semaphores(" ".join(f"rx_loaded{i}" for i in range(2)))
    S.ry_stored = semaphores(" ".join(f"ry_stored{i}" for i in range(2)))
    return S


def program(nc, A):
    with ExitStack() as stack:
        def sbuf(name, shape, dtype=F32):
            return stack.enter_context(nc.sbuf_tensor("b_" + name, shape, dtype))[:]

        def semaphores(names):
            return [stack.enter_context(nc.semaphore(name)) for name in names.split()]

        S = semaphores_by_name(semaphores)
        A.table0 = nc.dram_tensor("table0", [CAP * E0, 1], I32).ap()
        A.rows0 = nc.dram_tensor("rows0", [N, D], F32).ap()
        A.y0 = nc.dram_tensor("y0", [E0, CAP, D], F32).ap()
        A.table1 = nc.dram_tensor("table1", [BR * NB, 1], I32).ap()
        A.rows1 = nc.dram_tensor("rows1", [N, D], F32).ap()
        A.y1 = nc.dram_tensor("y1", [NB, BR, D], F32).ap()

        T = Named()
        T.dve_at = [0]
        T.ps = stack.enter_context(nc.psum_tensor("ps", [128, 8, 512], F32))

        T.x = sbuf("x", [P, NT, D])
        T.ident = sbuf("ident", [128, 128])
        T.before = sbuf("before", [P, P], BF16)
        T.ones_bf = sbuf("ones_bf", [P, 128], BF16)
        T.ones = sbuf("ones", [128, 128])
        T.expert_iota = sbuf("expert_iota", [P, E0])
        T.block_iota = sbuf("block_iota", [BR, NB])
        T.row_starts = sbuf("row_starts", [BR, BLOCKS])
        T.token_id = sbuf("token_id", [P, NT], I32)
        T.zero_ids = sbuf("zero_ids", [128, E0], I32)
        T.ids = sbuf("ids", [128, E0], I32)
        T.ex_ids = sbuf("ex_ids", [128, 4], I32)
        T.stats = sbuf("stats", [P, 6])
        T.moments = sbuf("moments", [P, NT, 2])
        T.spread, T.std, T.rstd, T.gap = (sbuf(n, [P, NT]) for n in ("spread", "std", "rstd", "gap"))
        T.row_max, T.neg_max = (sbuf(n, [P, 4]) for n in ("row_max", "neg_max"))
        T.sums = sbuf("sums", [P, 4, 2])
        T.total = sbuf("total", [P, 2])
        T.top = sbuf("top", [P, NT, 8])
        T.top_i = sbuf("top_i", [P, NT, 8], U32)
        T.expert, T.gate, T.position, T.keep, T.address, T.scratch = (
            sbuf(n, [P, NT, TOP]) for n in ("expert", "gate", "position", "keep", "address", "scratch"))
        T.address_i, T.row_i = (sbuf(n, [P, NT, TOP], I32) for n in ("address_i", "row_i"))
        T.feature_rows = sbuf("feature_rows", [3 * KD, 128])
        T.feature = sbuf("feature", [128, 3, KD])
        T.bn_parts = sbuf("bn_parts", [128, KD, 3, 6])
        T.bn_moments = sbuf("bn_moments", [128, KD, 2])
        T.bn_std, T.bn_scale, T.bn_shift = (sbuf(n, [128, KD]) for n in ("bn_std", "bn_scale", "bn_shift"))
        T.w_r = sbuf("w_r", [128, KD, E0])
        T.lo_iota = sbuf("lo_iota", [P, P], I16)
        T.cell_iota = sbuf("cell_iota", [P, WC], I16)
        T.win_starts = sbuf("win_starts", [NG, WINDOWS], I16)
        T.base_row = sbuf("base_row", [1, NG], I32)
        T.passes = sbuf("passes", [1, 1], I32)
        T.w_r1 = sbuf("w_r1", [128, KD, E1])
        T.totals = sbuf("totals", [BR, E1])
        T.first_block = sbuf("first_block", [BR, E1 + 1])
        T.block_expert_f = sbuf("block_expert_f", [BR, NB])
        T.block_expert = sbuf("block_expert", [BR, NB], I32)

        w_a, w_b = (sbuf(n, [128, KD, D]) for n in ("w_a", "w_b"))
        affine = sbuf("affine", [P, 4 * D])
        r1, r2, r5, r6 = (sbuf(n, [128, NT * D]) for n in ("r1", "r2", "r5", "r6"))
        r34 = sbuf("r34", [128, NT * N + NT * N // 2])
        T.w_a, T.w_b = w_a, w_b
        T.rows_a, T.rows_b, T.rows_c, T.rows_d = (rows_of(r) for r in (r1, r5, r6, r2))
        T.feats = feats_of(r2)

        T.at = r34[:P, 0:NT * N].rearrange("p (k n) -> p k n", k=NT)
        T.ct = r34[:P, NT * N:].bitcast(U16).rearrange("p (k n) -> p k n", k=NT)
        cut = Carve(r5)
        T.dst_i, T.src_i = (cut(NG, CJ * EC, I32).rearrange("p (j e) -> p j e", j=CJ) for _ in range(2))
        T.wgt, T.dst_f, T.src_f, T.hi_f, T.lo_row, T.cell_row = (
            cut(NG, CJ * EC).rearrange("p (j e) -> p j e", j=CJ) for _ in range(6))
        T.base_rows = cut(NG, 128)
        T.further = cut(NG, WINDOWS)
        T.group_min, T.group_max = cut(NG, 1), cut(NG, 1)
        T.base_all, T.base_now = cut(EC, NG), cut(EC, NG)
        cut = Carve(r2)
        T.lo_col, T.hi_col, T.dst_col, T.w_col, T.rel_col, T.valid_col, T.cell_col = (
            cut(EC, NG * CJ).rearrange("e (g j) -> e g j", j=CJ) for _ in range(7))
        cut = Carve(r6)
        T.sources = cut(EC, 2 * CJ * P).rearrange("e (b j s) -> e b j s", b=2, j=CJ)
        T.weighted = cut(EC, 2 * CJ * P).rearrange("e (b j s) -> e b j s", b=2, j=CJ)
        T.cells = cut(EC, 2 * CJ * WC).rearrange("e (b j c) -> e b j c", b=2, j=CJ)
        T.copied = cut(P, 2 * WC).rearrange("p (b c) -> p b c", b=2)
        T.sources_bf = r6[:EC, 0:2 * CJ * P].bitcast(BF16).rearrange("e (b j s h) -> e b j s h", b=2, j=CJ, h=2)
        T.cells_bf = r6[:EC, 4 * CJ * P:4 * CJ * P + 2 * CJ * WC].bitcast(BF16)\
            .rearrange("e (b j c h) -> e b j c h", b=2, j=CJ, h=2)
        T.affine = affine[:].rearrange("p (a d) -> p a d", a=4)

        constants(nc, T, S, A)
        first_projection(nc, T, S, A)
        adjacency(nc, T, S, A)
        first_convolution(nc, T, S, A)

        cut = Carve(r34[:, 0:NT * N])
        T.qt, T.kt = (cut(128, KD * N).rearrange("p (k n) -> p k n", k=KD) for _ in range(2))
        T.probs = cut(P, 2 * N).rearrange("p (s n) -> p s n", s=2)
        T.w_v = r6[:, 0:KD * D].rearrange("p (k d) -> p k d", k=KD)
        T.probs_t = r6[:P, 0:2 * N].rearrange("p (s n) -> p s n", s=2)
        T.v, T.o, T.ot = rows_of(r1), rows_of(r2), feats_of(r6)
        projections(nc, T, S, A)
        attention(nc, T, S, A)

        def router(cut, experts):
            T.logits, T.picked = (cut(P, NT * experts).rearrange("p (t e) -> p t e", t=NT) for _ in range(2))
            T.onehot = cut(P, (TOP + 1) * NT * experts, BF16).rearrange("p (j t e) -> p j t e", j=TOP + 1, t=NT)
            T.gate_rows = cut(P, NT * 128).rearrange("p (t e) -> p t e", t=NT)

        router(Carve(r34[:, 0:NT * N]), E0)
        T.gates_t, T.b2_rows = affine[:E0, 0:N], affine[:E0, N:N + D]
        first_router(nc, T, S, A)

        cut = Carve(r34[:, 0:NT * N])
        T.ew1 = cut(128, 4 * KD * F0).rearrange("p (s k f) -> p s k f", s=4, k=KD)
        T.ew2 = cut(128, 4 * F0 // 128 * D).rearrange("p (s k n) -> p s k n", s=4, k=F0 // 128)
        T.ex = cut(128, 2 * D).rearrange("p (s d) -> p s d", s=2)
        T.ex_t = cut(128, 2 * KD * CAP).rearrange("p (s k c) -> p s k c", s=2, k=KD)
        T.eh = cut(128, 2 * F0 // 128 * CAP).rearrange("p (s f c) -> p s f c", s=2, f=F0 // 128)
        T.ey = cut(128, 2 * D).rearrange("p (s d) -> p s d", s=2)
        T.eb1_rows = cut(E0, F0)
        T.eb1 = cut(128, F0 // 128 * E0).rearrange("p (f e) -> p f e", f=F0 // 128)
        first_experts(nc, T, S, A)

        T.ct_f = r34[:P, 0:NT * N].rearrange("p (k n) -> p k n", k=NT)
        T.rdeg = r34[:, NT * N:NT * N + N]
        T.wl_t = r5[:, 0:2 * KD * D].rearrange("p (i k d) -> p i k d", i=2, k=KD)
        T.means, T.conv = feats_of(r6), feats_of(r1)
        second_convolution(nc, T, S, A)

        cut = Carve(r34)
        T.w1 = cut(128, E1 * KD * F1).rearrange("p (e k f) -> p e k f", e=E1, k=KD)
        T.w2 = cut(128, E1 * F1 // 128 * D).rearrange("p (e k n) -> p e k n", e=E1, k=F1 // 128)
        router(cut, E1)
        T.gates_t1, T.b2_rows1 = affine[:E1, 0:N], affine[:E1, N:N + D]
        T.b1 = r6[:, 0:E1 * F1]
        cut = Carve(r6, E1 * F1)
        T.below = cut(BR, E1 * BLOCKS).rearrange("p (e k) -> p e k", e=E1)
        T.ended = cut(BR, NB * E1).rearrange("p (b e) -> p b e", b=NB)
        T.past = cut(P, NT * TOP * (BLOCKS - 1)).rearrange("p (c k) -> p c k", c=NT * TOP)
        second_router(nc, T, S, A)

        T.b1_of = T.b1.rearrange("p (e f) -> p e f", e=E1)
        cut = Carve(r1)
        T.rx = cut(128, 2 * D).rearrange("p (s d) -> p s d", s=2)
        T.rx_t = cut(128, 2 * KD * BR).rearrange("p (s k c) -> p s k c", s=2, k=KD)
        T.rh_sum, T.rh = (cut(128, 2 * F1).rearrange("p (s f) -> p s f", s=2) for _ in range(2))
        T.rh_t = cut(128, 2 * F1).rearrange("p (s f c) -> p s f c", s=2, f=F1 // 128)
        T.ry = cut(128, 2 * D).rearrange("p (s d) -> p s d", s=2)
        second_experts(nc, T, S, A)
        finish(nc, T, S, A)



NAMES = ["x", "src", "dst", "edge_weight", "L0_gnn_W", "L0_ffn_ln1_g", "L0_ffn_ln1_b", "L0_ffn_wq", "L0_ffn_wk",
         "L0_ffn_wv", "L0_ffn_wo", "L0_ffn_ln2_g", "L0_ffn_ln2_b", "L0_ffn_wr", "L0_ffn_w1", "L0_ffn_b1", "L0_ffn_w2",
         "L0_ffn_b2", "L1_gnn_W_l", "L1_gnn_b_l", "L1_gnn_W_r", "L1_gnn_gamma", "L1_gnn_beta", "L1_ffn_Wr", "L1_ffn_W1",
         "L1_ffn_b1", "L1_ffn_W2", "L1_ffn_b2"]


def by_name(places, out):
    A = Named()
    (A.x, A.src, A.dst, A.edge_weight, A.L0_gnn_W, A.L0_ffn_ln1_g, A.L0_ffn_ln1_b, A.L0_ffn_wq, A.L0_ffn_wk,
     A.L0_ffn_wv, A.L0_ffn_wo, A.L0_ffn_ln2_g, A.L0_ffn_ln2_b, A.L0_ffn_wr, A.L0_ffn_w1, A.L0_ffn_b1, A.L0_ffn_w2,
     A.L0_ffn_b2, A.L1_gnn_W_l, A.L1_gnn_b_l, A.L1_gnn_W_r, A.L1_gnn_gamma, A.L1_gnn_beta, A.L1_ffn_Wr, A.L1_ffn_W1,
     A.L1_ffn_b1, A.L1_ffn_W2, A.L1_ffn_b2) = [places[name] for name in NAMES]
    A.out = out
    return A


def kernel(**inputs):
    import numpy as np
    import concourse.bacc as bacc
    from concourse.bass_utils import run_bass_kernel_spmd

    nc = bacc.Bacc("TRN2", target_bir_lowering=False, num_devices=1)
    arrays, places = {}, {}
    for name in NAMES:
        arrays[name] = np.ascontiguousarray(inputs[name])
        places[name] = nc.dram_tensor(name, arrays[name].shape, mybir.dt.from_np(arrays[name].dtype),
                                      kind="ExternalInput").ap()
    out = nc.dram_tensor("out", [N, D], F32, kind="ExternalOutput").ap()
    program(nc, by_name(places, out))
    return run_bass_kernel_spmd(nc, [arrays], core_ids=[0]).results[0]["out"]
```

```python
from contextlib import ExitStack

import concourse.bass as bass
from concourse import mybir

F32 = mybir.dt.float32
BF16 = mybir.dt.bfloat16
I16 = mybir.dt.int16
U16 = mybir.dt.uint16
I32 = mybir.dt.int32
U32 = mybir.dt.uint32
ALU = mybir.AluOpType
ACT = mybir.ActivationFunctionType
AX = mybir.AxisListType

N = 1250
D = 512
P = 125
NT = N // P
KD = D // 128
EPS = 1e-5
GROUPS = [(0, 4), (4, 4), (8, 2)]
CHUNKS = [(0, 417), (417, 417), (834, 416)]

EDGES = 41250
EC = 125
CJ = 3
NCH = EDGES // EC
NG = NCH // CJ
WD = 16
WINDOWS = -(-N // WD)
LAST_WINDOW = N - WD
WC = NT * WD
UNROLL = 10

NH = 8
DH = D // NH
SCALE = DH ** -0.5

TOP = 2
E0, F0 = 64, 256
WS = 8
EARLY = 5
CAP = 2 * (N * TOP // E0)
E1, F1 = 8, 256
BR = 128
NB = 4 * -(-((N * TOP + E1 * (BR - 1)) // BR) // 4)
FOURS = -(-N * TOP // (4 * BR))
BLOCKS = -(-N // BR)


class Named:
    pass


class Chain:

    def __init__(self, engine, semaphore, at):
        self.engine, self.semaphore, self.at = engine, semaphore, at

    def __call__(self, instruction):
        self.at[0] += 1
        instruction.then_inc(self.semaphore, 1)
        self.engine.wait_ge(self.semaphore, self.at[0])


class Carve:

    def __init__(self, region, start=0):
        self.region, self.at = region, start

    def __call__(self, parts, cols, dtype=F32):
        size = mybir.dt.size(dtype)
        words = -(-cols * size // 4)
        view = self.region[:, self.at:self.at + words]
        self.at += words
        assert self.at <= self.region.shape[1], (self.at, self.region.shape)
        if dtype != F32:
            view = view.bitcast(dtype)
        return view[:parts, :cols]



TURNS = len(GROUPS) * KD


def transpose_group(pe, T, rows, ready, S, use, g, first=0, banks=8):
    t0, n = GROUPS[g]
    if ready is not None:
        pe.wait_ge(ready, t0 + n)
    for k in range(KD):
        j = g * KD + k
        if j >= banks:
            pe.wait_ge(S.tiles_copied, use * TURNS + j - banks + 1)
        for t in range(t0, t0 + n):
            last = pe.transpose(T.ps[:, first + j % banks, (t - t0) * P:(t - t0 + 1) * P],
                                rows[:, t, k * 128:(k + 1) * 128], T.ident[:P, :P])
        last.then_inc(S.tiles_turned, 1)


def copy_group(act, T, out, S, use, g, first=0, banks=8):
    t0, n = GROUPS[g]
    for k in range(KD):
        j = g * KD + k
        act.wait_ge(S.tiles_turned, use * TURNS + j + 1)
        act.activation(out[:, k, t0 * P:(t0 + n) * P], T.ps[:, first + j % banks, 0:n * P], ACT.Copy)\
           .then_inc(S.tiles_copied, 1)


def groups_after(t):
    return [g for g, (t0, n) in enumerate(GROUPS) if t == min(t0 + n + 1, NT - 1)]


def tiles_of(g):
    t0, n = GROUPS[g]
    return range(t0, t0 + n)


def row_moments(dve, link, T, rows, t, var_ready):
    link(dve.bn_stats(T.stats[:], rows[:, t, :]))
    link(dve.bn_aggr(T.moments[:, t, :], T.stats[:]))
    dve.tensor_scalar(T.spread[:, t:t + 1], T.moments[:, t, 1:2], EPS, None, ALU.add).then_inc(var_ready, 1)


def row_roots(act, T, tiles, var_ready, std_ready):
    for t in tiles:
        act.wait_ge(var_ready, t + 1)
        act.activation(T.std[:, t:t + 1], T.spread[:, t:t + 1], ACT.Sqrt).then_inc(std_ready, 1)


def normalize(dve, link, T, out, rows, t, gain=None, shift=None):
    link(dve.reciprocal(T.rstd[:, t:t + 1], T.std[:, t:t + 1]))
    if gain is None:
        return dve.tensor_scalar(out[:, t, :], rows[:, t, :], T.moments[:, t, 0:1], T.rstd[:, t:t + 1],
                                 ALU.subtract, ALU.mult)
    link(dve.scalar_tensor_tensor(out=out[:, t, :], in0=rows[:, t, :], scalar=T.moments[:, t, 0:1], in1=gain,
                                  op0=ALU.subtract, op1=ALU.mult))
    return dve.scalar_tensor_tensor(out=out[:, t, :], in0=out[:, t, :], scalar=T.rstd[:, t:t + 1], in1=shift,
                                    op0=ALU.mult, op1=ALU.add)


def rows_of(region, width=D):
    return region[:P, 0:NT * width].rearrange("p (t d) -> p t d", t=NT)


def feats_of(region):
    return region[:, 0:KD * N].rearrange("p (k n) -> p k n", k=KD)



def constants(nc, T, S, A):
    with nc.Block() as block:

        @block.gpsimd
        def _(pool):
            pool.memset(T.ident[:], 0.0).then_inc(S.const_pool, 1)
            pool.memset(T.before[:], 1.0).then_inc(S.const_pool, 1)
            pool.wait_ge(S.const_pool, 2)
            pool.affine_select(out=T.ident[:], in_=T.ident[:], compare_op=ALU.not_equal, fill=1.0, base=0,
                               pattern=[[-1, 128]], channel_multiplier=1)
            pool.affine_select(out=T.before[:], in_=T.before[:], compare_op=ALU.is_gt, fill=0.0, base=0,
                               pattern=[[1, P]], channel_multiplier=-1)
            exact = dict(allow_small_or_imprecise_dtypes=True)
            pool.iota(T.row_iota[:], [[1, 128]], base=0, channel_multiplier=0, **exact)
            pool.iota(T.cell_iota[:], [[1, WC]], base=0, channel_multiplier=0, **exact)
            pool.iota(T.win_starts[:], [[WD, WINDOWS]], base=0, channel_multiplier=0, **exact)
            pool.iota(T.expert_iota[:], [[1, E0]], base=0, channel_multiplier=0, **exact)
            pool.iota(T.block_iota[:], [[1, NB]], base=0, channel_multiplier=0, **exact)
            pool.iota(T.row_starts[:], [[BR, BLOCKS]], base=0, channel_multiplier=0, **exact)
            pool.iota(T.token[:], [[P, NT]], base=0, channel_multiplier=1, **exact)

        @block.vector
        def _(dve):
            dve.memset(T.ones_bf[:], 1.0)
            dve.memset(T.ones[:], 1.0)

        @block.sync
        def _(sp):
            sp.dma_start(T.dst_i, A.dst.rearrange("(p j e) -> p j e", j=CJ, e=EC)).then_inc(S.edges_loaded, 16)
            sp.dma_start(T.src_i, A.src.rearrange("(p j e) -> p j e", j=CJ, e=EC)).then_inc(S.edges_loaded, 16)
            sp.dma_start(T.wgt, A.edge_weight.rearrange("(p j e) -> p j e", j=CJ, e=EC)).then_inc(S.edges_loaded, 16)
            sp.dma_start(T.x[0:120], A.x.rearrange("(t p) d -> p t d", t=NT)[0:120]).then_inc(S.x_loaded, 16)
            sp.dma_start(T.x[120:P], A.x.rearrange("(t p) d -> p t d", t=NT)[120:P]).then_inc(S.x_loaded, 16)
            sp.dma_start(T.w_a, A.L0_gnn_W.rearrange("(k p) n -> p k n", k=KD)).then_inc(S.w0_loaded, 16)
            sp.dma_start(T.w_b, A.L0_ffn_wq.rearrange("(k p) n -> p k n", k=KD)).then_inc(S.wq_loaded, 16)
            for i, v in enumerate((A.L0_ffn_ln1_g, A.L0_ffn_ln1_b, A.L0_ffn_ln2_g, A.L0_ffn_ln2_b)):
                sp.dma_start(T.affine[:, i, :], v.rearrange("(o d) -> o d", o=1).to_broadcast([P, D]))\
                  .then_inc(S.affine_loaded, 16)


def edges_to_columns(dve, link, T, S):
    dve.wait_ge(S.edges_loaded, 48)
    dve.tensor_copy(T.dst_f, T.dst_i)
    link(dve.tensor_copy(T.src_f, T.src_i))
    link(dve.tensor_scalar(T.hi_f, T.src_f, float(P), None, ALU.is_ge))
    for k in range(2, NT):
        link(dve.scalar_tensor_tensor(out=T.hi_f, in0=T.src_f, scalar=float(k * P), in1=T.hi_f,
                                      op0=ALU.is_ge, op1=ALU.add))
    dve.scalar_tensor_tensor(out=T.lo_row, in0=T.hi_f, scalar=-float(P), in1=T.src_f, op0=ALU.mult, op1=ALU.add)
    dve.tensor_reduce(T.group_min, T.dst_f, AX.XY, ALU.min)
    link(dve.tensor_reduce(T.group_max, T.dst_f, AX.XY, ALU.max))
    link(dve.tensor_scalar(T.group_min, T.group_min, float(LAST_WINDOW), None, ALU.min))
    dve.tensor_scalar(T.base_rows, T.ones[:NG, :], T.group_min, None, ALU.mult)
    link(dve.tensor_tensor(T.group_max, T.group_max, T.group_min, ALU.subtract))
    link(dve.tensor_scalar(T.further, T.win_starts[:], T.group_max, None, ALU.is_le))
    link(dve.tensor_reduce(T.group_max, T.further, AX.X, ALU.add))
    dve.sem_inc(S.prep_done, 1)
    dve.wait_ge(S.prep_transposed, 1)
    for a, columns in enumerate((T.lo_col, T.hi_col, T.dst_col, T.w_col)):
        dve.tensor_copy(columns, T.ps[:P, a, 0:NCH].rearrange("q (j p) -> q p j", p=NG))
    dve.tensor_copy(T.base_all, T.ps[:P, 4, 0:NG])
    link(dve.tensor_reduce(T.further[0:1, 0:1], T.ps[0:1, 5, 0:NG], AX.X, ALU.max))
    link(dve.tensor_copy(T.passes[:], T.further[0:1, 0:1]))
    link(dve.tensor_scalar(T.hi_col, T.hi_col, float(WD), 1.0, ALU.mult, ALU.add))
    dve.sem_inc(S.columns_ready, 1)


def turn_edges(pe, T, S):
    pe.wait_ge(S.prep_done, 1)
    for a, rows in enumerate((T.lo_row, T.hi_f, T.dst_f, T.wgt)):
        for j in range(CJ):
            pe.transpose(T.ps[:P, a, j * NG:(j + 1) * NG], rows[:, j, :], T.ident[:NG, :NG])
    pe.transpose(T.ps[:, 4, 0:NG], T.base_rows, T.ident[:NG, :NG])
    pe.transpose(T.ps[0:1, 5, 0:NG], T.group_max, T.ident[:NG, :NG]).then_inc(S.prep_transposed, 1)


def first_projection(nc, T, S, A):
    with nc.Block() as block:

        @block.gpsimd
        def _(pool):
            pool.memset(T.at, 0.0)
            pool.memset(T.ct, 0.0)

        @block.vector
        def _(dve):
            link = Chain(dve, S.dve_chain, T.dve_at)
            edges_to_columns(dve, link, T, S)
            dve.wait_ge(S.x_loaded, 32)
            for t in range(NT + 1):
                if t < NT:
                    row_moments(dve, link, T, T.x, t, S.z_var)
                if t > 0:
                    dve.wait_ge(S.z_std, t)
                    normalize(dve, link, T, T.rows_a, T.x, t - 1).then_inc(S.z_rows, 1)

        @block.scalar
        def _(act):
            row_roots(act, T, range(0, 6), S.z_var, S.z_std)
            for g in range(len(GROUPS)):
                copy_group(act, T, T.feats, S, 0, g, 2, 4)
                if g == 0:
                    row_roots(act, T, range(6, NT), S.z_var, S.z_std)
                for t in tiles_of(g):
                    act.wait_ge(S.z_done, t + 1)
                    act.activation(T.rows_a[:, t, :], T.ps[:P, t % 2, :], ACT.Copy).then_inc(S.z_copied, 1)

        @block.tensor
        def _(pe):
            turn_edges(pe, T, S)
            pe.wait_ge(S.columns_ready, 1)
            pe.wait_ge(S.w0_loaded, 16)
            for g in range(len(GROUPS)):
                transpose_group(pe, T, T.rows_a, S.z_rows, S, 0, g, 2, 4)
                pe.wait_ge(S.tiles_copied, (g + 1) * KD)
                for t in tiles_of(g):
                    if t >= 2:
                        pe.wait_ge(S.z_copied, t - 1)
                    for k in range(KD):
                        last = pe.matmul(T.ps[:P, t % 2, :], T.feats[:, k, t * P:(t + 1) * P], T.w_a[:, k, :],
                                         start=(k == 0), stop=(k == KD - 1))
                    last.then_inc(S.z_done, 1)


def adjacency(nc, T, S, A):
    def visits(engine, name, body, before=None, after=None):
        count = engine.alloc_register(name + "_passes")
        seen = engine.alloc_register(name + "_visits")
        engine.reg_load(count, T.passes[0:1, 0:1])
        engine.reg_mov(seen, 0)
        with engine.Fori(0, engine.snap(count, min_val=1, max_val=WINDOWS)) as r:
            if before:
                before(r)
            peeled = 0
            if after:
                body(0, engine.snap(seen, min_val=0, max_val=NG * WINDOWS), True)
                engine.reg_add(seen, seen, UNROLL)
                peeled = 1
            with engine.Fori(0, NG // UNROLL - peeled) as q:
                body(q * UNROLL + peeled * UNROLL, engine.snap(seen, min_val=peeled * UNROLL, max_val=NG * WINDOWS), False)
                engine.reg_add(seen, seen, UNROLL)
            if after:
                after(engine.snap(seen, min_val=NG, max_val=NG * WINDOWS))

    def column(columns, g, width):
        return columns[:, bass.ds(g, 1), :].rearrange("e o j -> e (o j)").unsqueeze(2).to_broadcast([EC, CJ, width])

    def load_start(engine, start, g):
        engine.reg_load(start, T.base_row[0:1, bass.ds(g, 1)])

    def window(engine, sums, start):
        return sums[:, :, bass.ds(engine.snap(start, min_val=0, max_val=LAST_WINDOW), WD)]

    def products(bank):
        return T.ps[:P, bank, 0:WC].rearrange("p (k d) -> p k d", k=NT)

    with nc.Block() as block:

        @block.vector
        def _(dve):
            def next_pass(r):
                every = T.base_all.unsqueeze(2).to_broadcast([EC, NG, CJ])
                dve.wait_ge(S.at_added, r * NG + 2)
                dve.wait_ge(S.ct_added, r * NG + 2)
                steps = [
                    lambda: dve.tensor_tensor(T.rel_col, T.dst_col, every, ALU.subtract),
                    lambda: dve.tensor_scalar(T.base_now, T.base_all, float(LAST_WINDOW), None, ALU.min),
                    lambda: dve.tensor_copy(T.base_row[:], T.base_now[0:1, :]),
                    lambda: dve.tensor_scalar(T.valid_col, T.rel_col, 0.0, None, ALU.is_ge),
                    lambda: dve.scalar_tensor_tensor(out=T.valid_col, in0=T.rel_col, scalar=float(WD), in1=T.valid_col,
                                                     op0=ALU.is_lt, op1=ALU.mult),
                    lambda: dve.tensor_tensor(T.cell_col, T.dst_col, T.base_now.unsqueeze(2).to_broadcast([EC, NG, CJ]),
                                              ALU.subtract),
                    lambda: dve.tensor_tensor(T.cell_col, T.cell_col, T.hi_col, ALU.add),
                    lambda: dve.tensor_tensor(T.cell_col, T.cell_col, T.valid_col, ALU.mult),
                    lambda: dve.tensor_scalar(T.cell_col, T.cell_col, 1.0, None, ALU.subtract),
                    lambda: dve.tensor_scalar(T.base_all, T.base_all, float(WD), None, ALU.add),
                ]
                for i, step in enumerate(steps):
                    if i > 0:
                        dve.wait_ge(S.pass_step, r * len(steps) + i)
                    step().then_inc(S.pass_step, 1)
    
            starts = [dve.alloc_register(f"counts_start{b}") for b in range(2)]

            def add_counts(sums, seen, i):
                dve.wait_ge(S.ct_added, seen + (i + 2))
                dve.tensor_tensor(sums, sums, products(i % 2), ALU.add).then_inc(S.ct_added, 1)

            def body(g0, seen, first):
                for i in range(UNROLL):
                    g, b = g0 + i, i % 2
                    takes_over = i >= 2 or not first
                    if takes_over:
                        load_start(dve, starts[b], g0 + (i - 2))
                    dve.wait_ge(S.counts_done, seen + (i + 1))
                    dve.wait_ge(S.weighted_ready, seen + (i + 1))
                    dve.tensor_tensor(T.sources[:, b], T.lo_iota[:].unsqueeze(1).to_broadcast([EC, CJ, P]),
                                      column(T.lo_col, g, P), ALU.is_equal).then_inc(S.sources_ready, 1)
                    if takes_over:
                        add_counts(window(dve, T.ct, starts[b]), seen, i - 2)
                    dve.wait_ge(S.products_done, seen + (i + 1))
                    dve.tensor_tensor(T.cells[:, b], T.cell_iota[:].unsqueeze(1).to_broadcast([EC, CJ, WC]),
                                      column(T.cell_col, g, WC), ALU.is_equal).then_inc(S.cells_ready, 1)

            def last_counts(seen):
                for i in range(2):
                    load_start(dve, starts[i], NG - 2 + i)
                    sums = window(dve, T.ct, starts[i])
                    dve.wait_ge(S.counts_done, seen + (i + 1))
                    add_counts(sums, seen, i - 2)

            dve.sem_inc(S.ct_added, 2)
            visits(dve, "dve", body, next_pass, last_counts)

        @block.gpsimd
        def _(pool):
            start = pool.alloc_register("sums_start")

            def body(g0, seen, first):
                for i in range(UNROLL):
                    pool.wait_ge(S.weights_copied, seen + (i + 3))
                    load_start(pool, start, g0 + i)
                    sums = window(pool, T.at, start)
                    pool.wait_ge(S.at_added, seen + (i + 2))
                    pool.tensor_tensor(sums, sums, T.copied[:, i % 2, :].rearrange("p (k d) -> p k d", k=NT), ALU.add)\
                        .then_inc(S.at_added, 1)

            pool.sem_inc(S.at_added, 2)
            visits(pool, "pool", body)

        @block.scalar
        def _(act):
            def copy_weights(i, seen):
                act.wait_ge(S.products_done, seen + (i + 3))
                act.wait_ge(S.at_added, seen + (i + 1))
                act.activation(T.copied[:, i % 2, :], T.ps[:P, 2 + i % 2, 0:WC], ACT.Copy).then_inc(S.weights_copied, 1)

            def body(g0, seen, first):
                for i in range(UNROLL):
                    act.wait_ge(S.sources_ready, seen + (i + 1))
                    for j in range(CJ):
                        last = act.activation(T.weighted[:, i % 2, j, :], T.sources[:, i % 2, j, :], ACT.Copy,
                                              scale=T.w_col[:, bass.ds(g0 + i, 1), j])
                    last.then_inc(S.weighted_ready, 1)
                    if i > 0 or not first:
                        copy_weights(i - 1, seen)

            def last_weights(seen):
                copy_weights(-1, seen)

            act.sem_inc(S.weighted_ready, 2)
            act.sem_inc(S.weights_copied, 2)
            act.preload_act_table(ACT.Copy)
            visits(act, "act", body, None, last_weights)

        @block.tensor
        def _(pe):
            def body(g0, seen, first):
                for i in range(UNROLL):
                    b = i % 2
                    pe.wait_ge(S.ct_added, seen + (i + 1))
                    pe.wait_ge(S.cells_ready, seen + (i + 1))
                    for j in range(CJ):
                        last = pe.matmul(T.ps[:P, b, 0:WC], T.sources_bf[:, b, j, :, 1], T.cells_bf[:, b, j, :, 1],
                                         start=(j == 0), stop=(j == CJ - 1))
                    last.then_inc(S.counts_done, 1)
                    pe.wait_ge(S.weights_copied, seen + (i + 1))
                    pe.wait_ge(S.weighted_ready, seen + (i + 3))
                    for j in range(CJ):
                        last = pe.matmul(T.ps[:P, 2 + b, 0:WC], T.weighted[:, b, j, :], T.cells[:, b, j, :],
                                         start=(j == 0), stop=(j == CJ - 1))
                    last.then_inc(S.products_done, 1)

            pe.sem_inc(S.counts_done, 2)
            pe.sem_inc(S.products_done, 2)
            visits(pe, "pe", body)



def choose(dve, link, T, experts, chosen, gap_ready):
    for t in range(NT):
        last = dve.max(T.top[:, t, :], T.logits[:, t, 0:experts])
    link(last)
    dve.tensor_tensor(T.gap[:], T.top[:, :, 1], T.top[:, :, 0], ALU.subtract).then_inc(gap_ready, 1)
    for t in range(NT):
        last = dve.max_index(T.top_i[:, t, :], T.top[:, t, :], T.logits[:, t, 0:experts])
    link(last)
    link(dve.tensor_copy(T.expert[:], T.top_i[:, :, 0:TOP]))
    which = T.expert_iota[:, 0:experts].unsqueeze(1).to_broadcast([P, NT, experts])
    for j in range(TOP):
        last = dve.tensor_tensor(T.onehot[:, j, :, 0:experts], which,
                                 T.expert[:, :, j].unsqueeze(2).to_broadcast([P, NT, experts]), ALU.is_equal)
    link(last)
    dve.tensor_tensor(T.onehot[:, TOP, :, 0:experts], T.onehot[:, 0, :, 0:experts], T.onehot[:, 1, :, 0:experts],
                      ALU.add).then_inc(chosen, 1)


def gates(dve, link, T):
    link(dve.tensor_scalar(T.gate[:, :, 0], T.gap[:], 1.0, None, ALU.add))
    link(dve.reciprocal(T.gate[:, :, 0], T.gate[:, :, 0]))
    link(dve.tensor_tensor(T.gate[:, :, 1], T.gate[:, :, 0], T.gap[:], ALU.mult))


def count_before(pe, T, experts):
    for b in range(2):
        t0, t1 = 5 * b, 5 * b + 5
        pe.matmul(T.ps[:P, 2 + b, 0:5 * experts].rearrange("p (t e) -> p t e", t=5), T.before[:],
                  T.onehot[:, TOP, t0:t1, 0:experts], start=True, stop=False)
        for u in range(t1 - 1):
            after = max(u + 1, t0)
            last = pe.matmul(T.ps[:P, 2 + b, (after - t0) * experts:5 * experts].rearrange("p (t e) -> p t e", e=experts),
                             T.ones_bf[:, 0:P], T.onehot[:, TOP, u, 0:experts].unsqueeze(1).to_broadcast([P, t1 - after, experts]),
                             start=False, stop=(u == t1 - 2))
    return last


def positions(dve, link, T, experts):
    for j in range(TOP):
        for b in range(2):
            last = dve.tensor_tensor(T.picked[:, 5 * b:5 * b + 5, 0:experts], T.onehot[:, j, 5 * b:5 * b + 5, 0:experts],
                                     T.ps[:P, 2 + b, 0:5 * experts].rearrange("p (t e) -> p t e", t=5), ALU.mult)
        link(last)
        link(dve.tensor_reduce(T.position[:, :, j], T.picked[:, :, 0:experts], AX.X, ALU.add))


def gate_rows(dve, link, T, experts, ready):
    dve.tensor_tensor(T.picked[:, :, 0:experts], T.onehot[:, 0, :, 0:experts],
                      T.gate[:, :, 0].unsqueeze(2).to_broadcast([P, NT, experts]), ALU.mult)
    link(dve.tensor_tensor(T.gate_rows[:, :, 0:experts], T.onehot[:, 1, :, 0:experts],
                           T.gate[:, :, 1].unsqueeze(2).to_broadcast([P, NT, experts]), ALU.mult))
    dve.tensor_tensor(T.gate_rows[:, :, 0:experts], T.gate_rows[:, :, 0:experts], T.picked[:, :, 0:experts], ALU.add)\
       .then_inc(ready, 1)


def place(dve, link, T, rows, row, columns, ready):
    link(dve.tensor_tensor(T.place_rows[:], T.row_iota[:, 0:rows].unsqueeze(1).to_broadcast([P, NT * TOP, rows]),
                           row[:].rearrange("p t j -> p (t j)").unsqueeze(2).to_broadcast([P, NT * TOP, rows]),
                           ALU.is_equal))
    for j in range(TOP):
        last = dve.tensor_tensor(T.place_columns[:, j], T.place[:, j],
                                 T.token[:].unsqueeze(2).to_broadcast([P, NT, columns]), ALU.mult)
    last.then_inc(ready, 1)


def make_table(pe, T, bank, rows, columns):
    for t in range(NT):
        for j in range(TOP):
            last = pe.matmul(T.ps[:rows, bank, 0:columns], T.place_rows[:, t * TOP + j, :], T.place_columns[:, j, t, :],
                             start=(t + j == 0), stop=(t == NT - 1 and j == TOP - 1))
    return last


def load_expert(sp, T, S, A, e, slot):
    sp.dma_start(T.ew1[slot], A.L0_ffn_w1[bass.ds(e, 1)].rearrange("o (k p) f -> p (o k) f", k=KD))\
      .then_inc(S.ew_loaded[slot], 16)
    sp.dma_start(T.ew2[slot], A.L0_ffn_w2[bass.ds(e, 1)].rearrange("o (k p) n -> p (o k) n", k=F0 // 128))\
      .then_inc(S.ew_loaded[slot], 16)


def gate_matrices(act, T, t, before, ready):
    if t >= 2:
        act.wait_ge(before, t - 1)
    for j in range(TOP):
        last = act.activation(T.diagonal[:, t % 2, j, :], T.ident[:P, :P], ACT.Copy, scale=T.gate[:, t, j:j + 1])
    last.then_inc(ready, 1)


def gated_sum(pe, T, t, bank, gates_t, biases, rows):
    pe.matmul(T.ps[:P, bank, :], gates_t[:, t * P:(t + 1) * P], biases, start=True, stop=False)
    for j in range(TOP):
        last = pe.matmul(T.ps[:P, bank, :], T.diagonal[:, t % 2, j, :], rows[j][:, t, :], start=False, stop=(j == TOP - 1))
    return last




def first_convolution(nc, T, S, A):
    with nc.Block() as block:

        @block.sync
        def _(sp):
            sp.dma_start(T.w_a, A.L0_ffn_wk.rearrange("(k p) n -> p k n", k=KD)).then_inc(S.wk_loaded, 16)

        @block.tensor
        def _(pe):
            for t in range(NT):
                if t >= 2:
                    pe.wait_ge(S.agg_used, t - 1)
                for k in range(NT):
                    last = pe.matmul(T.ps[:P, t % 2, :], T.at[:, k, t * P:(t + 1) * P], T.rows_a[:, k, :],
                                     start=(k == 0), stop=(k == NT - 1))
                last.then_inc(S.agg_done, 1)
                for g in groups_after(t):
                    transpose_group(pe, T, T.rows_c, S.attn_rows, S, 1, g, 2, 6)

        @block.vector
        def _(dve):
            link = Chain(dve, S.dve_chain, T.dve_at)

            def residual(t):
                dve.wait_ge(S.agg_done, t + 1)
                dve.scalar_tensor_tensor(out=T.x[:, t, :], in0=T.ps[:P, t % 2, :], scalar=0.0, in1=T.x[:, t, :],
                                         op0=ALU.max, op1=ALU.add).then_inc(S.agg_used, 1)
                dve.wait_ge(S.agg_used, t + 1)
                row_moments(dve, link, T, T.x, t, S.xf_var)

            def ffn_input(t):
                dve.wait_ge(S.xf_std, 2 * t + 1)
                link(normalize(dve, link, T, T.rows_b, T.x, t))
                row_moments(dve, link, T, T.rows_b, t, S.xf_var)
                dve.wait_ge(S.xf_std, 2 * t + 2)
                normalize(dve, link, T, T.rows_c, T.rows_b, t, T.affine[:, 0, :], T.affine[:, 1, :])\
                    .then_inc(S.attn_rows, 1)

            dve.wait_ge(S.affine_loaded, 64)
            for t in range(NT):
                residual(t)
                ffn_input(t)

        @block.scalar
        def _(act):
            for t in range(NT):
                for half in range(2):
                    act.wait_ge(S.xf_var, 2 * t + half + 1)
                    act.activation(T.std[:, t:t + 1], T.spread[:, t:t + 1], ACT.Sqrt).then_inc(S.xf_std, 1)
                for g in groups_after(t):
                    copy_group(act, T, T.feats, S, 1, g, 2, 6)


def projections(nc, T, S, A):
    with nc.Block() as block:

        @block.sync
        def _(sp):
            sp.dma_start(T.w_v, A.L0_ffn_wv.rearrange("(k p) n -> p k n", k=KD)).then_inc(S.wv_loaded, 16)
            spare = NB - 4 * FOURS
            sp.dma_start(A.y1[4 * FOURS:NB].rearrange("b r d -> r b d"),
                         T.feats.rearrange("p k n -> p (k n)")[:, 0:spare * D].rearrange("p (b d) -> p b d", b=spare))\
              .then_inc(S.spare_filled, 16)
            sp.wait_ge(S.spare_filled, 16)

        @block.tensor
        def _(pe):
            j = 0
            for weights, loaded in ((T.w_b, S.wq_loaded), (T.w_a, S.wk_loaded)):
                if j > 0:
                    pe.wait_ge(S.partial_degrees, 1)
                    for c, (c0, n) in enumerate(CHUNKS):
                        last = pe.matmul(T.ps[:, 5 + c, 0:n], T.ones[:P, :], T.rdeg[:P, c0:c0 + n], start=True, stop=True)
                    last.then_inc(S.degrees_done, 1)
                pe.wait_ge(loaded, 16)
                for m in range(KD):
                    for c0, n in CHUNKS:
                        if j >= 5:
                            pe.wait_ge(S.proj_copied, j - 4)
                        for k in range(KD):
                            last = pe.matmul(T.ps[:, j % 5, 0:n], weights[:, k, m * 128:(m + 1) * 128],
                                             T.feats[:, k, c0:c0 + n], start=(k == 0), stop=(k == KD - 1))
                        last.then_inc(S.proj_done, 1)
                        j += 1

        @block.vector
        def _(dve):
            link = Chain(dve, S.dve_chain, T.dve_at)
            dve.tensor_reduce(T.rdeg[:P, :], T.ct.rearrange("p k n -> p n k"), AX.X, ALU.add).then_inc(S.partial_degrees, 1)
            dve.wait_ge(S.degrees_done, 1)
            for c, (c0, n) in enumerate(CHUNKS):
                last = dve.tensor_scalar(T.rdeg[:, c0:c0 + n], T.ps[:, 5 + c, 0:n], 1.0, None, ALU.max)
            link(last)
            dve.reciprocal(T.rdeg[:], T.rdeg[:])

        @block.scalar
        def _(act):
            j = 0
            for out in (T.qt, T.kt):
                for m in range(KD):
                    for c0, n in CHUNKS:
                        act.wait_ge(S.proj_done, j + 1)
                        act.activation(out[:, m, c0:c0 + n], T.ps[:, j % 5, 0:n], ACT.Copy).then_inc(S.proj_copied, 1)
                        j += 1


def attention(nc, T, S, A):
    steps = [(m, t, half) for m in range(KD) for t in range(NT) for half in range(2)]
    LAST = N - CHUNKS[0][1]
    starts = [0, CHUNKS[0][1], LAST]
    CW = CHUNKS[0][1]
    twice = 2 * CW - LAST
    TURNED = (7, 6, 7)
    LATER = 3

    def pair_after(n):
        p, rest = divmod(n - LATER - 2, 2)
        return p if rest == 0 and p >= 0 else None

    with nc.Block() as block:

        @block.sync
        def _(sp):
            sp.dma_start(T.w_b, A.L0_ffn_wo.rearrange("(k p) n -> p k n", k=KD)).then_inc(S.wo_loaded, 16)

        @block.tensor
        def _(pe):
            def scores(n, c):
                m, t, half = steps[n]
                b = DH * half
                if c == 0 and n >= 2:
                    pe.wait_ge(S.exp_done, n - 1)
                last = pe.matmul(T.ps[:P, 3 * (n % 2) + c, 0:CW], T.qt[b:b + DH, m, t * P:(t + 1) * P],
                                 T.kt[b:b + DH, m, starts[c]:starts[c] + CW], start=True, stop=True)
                if c == 2:
                    last.then_inc(S.scores_done, 1)

            def turn(n, g):
                t0, k = GROUPS[g]
                if g == 0:
                    pe.wait_ge(S.probs_ready, n + 1)
                    if n >= 1:
                        pe.wait_ge(S.probs_copied, 3 * n)
                elif g == 1 and n >= 3 and n % 2 == 1:
                    pe.wait_ge(S.out_copied, (n - 1) // 2)
                elif g == 2:
                    pe.wait_ge(S.probs_copied, 3 * n + 1)
                for t in range(t0, t0 + k):
                    last = pe.transpose(T.ps[:P, TURNED[g], (t - t0) * P:(t - t0 + 1) * P],
                                        T.probs[n % LATER][:, t * P:(t + 1) * P], T.ident[:P, :P])
                last.then_inc(S.probs_turned, 1)

            def values(p):
                m, _, _ = steps[2 * p]
                pe.wait_ge(S.probs_copied, 6 * p + (8 if 2 * p + 2 < len(steps) else 6))
                for k in range(NT):
                    for half in range(2):
                        b = DH * half
                        last = pe.matmul(T.ps[b:b + DH, 6, 0:P], T.v[:, k, m * 128 + b:m * 128 + b + DH],
                                         T.probs_t[:, (2 * p + half) % 4, k * P:(k + 1) * P],
                                         start=(k == 0), stop=(k == NT - 1))
                last.then_inc(S.values_done, 1)

            def value_rows():
                pe.wait_ge(S.wv_loaded, 16)
                for t in range(NT):
                    if t >= 2:
                        pe.wait_ge(S.v_copied, t - 1)
                    for k in range(KD):
                        last = pe.matmul(T.ps[:P, 6 + t % 2, :], T.feats[:, k, t * P:(t + 1) * P], T.w_v[:, k, :],
                                         start=(k == 0), stop=(k == KD - 1))
                    last.then_inc(S.v_done, 1)
                pe.wait_ge(S.v_copied, NT)

            for n in range(len(steps) + LATER + 1):
                turns = LATER <= n < len(steps) + LATER
                if n == 2:
                    value_rows()
                for part in range(3):
                    if turns:
                        turn(n - LATER, part)
                    if n < len(steps):
                        scores(n, part)
                if pair_after(n) is not None:
                    values(pair_after(n))

        @block.scalar
        def _(act):
            for n in range(len(steps)):
                act.wait_ge(S.max_ready, n + 1)
                if n >= LATER:
                    act.wait_ge(S.probs_turned, 3 * (n - LATER + 1))
                s, probs = 3 * (n % 2), T.probs[n % LATER]
                act.activation(probs[:, 0:2 * CW].rearrange("q (c k) -> q c k", c=2), T.ps[:P, s:s + 2, 0:CW],
                               ACT.Exp, bias=T.neg_max[:, n % 4:n % 4 + 1], scale=SCALE,
                               accum_out=T.sums[:, n % 4, 0:1])
                act.activation(probs[:, 2 * CW:N], T.ps[:P, s + 2, twice:CW],
                               ACT.Exp, bias=T.neg_max[:, n % 4:n % 4 + 1], scale=SCALE,
                               accum_out=T.sums[:, n % 4, 1:2]).then_inc(S.exp_done, 1)
                act.wait_ge(S.inverse_ready, n + 1)
                act.activation(probs, probs, ACT.Copy, scale=T.total[:, n % 2:n % 2 + 1]).then_inc(S.probs_ready, 1)

        @block.vector
        def _(dve):
            link = Chain(dve, S.dve_chain, T.dve_at)

            def maxima(n):
                s = 3 * (n % 2)
                dve.wait_ge(S.scores_done, n + 1)
                link(dve.tensor_reduce(T.row_max[:, n % 4:n % 4 + 1], T.ps[:P, s:s + 3, 0:CW], AX.XY, ALU.max))
                dve.tensor_scalar(T.neg_max[:, n % 4:n % 4 + 1], T.row_max[:, n % 4:n % 4 + 1], -SCALE, None, ALU.mult)\
                   .then_inc(S.max_ready, 1)

            def inverse(n):
                total = T.total[:, n % 2:n % 2 + 1]
                dve.wait_ge(S.exp_done, n + 1)
                if n >= 2:
                    dve.wait_ge(S.probs_ready, n - 1)
                link(dve.tensor_tensor(total, T.sums[:, n % 4, 0:1], T.sums[:, n % 4, 1:2], ALU.add))
                dve.reciprocal(total, total).then_inc(S.inverse_ready, 1)

            def output(p):
                m, t, _ = steps[2 * p]
                dve.wait_ge(S.values_done, p + 1)
                dve.tensor_copy(T.ot[:, m, t * P:(t + 1) * P], T.ps[:, 6, 0:P]).then_inc(S.out_copied, 1)

            def turned(n):
                for g, (t0, k) in enumerate(GROUPS):
                    dve.wait_ge(S.probs_turned, 3 * n + g + 1)
                    dve.tensor_copy(T.probs_t[:, n % 4, t0 * P:(t0 + k) * P], T.ps[:P, TURNED[g], 0:k * P])\
                       .then_inc(S.probs_copied, 1)

            for n in range(len(steps) + LATER + 1):
                if n == 2:
                    for t in range(NT):
                        dve.wait_ge(S.v_done, t + 1)
                        dve.tensor_copy(T.v[:, t, :], T.ps[:P, 6 + t % 2, :]).then_inc(S.v_copied, 1)
                if LATER <= n < len(steps) + LATER:
                    turned(n - LATER)
                if 1 <= n <= len(steps):
                    inverse(n - 1)
                if n < len(steps):
                    maxima(n)
                if pair_after(n) is not None:
                    output(pair_after(n))


def first_router(nc, T, S, A):
    with nc.Block() as block:

        @block.tensor
        def _(pe):
            def logits(g):
                pe.wait_ge(S.tiles_copied, 2 * TURNS + (g + 1) * KD)
                for t in tiles_of(g):
                    for k in range(KD):
                        last = pe.matmul(T.ps[:P, 6 + t // 5, t % 5 * E0:(t % 5 + 1) * E0],
                                         T.feats[:, k, t * P:(t + 1) * P], T.w_r[:, k, :], start=(k == 0), stop=(k == KD - 1))
                return last

            pe.wait_ge(S.wo_loaded, 16)
            pe.wait_ge(S.wr_loaded, 16)
            for t in range(NT):
                if t >= 2:
                    pe.wait_ge(S.wo_used, t - 1)
                for k in range(KD):
                    last = pe.matmul(T.ps[:P, t % 2, :], T.ot[:, k, t * P:(t + 1) * P], T.w_b[:, k, :],
                                     start=(k == 0), stop=(k == KD - 1))
                last.then_inc(S.wo_done, 1)
                for g in groups_after(t - 1):
                    logits(g)
                for g in groups_after(t):
                    transpose_group(pe, T, T.rows_a, S.x2_rows, S, 2, g, 2, 4)
            for g in groups_after(NT - 1):
                last = logits(g)
            last.then_inc(S.logits_done, 1)
            pe.wait_ge(S.chosen, 1)
            count_before(pe, T, E0).then_inc(S.counted, 1)
            pe.wait_ge(S.placed, 1)
            make_table(pe, T, 7, CAP, E0).then_inc(S.table_made, 1)
            pe.wait_ge(S.gates_ready, 1)
            for t in range(NT):
                last = pe.transpose(T.ps[:E0, 4 + t // 4, t % 4 * P:(t % 4 + 1) * P], T.gate_rows[:, t, 0:E0], T.ident[:P, :P])
            last.then_inc(S.gates_turned, 1)

        @block.scalar
        def _(act):
            for t in range(NT):
                row_roots(act, T, [t], S.x2_var, S.x2_std)
                for g in groups_after(t):
                    copy_group(act, T, T.feats, S, 2, g, 2, 4)
            act.wait_ge(S.logits_done, 1)
            for b in range(2):
                act.activation(T.logits[:, 5 * b:5 * b + 5, 0:E0],
                               T.ps[:P, 6 + b, 0:5 * E0].rearrange("p (t e) -> p t e", t=5), ACT.Copy).then_inc(S.logits_ready, 1)
            act.wait_ge(S.gap_ready, 1)
            act.activation(T.gap[:], T.gap[:], ACT.Exp).then_inc(S.gap_exp, 1)
            act.wait_ge(S.gates_turned, 1)
            for b in range(3):
                n = min(4, NT - 4 * b)
                act.activation(T.gates_t[:, 4 * b * P:(4 * b + n) * P], T.ps[:E0, 4 + b, 0:n * P], ACT.Copy)\
                   .then_inc(S.gates_t_ready, 1)

        @block.vector
        def _(dve):
            link = Chain(dve, S.dve_chain, T.dve_at)
            def added(t):
                dve.wait_ge(S.wo_done, t + 1)
                dve.tensor_tensor(T.rows_b[:, t, :], T.ps[:P, t % 2, :], T.rows_b[:, t, :], ALU.add).then_inc(S.wo_used, 1)
                dve.wait_ge(S.wo_used, t + 1)
                row_moments(dve, link, T, T.rows_b, t, S.x2_var)

            def normalized(t):
                dve.wait_ge(S.x2_std, t + 1)
                normalize(dve, link, T, T.rows_a, T.rows_b, t, T.affine[:, 2, :], T.affine[:, 3, :])\
                    .then_inc(S.x2_rows, 1)

            for t in range(NT):
                added(t)
                if t > 0:
                    normalized(t - 1)
            normalized(NT - 1)
            dve.wait_ge(S.logits_ready, 2)
            choose(dve, link, T, E0, S.chosen, S.gap_ready)
            dve.wait_ge(S.gap_exp, 1)
            gates(dve, link, T)
            dve.wait_ge(S.counted, 1)
            positions(dve, link, T, E0)
            place(dve, link, T, CAP, T.position, E0, S.placed)
            keep, row = T.keep, T.scratch
            link(dve.tensor_scalar(keep[:], T.position[:], float(CAP), None, ALU.is_lt))
            link(dve.tensor_tensor(T.gate[:], T.gate[:], keep[:], ALU.mult))
            link(dve.tensor_scalar(row[:], T.position[:], float(CAP - 1), None, ALU.min))
            link(dve.scalar_tensor_tensor(out=row[:], in0=T.expert[:], scalar=float(CAP), in1=row[:],
                                          op0=ALU.mult, op1=ALU.add))
            dve.tensor_copy(T.row_i[:], row[:])
            gate_rows(dve, link, T, E0, S.gates_ready)
            dve.wait_ge(S.table_made, 1)
            dve.tensor_copy(T.ids[:CAP, 0:E0], T.ps[:CAP, 7, 0:E0])

        @block.sync
        def _(sp):
            sp.dma_start(T.w_r, A.L0_ffn_wr.rearrange("(k p) e -> p k e", k=KD)).then_inc(S.wr_loaded, 16)
            for slot in range(EARLY):
                load_expert(sp, T, S, A, slot, slot)
            sp.wait_ge(S.x2_rows, NT)
            for p0, p1 in ((0, 120), (120, P)):
                sp.dma_start(A.rows0.rearrange("(t p) d -> p t d", t=NT)[p0:p1], T.rows_a[p0:p1]).then_inc(S.rows0_stored, 16)
            sp.wait_ge(S.rows0_stored, 32)

        @block.gpsimd
        def _(pool):
            for t in range(NT):
                pool.wait_ge(S.wo_used, t + 1)
                pool.tensor_tensor(T.x[:, t, :], T.x[:, t, :], T.rows_b[:, t, :], ALU.add)


def wait_count(engine, semaphore, q, per, n):
    if not isinstance(q, int) or per * q + n > 0:
        engine.wait_ge(semaphore, q * per + n)


def gather_rows(pool, T, rows, slots, parts, loops, ids_ready, turned, loaded):
    def column(q, r):
        pool.tensor_copy(T.ex_ids[:parts, r % 4:r % 4 + 1], T.ids[:parts, bass.ds(q * 4 + r, 1)]).then_inc(ids_ready, 1)

    def gather(q, r, last=False):
        wait_count(pool, turned, q, 4, r - 1)
        pool.wait_ge(ids_ready, q * 4 + (r + 1))
        if not last:
            column(q, r + 1)
        pool.indirect_dma_start(slots[:parts, r % 2, :], None, rows,
                                bass.IndirectOffsetOnAxis(ap=T.ex_ids[:parts, r % 4:r % 4 + 1], axis=0))\
            .then_inc(loaded[r % 2], 16)

    column(0, 0)
    for r in range(4):
        gather(0, r)
    with pool.Fori(0, loops) as q:
        for r in range(4, 8):
            gather(q, r)
    for r in range(4, 8):
        gather(loops, r, isinstance(loops, int) and r == 7)


def first_experts(nc, T, S, A):
    FK = F0 // 128
    LOOPS = (E0 - 2) // WS

    def experts(engine, step):
        for r in range(2):
            step(0, r)
        with engine.Fori(0, LOOPS) as q:
            for r in range(2, 2 + WS):
                step(q, r)
        for r in range(2, 2 + (E0 - 2) % WS):
            step(LOOPS, r)

    def is_last(q, r):
        return isinstance(q, int) and WS * q + r == E0 - 1

    with nc.Block() as block:

        @block.sync
        def _(sp):
            sp.dma_start(T.eb1_rows, A.L0_ffn_b1).then_inc(S.columns_loaded, 16)
            for i, v in enumerate((A.L1_gnn_b_l, A.L1_gnn_gamma, A.L1_gnn_beta)):
                sp.dma_start(T.feature_rows[i * KD:(i + 1) * KD], v.rearrange("(m p) -> m p", m=KD)).then_inc(S.columns_loaded, 16)
            for slot in range(2):
                sp.wait_ge(S.ex_loaded[slot], 16)
            for slot in range(EARLY, WS):
                load_expert(sp, T, S, A, slot, slot)
            with sp.Fori(0, E0 // WS - 1) as q:
                for slot in range(WS):
                    sp.wait_ge(S.ey_done, q * WS + (slot + 1))
                    load_expert(sp, T, S, A, q * WS + (slot + WS), slot)
            sp.dma_start(T.w_a, A.L1_gnn_W_l.rearrange("(m p) n -> p m n", m=KD)).then_inc(S.wl_loaded, 16)
            sp.dma_start(T.w_b, A.L1_gnn_W_r.rearrange("(m p) n -> p m n", m=KD)).then_inc(S.wl_loaded, 16)
            sp.dma_start(T.b2_rows, A.L0_ffn_b2).then_inc(S.b2_loaded, 16)

        @block.gpsimd
        def _(pool):
            gather_rows(pool, T, A.rows0, T.ex, CAP, E0 // 4 - 2, S.ex_ids_ready, S.ex_turned, S.ex_loaded)

        @block.tensor
        def _(pe):
            def turn(q, r):
                wait_count(pe, S.ex_loaded[r % 2], q, 8 * WS, 16 * (r // 2 + 1))
                wait_count(pe, S.ex_turned_copied, q, WS, r - 1)
                for k in range(KD):
                    last = pe.transpose(T.ps[:, r % 2, k * CAP:(k + 1) * CAP], T.ex[:CAP, r % 2, k * 128:(k + 1) * 128],
                                        T.ident[:CAP, :CAP])
                last.then_inc(S.ex_turned, 1)

            def hidden(q, r):
                wait_count(pe, S.ex_turned_copied, q, WS, r + 1)
                wait_count(pe, S.ew_loaded[r % WS], q, 32, 32 * (r // WS + 1))
                wait_count(pe, S.eh_ready, q, WS, r - 1)
                for f in range(FK):
                    for k in range(KD):
                        last = pe.matmul(T.ps[:, 2 + r % 2, f * CAP:(f + 1) * CAP],
                                         T.ew1[r % WS][:, k, f * 128:(f + 1) * 128], T.ex_t[:, r % 2, k, :],
                                         start=(k == 0), stop=(k == KD - 1))
                last.then_inc(S.eh_done, 1)

            def output(q, r):
                wait_count(pe, S.eh_ready, q, WS, r + 1)
                wait_count(pe, S.ey_copied, q, WS, r - 1)
                for f in range(FK):
                    last = pe.matmul(T.ps[:CAP, 4 + r % 2, :], T.eh[:, r % 2, f, :], T.ew2[r % WS][:, f, :],
                                     start=(f == 0), stop=(f == FK - 1))
                last.then_inc(S.ey_done, 1)

            def step(q, r):
                hidden(q, r)
                if not is_last(q, r):
                    turn(q, r + 1)
                if not isinstance(q, int) or WS * q + r > 0:
                    output(q, r - 1)

            pe.wait_ge(S.columns_loaded, 64)
            for f in range(FK):
                pe.transpose(T.ps[:, 7, f * E0:(f + 1) * E0], T.eb1_rows[:, f * 128:(f + 1) * 128], T.ident[:E0, :E0])
            pe.transpose(T.ps[:, 6, 0:3 * KD], T.feature_rows, T.ident[:3 * KD, :3 * KD]).then_inc(S.columns_turned, 1)
            turn(0, 0)
            experts(pe, step)
            output(LOOPS, (E0 - 1) - WS * LOOPS)

        @block.scalar
        def _(act):
            act.wait_ge(S.columns_turned, 1)
            act.activation(T.feature[:], T.ps[:, 6, 0:3 * KD].rearrange("p (i m) -> p i m", m=KD), ACT.Copy)
            act.activation(T.eb1, T.ps[:, 7, 0:FK * E0].rearrange("p (f e) -> p f e", f=FK), ACT.Copy).then_inc(S.eb1_ready, 1)
            act.preload_act_table(ACT.Gelu_apprx_tanh)
            act.wait_ge(S.eb1_ready, 1)

            def store(q, r):
                wait_count(act, S.ey_copied, q, WS, r + 1)
                act.dma_start(A.y0[bass.ds(q * WS + r, 1)].rearrange("o c d -> (o c) d"), T.ey[:CAP, r % 2, :])\
                   .then_inc(S.ey_stored[r % 2], 16)

            def step(q, r):
                wait_count(act, S.eh_done, q, WS, r + 1)
                wait_count(act, S.ey_done, q, WS, r - 1)
                for f in range(FK):
                    last = act.activation(T.eh[:, r % 2, f, :], T.ps[:, 2 + r % 2, f * CAP:(f + 1) * CAP],
                                          ACT.Gelu_apprx_tanh, bias=T.eb1[:, f, bass.ds(q * WS + r, 1)])
                last.then_inc(S.eh_ready, 1)
                if not isinstance(q, int) or WS * q + r > 0:
                    store(q, r - 1)

            experts(act, step)
            store(LOOPS, (E0 - 1) - WS * LOOPS)
            for slot in range(2):
                act.wait_ge(S.ey_stored[slot], 8 * E0)

        @block.vector
        def _(dve):
            def turned(q, r):
                wait_count(dve, S.ex_turned, q, WS, r + 1)
                wait_count(dve, S.eh_done, q, WS, r - 1)
                dve.tensor_copy(T.ex_t[:, r % 2], T.ps[:, r % 2, 0:KD * CAP].rearrange("p (k c) -> p k c", k=KD))\
                   .then_inc(S.ex_turned_copied, 1)

            def output(q, r):
                wait_count(dve, S.ey_done, q, WS, r + 1)
                wait_count(dve, S.ey_stored[r % 2], q, 8 * WS, 16 * (r // 2))
                dve.tensor_copy(T.ey[:CAP, r % 2, :], T.ps[:CAP, 4 + r % 2, :]).then_inc(S.ey_copied, 1)

            def step(q, r):
                if not is_last(q, r):
                    turned(q, r + 1)
                if not isinstance(q, int) or WS * q + r > 0:
                    output(q, r - 1)

            turned(0, 0)
            experts(dve, step)
            output(LOOPS, (E0 - 1) - WS * LOOPS)


def second_convolution(nc, T, S, A):
    rows = (T.rows_a, T.rows_c)

    with nc.Block() as block:

        @block.gpsimd
        def _(pool):
            for t in range(NT):
                for j in range(TOP):
                    pool.indirect_dma_start(rows[j][:, t, :], None, A.y0.rearrange("e c d -> (e c) d"),
                                            bass.IndirectOffsetOnAxis(ap=T.row_i[:, t, j:j + 1], axis=0))\
                        .then_inc(S.y_gathered[t], 16)

        @block.tensor
        def _(pe):
            pe.wait_ge(S.wl_loaded, 32)
            for i, w in enumerate((T.w_a, T.w_b)):
                for k in range(KD):
                    for m in range(KD):
                        last = pe.transpose(T.ps[:, 4 * i + k, m * 128:(m + 1) * 128], w[:, m, k * 128:(k + 1) * 128],
                                            T.ident[:])
                    last.then_inc(S.wl_turned, 1)
            pe.wait_ge(S.wl_copied, 2 * KD)
            pe.wait_ge(S.b2_loaded, 16)
            for t in range(NT):
                if t >= 2:
                    pe.wait_ge(S.moe_added, t - 1)
                pe.wait_ge(S.diagonals_ready, t + 1)
                pe.wait_ge(S.y_gathered[t], 32)
                gated_sum(pe, T, t, t % 2, T.gates_t, T.b2_rows, rows).then_inc(S.moe_done, 1)
                for g in groups_after(t):
                    transpose_group(pe, T, T.rows_a, S.conv_rows, S, 3, g, 2, 6)
            pe.wait_ge(S.tiles_copied, 4 * TURNS)
            pe.wait_ge(S.ct_ready, NT)
            for m in range(KD):
                for c, (c0, n) in enumerate(CHUNKS):
                    j = 3 * m + c
                    if j >= 8:
                        pe.wait_ge(S.means_ready, j - 7)
                    for k in range(NT):
                        last = pe.matmul(T.ps[:, j % 8, 0:n], T.rows_a[:, k, m * 128:(m + 1) * 128],
                                         T.ct_f[:, k, c0:c0 + n], start=(k == 0), stop=(k == NT - 1))
                    last.then_inc(S.sums_done, 1)
            for m in range(KD):
                for c, (c0, n) in enumerate(CHUNKS):
                    j = 3 * m + c
                    if j < 8:
                        pe.wait_ge(S.means_ready, min(j + 9, KD * 3) if j < 4 else j + 1)
                    else:
                        pe.wait_ge(S.conv_relu, j - 7)
                    for k in range(KD):
                        pe.matmul(T.ps[:, j % 8, 0:n], T.wl_t[:, 1, k, m * 128:(m + 1) * 128],
                                  T.feats[:, k, c0:c0 + n], start=(k == 0), stop=False)
                    if j == 0:
                        pe.wait_ge(S.means_ready, KD * 3)
                    for k in range(KD):
                        last = pe.matmul(T.ps[:, j % 8, 0:n], T.wl_t[:, 0, k, m * 128:(m + 1) * 128],
                                         T.means[:, k, c0:c0 + n], start=False, stop=(k == KD - 1))
                    last.then_inc(S.conv_done, 1)
            pe.wait_ge(S.conv_relu, KD * 3)
            pe.wait_ge(S.conv_normed, KD)
            for t in range(NT):
                if t >= 8:
                    pe.wait_ge(S.conv_added, t - 7)
                for m in range(KD):
                    last = pe.transpose(T.ps[:P, t % 8, m * 128:(m + 1) * 128], T.conv[:, m, t * P:(t + 1) * P], T.ident[:])
                last.then_inc(S.conv_turned, 1)

        @block.scalar
        def _(act):
            def counts(t):
                act.activation(T.ct_f[:, t], T.ct[:, t], ACT.Copy).then_inc(S.ct_ready, 1)

            for i in range(2):
                for k in range(KD):
                    act.wait_ge(S.wl_turned, 4 * i + k + 1)
                    act.activation(T.wl_t[:, i, k, :], T.ps[:, 4 * i + k, :], ACT.Copy).then_inc(S.wl_copied, 1)
            for t in range(2):
                gate_matrices(act, T, t, S.moe_done, S.diagonals_ready)
            counts(0)
            for t in range(NT):
                if t + 1 < NT:
                    counts(t + 1)
                act.wait_ge(S.conv_var, t + 1)
                act.activation(T.std[:, t:t + 1], T.spread[:, t:t + 1], ACT.Sqrt).then_inc(S.conv_std, 1)
                if t + 2 < NT:
                    gate_matrices(act, T, t + 2, S.moe_done, S.diagonals_ready)
                for g in groups_after(t):
                    copy_group(act, T, T.feats, S, 3, g, 2, 6)
            for m in range(KD):
                for c, (c0, n) in enumerate(CHUNKS):
                    j = 3 * m + c
                    act.wait_ge(S.conv_done, j + 1)
                    act.activation(T.conv[:, m, c0:c0 + n], T.ps[:, j % 8, 0:n], ACT.Relu, bias=T.feature[:, 0, m:m + 1])\
                       .then_inc(S.conv_relu, 1)
                act.wait_ge(S.bn_var, m + 1)
                act.activation(T.bn_std[:, m:m + 1], T.bn_std[:, m:m + 1], ACT.Sqrt).then_inc(S.bn_root, 1)
                act.wait_ge(S.bn_ready, m + 1)
                act.activation(T.conv[:, m, :], T.conv[:, m, :], ACT.Identity, bias=T.bn_shift[:, m:m + 1],
                               scale=T.bn_scale[:, m:m + 1]).then_inc(S.conv_normed, 1)

        @block.vector
        def _(dve):
            link = Chain(dve, S.dve_chain, T.dve_at)

            def add(t):
                dve.wait_ge(S.moe_done, t + 1)
                dve.tensor_tensor(T.x[:, t, :], T.ps[:P, t % 2, :], T.x[:, t, :], ALU.add).then_inc(S.moe_added, 1)
                dve.wait_ge(S.moe_added, t + 1)
                row_moments(dve, link, T, T.x, t, S.conv_var)

            def normalized(t):
                dve.wait_ge(S.conv_std, t + 1)
                normalize(dve, link, T, T.rows_a, T.x, t).then_inc(S.conv_rows, 1)

            for t in range(NT):
                add(t)
                if t > 0:
                    normalized(t - 1)
            normalized(NT - 1)
            for m in range(KD):
                for c, (c0, n) in enumerate(CHUNKS):
                    j = 3 * m + c
                    dve.wait_ge(S.sums_done, j + 1)
                    dve.tensor_tensor(T.means[:, m, c0:c0 + n], T.ps[:, j % 8, 0:n], T.rdeg[:, c0:c0 + n], ALU.mult)\
                       .then_inc(S.means_ready, 1)
            for m in range(KD):
                for c, (c0, n) in enumerate(CHUNKS):
                    dve.wait_ge(S.conv_relu, 3 * m + c + 1)
                    last = dve.bn_stats(T.bn_parts[:, m, c, :], T.conv[:, m, c0:c0 + n])
                link(last)
                mean, scale, shift = T.bn_moments[:, m, 0:1], T.bn_scale[:, m:m + 1], T.bn_shift[:, m:m + 1]
                link(dve.bn_aggr(T.bn_moments[:, m, :], T.bn_parts[:, m].rearrange("p c s -> p (c s)")))
                dve.tensor_scalar(T.bn_std[:, m:m + 1], T.bn_moments[:, m, 1:2], EPS, None, ALU.add).then_inc(S.bn_var, 1)
                dve.wait_ge(S.bn_root, m + 1)
                link(dve.reciprocal(scale, T.bn_std[:, m:m + 1]))
                link(dve.tensor_tensor(scale, scale, T.feature[:, 1, m:m + 1], ALU.mult))
                link(dve.tensor_tensor(shift, mean, scale, ALU.mult))
                dve.tensor_tensor(shift, T.feature[:, 2, m:m + 1], shift, ALU.subtract).then_inc(S.bn_ready, 1)
            for t in range(NT):
                dve.wait_ge(S.conv_turned, t + 1)
                dve.tensor_tensor(T.x[:, t, :], T.ps[:P, t % 8, :], T.x[:, t, :], ALU.add).then_inc(S.conv_added, 1)


def second_router(nc, T, S, A):
    with nc.Block() as block:

        @block.sync
        def _(sp):
            sp.dma_start(T.w_r1, A.L1_ffn_Wr.rearrange("(k p) e -> p k e", k=KD)).then_inc(S.wr1_loaded, 16)
            sp.dma_start(T.b2_rows1, A.L1_ffn_b2).then_inc(S.b21_loaded, 16)
            sp.dma_start(T.w1, A.L1_ffn_W1.rearrange("e (k p) f -> p e k f", k=KD)).then_inc(S.w12_loaded, 16)
            sp.dma_start(T.w2, A.L1_ffn_W2.rearrange("e (k p) n -> p e k n", k=F1 // 128)).then_inc(S.w12_loaded, 16)
            sp.dma_start(T.b1, A.L1_ffn_b1.rearrange("(o e) f -> o (e f)", o=1).to_broadcast([BR, E1 * F1]))\
              .then_inc(S.b11_loaded, 16)
            sp.wait_ge(S.f_rows, NT)
            sp.dma_start(A.rows1.rearrange("(t p) d -> p t d", t=NT)[0:120], T.rows_b[0:120]).then_inc(S.rows1_stored, 16)
            sp.dma_start(A.rows1.rearrange("(t p) d -> p t d", t=NT)[120:P], T.rows_b[120:P]).then_inc(S.rows1_stored, 16)
            sp.wait_ge(S.rows1_stored, 32)

        @block.tensor
        def _(pe):
            pe.wait_ge(S.wr1_loaded, 16)
            for g in range(len(GROUPS)):
                transpose_group(pe, T, T.rows_b, S.f_rows, S, 4, g, 2, 4)
                pe.wait_ge(S.tiles_copied, 4 * TURNS + (g + 1) * KD)
                for t in tiles_of(g):
                    for k in range(KD):
                        last = pe.matmul(T.ps[:P, 0, t * E1:(t + 1) * E1], T.feats[:, k, t * P:(t + 1) * P], T.w_r1[:, k, :],
                                         start=(k == 0), stop=(k == KD - 1))
            last.then_inc(S.logits1_done, 1)
            pe.wait_ge(S.chosen, 2)
            for t in range(NT):
                pe.matmul(T.ps[:, 1, 0:E1], T.ones_bf[:, 0:BR], T.onehot[:, TOP, t, 0:E1], start=(t == 0), stop=(t == NT - 1))
            count_before(pe, T, E1).then_inc(S.counted, 1)
            pe.wait_ge(S.placed, 2)
            make_table(pe, T, 7, BR, NB).then_inc(S.table_made, 1)
            pe.wait_ge(S.gates_ready, 2)
            for t in range(NT):
                last = pe.transpose(T.ps[:E1, 4 + t // 4, t % 4 * P:(t % 4 + 1) * P], T.gate_rows[:, t, 0:E1], T.ident[:P, :P])
            last.then_inc(S.gates_turned, 1)

        @block.scalar
        def _(act):
            row_roots(act, T, range(0, 6), S.f_var, S.f_std)
            copy_group(act, T, T.feats, S, 4, 0, 2, 4)
            row_roots(act, T, range(6, NT), S.f_var, S.f_std)
            for g in range(1, len(GROUPS)):
                copy_group(act, T, T.feats, S, 4, g, 2, 4)
            act.wait_ge(S.logits1_done, 1)
            act.activation(T.logits[:, :, 0:E1], T.ps[:P, 0, 0:NT * E1].rearrange("p (t e) -> p t e", t=NT), ACT.Copy)\
               .then_inc(S.logits1_ready, 1)
            act.wait_ge(S.gap_ready, 2)
            act.activation(T.gap[:], T.gap[:], ACT.Exp).then_inc(S.gap_exp, 1)
            act.wait_ge(S.gates_turned, 2)
            for b in range(3):
                n = min(4, NT - 4 * b)
                act.activation(T.gates_t1[:, 4 * b * P:(4 * b + n) * P], T.ps[:E1, 4 + b, 0:n * P], ACT.Copy)

        @block.vector
        def _(dve):
            link = Chain(dve, S.dve_chain, T.dve_at)
            for t in range(NT + 1):
                if t < NT:
                    row_moments(dve, link, T, T.x, t, S.f_var)
                if t > 0:
                    dve.wait_ge(S.f_std, t)
                    normalize(dve, link, T, T.rows_b, T.x, t - 1).then_inc(S.f_rows, 1)
            dve.wait_ge(S.logits1_ready, 1)
            choose(dve, link, T, E1, S.chosen, S.gap_ready)
            dve.wait_ge(S.gap_exp, 2)
            gates(dve, link, T)
            dve.wait_ge(S.counted, 2)
            positions(dve, link, T, E1)
            link(dve.tensor_copy(T.totals[:], T.ps[:, 1, 0:E1]))
            link(dve.tensor_tensor(T.below[:], T.row_starts[:].unsqueeze(1).to_broadcast([BR, E1, BLOCKS]),
                                   T.totals[:].unsqueeze(2).to_broadcast([BR, E1, BLOCKS]), ALU.is_lt))
            dve.memset(T.first_block[:, 0:1], 0.0)
            link(dve.tensor_reduce(T.totals[:], T.below[:], AX.X, ALU.add))
            for e in range(E1):
                link(dve.tensor_tensor(T.first_block[:, e + 1:e + 2], T.first_block[:, e:e + 1], T.totals[:, e:e + 1], ALU.add))
            link(dve.tensor_tensor(T.ended[:], T.block_iota[:].unsqueeze(2).to_broadcast([BR, NB, E1]),
                                   T.first_block[:, 1:E1 + 1].unsqueeze(1).to_broadcast([BR, NB, E1]), ALU.is_ge))
            link(dve.tensor_reduce(T.block_expert_f[:], T.ended[:], AX.X, ALU.add))
            dve.tensor_scalar(T.block_expert[:], T.block_expert_f[:], float(E1 - 1), None, ALU.min)
            link(dve.tensor_tensor(T.ended[:, 0:NB // 4, 0], T.block_iota[:].rearrange("p (f b) -> p f b", b=4)[:, :, 0],
                                   T.first_block[:, E1:E1 + 1].to_broadcast([BR, NB // 4]), ALU.is_lt))
            link(dve.tensor_reduce(T.totals[:, 0:1], T.ended[:, 0:NB // 4, 0], AX.X, ALU.add))
            dve.tensor_scalar(T.loops[0:1, 0:1], T.totals[0:1, 0:1], 2.0, None, ALU.subtract)
            dve.tensor_scalar(T.loops[0:1, 1:2], T.totals[0:1, 0:1], 2.0, 2.0, ALU.mult, ALU.subtract)
            within, row, at = T.keep, T.scratch, T.begin
            choices = T.position[:].rearrange("p t j -> p (t j)")
            link(dve.tensor_tensor(T.past[:], T.row_starts[:P, 1:].unsqueeze(1).to_broadcast([P, NT * TOP, BLOCKS - 1]),
                                   choices.unsqueeze(2).to_broadcast([P, NT * TOP, BLOCKS - 1]), ALU.is_le))
            link(dve.tensor_reduce(within[:].rearrange("p t j -> p (t j)"), T.past[:], AX.X, ALU.add))
            link(dve.scalar_tensor_tensor(out=row[:], in0=within[:], scalar=-float(BR), in1=T.position[:],
                                          op0=ALU.mult, op1=ALU.add))
            for j in range(TOP):
                link(dve.tensor_tensor(T.picked[:, :, 0:E1], T.onehot[:, j, :, 0:E1],
                                       T.first_block[:P, 0:E1].unsqueeze(1).to_broadcast([P, NT, E1]), ALU.mult))
                link(dve.tensor_reduce(at[:, :, j], T.picked[:, :, 0:E1], AX.X, ALU.add))
            link(dve.tensor_tensor(within[:], within[:], at[:], ALU.add))
            for j in range(TOP):
                last = dve.tensor_tensor(T.place[:, j], T.block_iota[:P].unsqueeze(1).to_broadcast([P, NT, NB]),
                                         within[:, :, j].unsqueeze(2).to_broadcast([P, NT, NB]), ALU.is_equal)
            link(last)
            place(dve, link, T, BR, row, NB, S.placed)
            link(dve.scalar_tensor_tensor(out=row[:], in0=within[:], scalar=float(BR), in1=row[:], op0=ALU.mult, op1=ALU.add))
            dve.tensor_copy(T.row_i[:], row[:])
            gate_rows(dve, link, T, E1, S.gates_ready)
            dve.wait_ge(S.table_made, 2)
            dve.tensor_copy(T.ids[:, 0:NB], T.ps[:, 7, 0:NB])


def second_experts(nc, T, S, A):
    FK = F1 // 128

    def blocks(engine, step):
        pairs = engine.value_load(T.loops[0:1, 1:2], min_val=2 * FOURS - 2, max_val=NB // 2 - 2)
        for r in range(2):
            step(0, r)
        with engine.Fori(0, pairs) as q:
            for r in range(2, 4):
                step(q, r)
        step(pairs, 2)
        step(pairs, 3, last=True)
        return pairs, 3

    def is_first(q, r):
        return isinstance(q, int) and 2 * q + r == 0

    def expert_of(engine, q, r):
        return engine.value_load(T.block_expert[0:1, bass.ds(q * 2 + r, 1)], min_val=0, max_val=E1 - 1)

    with nc.Block() as block:

        @block.gpsimd
        def _(pool):
            loops = pool.value_load(T.loops[0:1, 0:1], min_val=FOURS - 2, max_val=NB // 4 - 2)
            gather_rows(pool, T, A.rows1, T.rx, BR, loops, S.rx_ids_ready, S.rx_turned, S.rx_loaded)

        @block.tensor
        def _(pe):
            def turn(q, r):
                wait_count(pe, S.rx_loaded[r % 2], q, 16, 16 * (r // 2 + 1))
                wait_count(pe, S.rx_copied, q, 2, r - 1)
                for k in range(KD):
                    last = pe.transpose(T.ps[:, r % 2, k * BR:(k + 1) * BR], T.rx[:, r % 2, k * 128:(k + 1) * 128], T.ident[:])
                last.then_inc(S.rx_turned, 1)

            def hidden(q, r):
                e = expert_of(pe, q, r)
                wait_count(pe, S.rx_copied, q, 2, r + 1)
                wait_count(pe, S.rh_summed, q, 2, r - 1)
                for k in range(KD):
                    last = pe.matmul(T.ps[:, 2 + r % 2, 0:F1], T.rx_t[:, r % 2, k, :],
                                     T.w1[:, bass.ds(e, 1), k, :].rearrange("p o f -> p (o f)"),
                                     start=(k == 0), stop=(k == KD - 1))
                last.then_inc(S.rh_done, 1)

            def turn_hidden(q, r):
                wait_count(pe, S.rh_ready, q, 2, r + 1)
                wait_count(pe, S.rh_copied, q, 2, r - 1)
                for f in range(FK):
                    last = pe.transpose(T.ps[:, 4 + r % 2, f * BR:(f + 1) * BR], T.rh[:, r % 2, f * 128:(f + 1) * 128], T.ident[:])
                last.then_inc(S.rh_turned, 1)

            def output(q, r):
                e = expert_of(pe, q, r)
                wait_count(pe, S.rh_copied, q, 2, r + 1)
                wait_count(pe, S.ry_copied, q, 2, r - 1)
                for f in range(FK):
                    last = pe.matmul(T.ps[:, 6 + r % 2, :], T.rh_t[:, r % 2, f, :],
                                     T.w2[:, bass.ds(e, 1), f, :].rearrange("p o n -> p (o n)"),
                                     start=(f == 0), stop=(f == FK - 1))
                last.then_inc(S.ry_done, 1)

            def step(q, r, last=False):
                if not is_first(q, r):
                    turn_hidden(q, r - 1)
                hidden(q, r)
                if not last:
                    turn(q, r + 1)
                if not is_first(q, r):
                    output(q, r - 1)

            pe.wait_ge(S.w12_loaded, 32)
            turn(0, 0)
            end = blocks(pe, step)
            turn_hidden(*end)
            output(*end)

        @block.scalar
        def _(act):
            def hidden(q, r):
                wait_count(act, S.rh_summed, q, 2, r + 1)
                wait_count(act, S.rh_turned, q, 2, r - 1)
                act.activation(T.rh[:, r % 2, :], T.rh_sum[:, r % 2, :], ACT.Gelu).then_inc(S.rh_ready, 1)

            def turned(q, r):
                wait_count(act, S.rh_turned, q, 2, r + 1)
                wait_count(act, S.ry_done, q, 2, r - 1)
                act.activation(T.rh_t[:, r % 2], T.ps[:, 4 + r % 2, 0:F1].rearrange("p (f c) -> p f c", f=FK), ACT.Copy)\
                   .then_inc(S.rh_copied, 1)

            def store(q, r, stored):
                wait_count(act, S.ry_copied, q, 2, r + 1)
                act.dma_start(A.y1[bass.ds(q * 2 + r, 1)].rearrange("o c d -> (o c) d"), T.ry[:, r % 2, :])\
                   .then_inc(stored, 16)

            def step(q, r, last=False):
                if not is_first(q, r):
                    turned(q, r - 1)
                hidden(q, r)
                if not is_first(q, r):
                    store(q, r - 1, S.ry_last if last else S.ry_stored[(r - 1) % 2])

            act.preload_act_table(ACT.Gelu)
            end = blocks(act, step)
            turned(*end)
            store(*end, S.ry_last)
            act.wait_ge(S.ry_last, 32)

        @block.vector
        def _(dve):
            def turned(q, r):
                wait_count(dve, S.rx_turned, q, 2, r + 1)
                wait_count(dve, S.rh_done, q, 2, r - 1)
                dve.tensor_copy(T.rx_t[:, r % 2], T.ps[:, r % 2, :].rearrange("p (k c) -> p k c", k=KD)).then_inc(S.rx_copied, 1)

            def hidden(q, r):
                e = expert_of(dve, q, r)
                wait_count(dve, S.rh_done, q, 2, r + 1)
                wait_count(dve, S.rh_ready, q, 2, r - 1)
                dve.tensor_tensor(T.rh_sum[:, r % 2, :], T.ps[:, 2 + r % 2, 0:F1],
                                  T.b1_of[:, bass.ds(e, 1), :].rearrange("p o f -> p (o f)"), ALU.add).then_inc(S.rh_summed, 1)

            def output(q, r):
                wait_count(dve, S.ry_done, q, 2, r + 1)
                wait_count(dve, S.ry_stored[r % 2], q, 16, 16 * (r // 2))
                dve.tensor_copy(T.ry[:, r % 2, :], T.ps[:, 6 + r % 2, :]).then_inc(S.ry_copied, 1)

            def step(q, r, last=False):
                hidden(q, r)
                if not last:
                    turned(q, r + 1)
                if not is_first(q, r):
                    output(q, r - 1)

            dve.wait_ge(S.b11_loaded, 16)
            turned(0, 0)
            end = blocks(dve, step)
            output(*end)


def finish(nc, T, S, A):
    rows = (T.rows_a, T.rows_d)

    with nc.Block() as block:

        @block.gpsimd
        def _(pool):
            for t in range(NT):
                for j in range(TOP):
                    pool.indirect_dma_start(rows[j][:, t, :], None, A.y1.rearrange("b c d -> (b c) d"),
                                            bass.IndirectOffsetOnAxis(ap=T.row_i[:, t, j:j + 1], axis=0))\
                        .then_inc(S.y_gathered[t], 16)

        @block.scalar
        def _(act):
            for t in range(NT):
                gate_matrices(act, T, t, S.moe1_done, S.diagonals1_ready)

        @block.tensor
        def _(pe):
            pe.wait_ge(S.b21_loaded, 16)
            for t in range(NT):
                if t >= 8:
                    pe.wait_ge(S.out_ready, t - 7)
                pe.wait_ge(S.diagonals1_ready, t + 1)
                pe.wait_ge(S.y_gathered[t], 64)
                gated_sum(pe, T, t, t % 8, T.gates_t1, T.b2_rows1, rows).then_inc(S.moe1_done, 1)

        @block.vector
        def _(dve):
            for t in range(NT):
                dve.wait_ge(S.moe1_done, t + 1)
                dve.tensor_tensor(T.x[:, t, :], T.ps[:P, t % 8, :], T.x[:, t, :], ALU.add).then_inc(S.out_ready, 1)

        @block.sync
        def _(sp):
            for t in range(NT):
                sp.wait_ge(S.out_ready, t + 1)
                for p0, p1 in ((0, 120), (120, P)):
                    sp.dma_start(A.out[t * P + p0:t * P + p1], T.x[p0:p1, t, :]).then_inc(S.out_stored, 16)
            sp.wait_ge(S.out_stored, 32 * NT)



def semaphores_by_name(semaphores):
    S = Named()
    S.tiles_copied, S.tiles_turned = semaphores("tiles_copied tiles_turned")
    S.const_pool, S.edges_loaded, S.x_loaded = semaphores("const_pool edges_loaded x_loaded")
    S.w0_loaded, S.wq_loaded, S.affine_loaded = semaphores("w0_loaded wq_loaded affine_loaded")
    S.prep_done, S.prep_transposed, S.columns_ready = semaphores("prep_done prep_transposed columns_ready")
    S.dve_chain, S.z_var, S.z_std = semaphores("dve_chain z_var z_std")
    S.z_rows, S.z_done, S.z_copied = semaphores("z_rows z_done z_copied")
    S.at_added, S.ct_added, S.pass_step = semaphores("at_added ct_added pass_step")
    S.counts_done, S.weighted_ready, S.sources_ready = semaphores("counts_done weighted_ready sources_ready")
    S.products_done, S.cells_ready, S.weights_copied = semaphores("products_done cells_ready weights_copied")
    S.ew_loaded = semaphores(" ".join(f"ew_loaded{i}" for i in range(WS)))
    S.wk_loaded, S.agg_used, S.agg_done = semaphores("wk_loaded agg_used agg_done")
    S.attn_rows, S.xf_var, S.xf_std = semaphores("attn_rows xf_var xf_std")
    S.wv_loaded, S.spare_filled, S.partial_degrees = semaphores("wv_loaded spare_filled partial_degrees")
    S.degrees_done, S.proj_copied, S.proj_done = semaphores("degrees_done proj_copied proj_done")
    S.wo_loaded, S.exp_done, S.scores_done = semaphores("wo_loaded exp_done scores_done")
    S.probs_ready, S.probs_copied, S.out_copied = semaphores("probs_ready probs_copied out_copied")
    S.probs_turned, S.values_done, S.v_copied = semaphores("probs_turned values_done v_copied")
    S.v_done, S.max_ready, S.inverse_ready = semaphores("v_done max_ready inverse_ready")
    S.wr_loaded, S.wo_used, S.wo_done = semaphores("wr_loaded wo_used wo_done")
    S.x2_rows, S.logits_done, S.chosen = semaphores("x2_rows logits_done chosen")
    S.counted, S.placed, S.table_made = semaphores("counted placed table_made")
    S.gates_ready, S.gates_turned, S.x2_var = semaphores("gates_ready gates_turned x2_var")
    S.x2_std, S.logits_ready, S.gap_ready = semaphores("x2_std logits_ready gap_ready")
    S.gap_exp, S.gates_t_ready, S.rows0_stored = semaphores("gap_exp gates_t_ready rows0_stored")
    S.columns_loaded, S.ey_done, S.wl_loaded = semaphores("columns_loaded ey_done wl_loaded")
    S.b2_loaded, S.ex_ids_ready, S.ex_turned = semaphores("b2_loaded ex_ids_ready ex_turned")
    S.ex_turned_copied, S.eh_ready, S.eh_done = semaphores("ex_turned_copied eh_ready eh_done")
    S.ey_copied, S.columns_turned, S.eb1_ready = semaphores("ey_copied columns_turned eb1_ready")
    S.wl_turned, S.wl_copied, S.moe_added = semaphores("wl_turned wl_copied moe_added")
    S.diagonals_ready, S.moe_done, S.conv_rows = semaphores("diagonals_ready moe_done conv_rows")
    S.ct_ready, S.means_ready, S.sums_done = semaphores("ct_ready means_ready sums_done")
    S.conv_relu, S.conv_done, S.conv_normed = semaphores("conv_relu conv_done conv_normed")
    S.conv_added, S.conv_turned, S.conv_var = semaphores("conv_added conv_turned conv_var")
    S.conv_std, S.bn_var, S.bn_root = semaphores("conv_std bn_var bn_root")
    [S.bn_ready] = semaphores("bn_ready")
    S.ex_loaded = semaphores(" ".join(f"ex_loaded{i}" for i in range(2)))
    S.ey_stored = semaphores(" ".join(f"ey_stored{i}" for i in range(2)))
    S.y_gathered = semaphores(" ".join(f"y_gathered{i}" for i in range(NT)))
    S.wr1_loaded, S.b21_loaded, S.w12_loaded = semaphores("wr1_loaded b21_loaded w12_loaded")
    S.b11_loaded, S.f_rows, S.rows1_stored = semaphores("b11_loaded f_rows rows1_stored")
    S.logits1_done, S.f_var, S.f_std = semaphores("logits1_done f_var f_std")
    S.logits1_ready, S.rx_ids_ready, S.rx_turned = semaphores("logits1_ready rx_ids_ready rx_turned")
    S.rx_copied, S.rh_summed, S.rh_done = semaphores("rx_copied rh_summed rh_done")
    S.rh_ready, S.rh_copied, S.rh_turned = semaphores("rh_ready rh_copied rh_turned")
    S.ry_copied, S.ry_done, S.ry_last = semaphores("ry_copied ry_done ry_last")
    S.moe1_done, S.diagonals1_ready, S.out_ready = semaphores("moe1_done diagonals1_ready out_ready")
    [S.out_stored] = semaphores("out_stored")
    S.rx_loaded = semaphores(" ".join(f"rx_loaded{i}" for i in range(2)))
    S.ry_stored = semaphores(" ".join(f"ry_stored{i}" for i in range(2)))
    return S


def program(nc, A):
    with ExitStack() as stack:
        def sbuf(name, shape, dtype=F32):
            return stack.enter_context(nc.sbuf_tensor("b_" + name, shape, dtype))[:]

        def semaphores(names):
            return [stack.enter_context(nc.semaphore(name)) for name in names.split()]

        S = semaphores_by_name(semaphores)
        A.rows0 = nc.dram_tensor("rows0", [N, D], F32).ap()
        A.y0 = nc.dram_tensor("y0", [E0, CAP, D], F32).ap()
        A.rows1 = nc.dram_tensor("rows1", [N, D], F32).ap()
        A.y1 = nc.dram_tensor("y1", [NB, BR, D], F32).ap()

        T = Named()
        T.dve_at = [0]
        T.ps = stack.enter_context(nc.psum_tensor("ps", [128, 8, 512], F32))

        T.x = sbuf("x", [P, NT, D])
        T.ident = sbuf("ident", [128, 128])
        T.before = sbuf("before", [P, P], BF16)
        T.ones_bf = sbuf("ones_bf", [P, 128], BF16)
        T.ones = sbuf("ones", [128, 128])
        T.expert_iota = sbuf("expert_iota", [P, E0])
        T.block_iota = sbuf("block_iota", [BR, NB])
        T.row_starts = sbuf("row_starts", [BR, BLOCKS])
        T.token = sbuf("token", [P, NT])
        T.ids = sbuf("ids", [128, E0], I32)
        T.ex_ids = sbuf("ex_ids", [128, 4], I32)
        T.stats = sbuf("stats", [P, 6])
        T.moments = sbuf("moments", [P, NT, 2])
        T.spread, T.std, T.rstd, T.gap = (sbuf(n, [P, NT]) for n in ("spread", "std", "rstd", "gap"))
        T.row_max, T.neg_max = (sbuf(n, [P, 4]) for n in ("row_max", "neg_max"))
        T.sums = sbuf("sums", [P, 4, 2])
        T.total = sbuf("total", [P, 2])
        T.top = sbuf("top", [P, NT, 8])
        T.top_i = sbuf("top_i", [P, NT, 8], U32)
        T.expert, T.gate, T.position, T.keep, T.begin, T.scratch = (
            sbuf(n, [P, NT, TOP]) for n in ("expert", "gate", "position", "keep", "begin", "scratch"))
        T.row_i = sbuf("row_i", [P, NT, TOP], I32)
        T.feature = sbuf("feature", [128, 3, KD])
        T.bn_parts = sbuf("bn_parts", [128, KD, 3, 6])
        T.bn_moments = sbuf("bn_moments", [128, KD, 2])
        T.bn_std, T.bn_scale, T.bn_shift = (sbuf(n, [128, KD]) for n in ("bn_std", "bn_scale", "bn_shift"))
        T.row_iota = sbuf("row_iota", [P, 128], I16)
        T.lo_iota = T.row_iota[:, 0:P]
        T.w_r1 = sbuf("w_r1", [128, KD, E1])
        T.totals = sbuf("totals", [BR, E1])
        T.first_block = sbuf("first_block", [BR, E1 + 1])
        T.block_expert_f = sbuf("block_expert_f", [BR, NB])
        T.loops = sbuf("loops", [1, 2], I32)
        T.block_expert = sbuf("block_expert", [BR, NB], I32)

        T.rdeg = sbuf("rdeg", [128, N])

        w_a, w_b = (sbuf(n, [128, KD, D]) for n in ("w_a", "w_b"))
        affine = sbuf("affine", [P, 4 * D])
        r1, r2, r5, r6 = (sbuf(n, [128, NT * D]) for n in ("r1", "r2", "r5", "r6"))
        r34 = sbuf("r34", [128, NT * N + NT * N // 2])
        T.w_a, T.w_b = w_a, w_b
        T.rows_a, T.rows_b, T.rows_c, T.rows_d = (rows_of(r) for r in (r1, r5, r6, r2))
        T.feats = feats_of(r2)

        T.at = r34[:P, 0:NT * N].rearrange("p (k n) -> p k n", k=NT)
        T.ct = r34[:P, NT * N:].bitcast(U16).rearrange("p (k n) -> p k n", k=NT)
        cut = Carve(r5)
        T.dst_i, T.src_i = (cut(NG, CJ * EC, I32).rearrange("p (j e) -> p j e", j=CJ) for _ in range(2))
        T.wgt, T.dst_f, T.src_f, T.hi_f, T.lo_row, T.cell_row = (
            cut(NG, CJ * EC).rearrange("p (j e) -> p j e", j=CJ) for _ in range(6))
        T.base_rows = cut(NG, 128)
        T.further = cut(NG, WINDOWS)
        T.group_min, T.group_max = cut(NG, 1), cut(NG, 1)
        T.win_starts, T.cell_iota = cut(NG, WINDOWS, I16), cut(P, WC, I16)
        T.base_row, T.passes = cut(1, NG, I32), cut(1, 1, I32)
        T.base_all, T.base_now = cut(EC, NG), cut(EC, NG)
        cut = Carve(r6)
        T.sources = cut(EC, 2 * CJ * P).rearrange("e (b j s) -> e b j s", b=2, j=CJ)
        T.weighted = cut(EC, 2 * CJ * P).rearrange("e (b j s) -> e b j s", b=2, j=CJ)
        T.cells = cut(EC, 2 * CJ * WC).rearrange("e (b j c) -> e b j c", b=2, j=CJ)
        T.copied = cut(P, 2 * WC).rearrange("p (b c) -> p b c", b=2)
        T.lo_col, T.hi_col, T.dst_col, T.w_col, T.rel_col, T.valid_col, T.cell_col = (
            cut(EC, NG * CJ).rearrange("e (g j) -> e g j", j=CJ) for _ in range(7))
        T.sources_bf = r6[:EC, 0:2 * CJ * P].bitcast(BF16).rearrange("e (b j s h) -> e b j s h", b=2, j=CJ, h=2)
        T.cells_bf = r6[:EC, 4 * CJ * P:4 * CJ * P + 2 * CJ * WC].bitcast(BF16)\
            .rearrange("e (b j c h) -> e b j c h", b=2, j=CJ, h=2)
        T.affine = affine[:].rearrange("p (a d) -> p a d", a=4)

        constants(nc, T, S, A)
        first_projection(nc, T, S, A)
        adjacency(nc, T, S, A)
        first_convolution(nc, T, S, A)

        cut = Carve(r34[:, 0:NT * N])
        T.qt, T.kt = (cut(128, KD * N).rearrange("p (k n) -> p k n", k=KD) for _ in range(2))
        T.probs = [cut(P, N), cut(P, N), w_a.rearrange("p k d -> p (k d)")[:P, 0:N]]
        T.w_v = r6[:, 0:KD * D].rearrange("p (k d) -> p k d", k=KD)
        T.probs_t = r6[:P, 0:4 * N].rearrange("p (s n) -> p s n", s=4)
        T.v, T.ot = rows_of(r1), feats_of(r2)
        projections(nc, T, S, A)
        attention(nc, T, S, A)

        def table(cut, rows, columns):
            T.place_rows = cut(P, NT * TOP * rows).rearrange("p (c r) -> p c r", r=rows)
            T.place_columns = cut(P, TOP * NT * columns).rearrange("p (j t c) -> p j t c", j=TOP, t=NT)

        def router(cut, experts, rows):
            T.logits, T.picked = (cut(P, NT * experts).rearrange("p (t e) -> p t e", t=NT) for _ in range(2))
            T.onehot = cut(P, (TOP + 1) * NT * experts, BF16).rearrange("p (j t e) -> p j t e", j=TOP + 1, t=NT)
            T.gate_rows = rows(P, NT * 128).rearrange("p (t e) -> p t e", t=NT)

        slot = KD * F0 + F0 // 128 * D
        slots = [region[:, i * slot:(i + 1) * slot] for region, n in ((r34, EARLY), (r2, 2), (r6, WS - EARLY - 2))
                 for i in range(n)]
        T.ew1 = [s[:, 0:KD * F0].rearrange("p (k f) -> p k f", k=KD) for s in slots]
        T.ew2 = [s[:, KD * F0:].rearrange("p (k n) -> p k n", k=F0 // 128) for s in slots]
        cut = Carve(w_a.rearrange("p k d -> p (k d)"))
        T.w_r = cut(128, KD * E0).rearrange("p (k e) -> p k e", k=KD)
        router(Carve(r34[:, 0:NT * N], EARLY * slot), E0, cut)
        table(Carve(r6), CAP, E0)
        T.place = T.onehot
        T.gates_t, T.b2_rows = affine[:E0, 0:N], affine[:E0, N:N + D]
        T.feats = feats_of(r6)
        first_router(nc, T, S, A)

        cut = Carve(r1)
        T.ex = cut(128, 2 * D).rearrange("p (s d) -> p s d", s=2)
        T.ex_t = cut(128, 2 * KD * CAP).rearrange("p (s k c) -> p s k c", s=2, k=KD)
        T.eh = cut(128, 2 * F0 // 128 * CAP).rearrange("p (s f c) -> p s f c", s=2, f=F0 // 128)
        T.ey = cut(128, 2 * D).rearrange("p (s d) -> p s d", s=2)
        T.eb1_rows = cut(E0, F0)
        T.feature_rows = cut(3 * KD, 128)
        T.eb1 = cut(128, F0 // 128 * E0).rearrange("p (f e) -> p f e", f=F0 // 128)
        first_experts(nc, T, S, A)

        T.ct_f = r34[:P, 0:NT * N].rearrange("p (k n) -> p k n", k=NT)
        T.wl_t = r5[:, 0:2 * KD * D].rearrange("p (i k d) -> p i k d", i=2, k=KD)
        T.diagonal = r5[:P, 2 * KD * D:2 * KD * D + 2 * TOP * P].rearrange("p (b j q) -> p b j q", b=2, j=TOP)
        T.feats = feats_of(r2)
        T.means, T.conv = feats_of(r6), feats_of(r1)
        second_convolution(nc, T, S, A)

        cut = Carve(r34)
        T.w1 = cut(128, E1 * KD * F1).rearrange("p (e k f) -> p e k f", e=E1, k=KD)
        T.w2 = cut(128, E1 * F1 // 128 * D).rearrange("p (e k n) -> p e k n", e=E1, k=F1 // 128)
        router(cut, E1, cut)
        T.gates_t1, T.b2_rows1 = affine[:E1, 0:N], affine[:E1, N:N + D]
        T.b1 = r6[:, 0:E1 * F1]
        cut = Carve(r1)
        table(cut, BR, NB)
        T.place = cut(P, TOP * NT * NB).rearrange("p (j t b) -> p j t b", j=TOP, t=NT)
        cut = Carve(r6, E1 * F1)
        T.below = cut(BR, E1 * BLOCKS).rearrange("p (e k) -> p e k", e=E1)
        T.ended = cut(BR, NB * E1).rearrange("p (b e) -> p b e", b=NB)
        T.past = cut(P, NT * TOP * (BLOCKS - 1)).rearrange("p (c k) -> p c k", c=NT * TOP)
        second_router(nc, T, S, A)

        T.b1_of = T.b1.rearrange("p (e f) -> p e f", e=E1)
        cut = Carve(r1)
        T.rx = cut(128, 2 * D).rearrange("p (s d) -> p s d", s=2)
        T.rx_t = cut(128, 2 * KD * BR).rearrange("p (s k c) -> p s k c", s=2, k=KD)
        T.rh_sum, T.rh = (cut(128, 2 * F1).rearrange("p (s f) -> p s f", s=2) for _ in range(2))
        T.rh_t = cut(128, 2 * F1).rearrange("p (s f c) -> p s f c", s=2, f=F1 // 128)
        T.ry = cut(128, 2 * D).rearrange("p (s d) -> p s d", s=2)
        second_experts(nc, T, S, A)
        finish(nc, T, S, A)



NAMES = ["x", "src", "dst", "edge_weight", "L0_gnn_W", "L0_ffn_ln1_g", "L0_ffn_ln1_b", "L0_ffn_wq", "L0_ffn_wk",
         "L0_ffn_wv", "L0_ffn_wo", "L0_ffn_ln2_g", "L0_ffn_ln2_b", "L0_ffn_wr", "L0_ffn_w1", "L0_ffn_b1", "L0_ffn_w2",
         "L0_ffn_b2", "L1_gnn_W_l", "L1_gnn_b_l", "L1_gnn_W_r", "L1_gnn_gamma", "L1_gnn_beta", "L1_ffn_Wr", "L1_ffn_W1",
         "L1_ffn_b1", "L1_ffn_W2", "L1_ffn_b2"]


def by_name(places, out):
    A = Named()
    (A.x, A.src, A.dst, A.edge_weight, A.L0_gnn_W, A.L0_ffn_ln1_g, A.L0_ffn_ln1_b, A.L0_ffn_wq, A.L0_ffn_wk,
     A.L0_ffn_wv, A.L0_ffn_wo, A.L0_ffn_ln2_g, A.L0_ffn_ln2_b, A.L0_ffn_wr, A.L0_ffn_w1, A.L0_ffn_b1, A.L0_ffn_w2,
     A.L0_ffn_b2, A.L1_gnn_W_l, A.L1_gnn_b_l, A.L1_gnn_W_r, A.L1_gnn_gamma, A.L1_gnn_beta, A.L1_ffn_Wr, A.L1_ffn_W1,
     A.L1_ffn_b1, A.L1_ffn_W2, A.L1_ffn_b2) = [places[name] for name in NAMES]
    A.out = out
    return A


def kernel(**inputs):
    import numpy as np
    import concourse.bacc as bacc
    from concourse.bass_utils import run_bass_kernel_spmd

    nc = bacc.Bacc("TRN2", target_bir_lowering=False, num_devices=1)
    arrays, places = {}, {}
    for name in NAMES:
        arrays[name] = np.ascontiguousarray(inputs[name])
        places[name] = nc.dram_tensor(name, arrays[name].shape, mybir.dt.from_np(arrays[name].dtype),
                                      kind="ExternalInput").ap()
    out = nc.dram_tensor("out", [N, D], F32, kind="ExternalOutput").ap()
    program(nc, by_name(places, out))
    return run_bass_kernel_spmd(nc, [arrays], core_ids=[0]).results[0]["out"]
```
